# Optimizing a Trainium2 kernel written in Bass

```python
import numpy as np
import jax
import jax.numpy as jnp

def _softmax(x, axis=-1):
    return jax.nn.softmax(x, axis=axis)

def _gelu(x):
    return jax.nn.gelu(x, approximate=True)

def _silu(x):
    return jax.nn.silu(x)

def _sigmoid(x):
    return jax.nn.sigmoid(x)

def _layernorm(x, axis=-1, eps=1e-05):
    m = jnp.mean(x, axis=axis, keepdims=True)
    v = jnp.var(x, axis=axis, keepdims=True)
    return (x - m) / jnp.sqrt(v + eps)

def _scatter_add(tgt, idx, src, axis=0):
    return tgt.at[idx].add(src)

def _segment_sum(src, seg, n):
    return jax.ops.segment_sum(src, seg, n)
kernel_name = 'mk_adaln_d1_jaxref_r8_b4ddaa'

def setup_inputs(seed: int=0):
    np.random.seed(seed)
    _w = jnp.asarray

    def _L0_attn_setup():
        import jax, jax.numpy as jnp
        import numpy as np
        INIT_L = 512.0
        EPS = 1e-06
        N_HEAD = 16

        def fire_bias(T, w1, b1, w2, b2, c, L_multiplier):
            pos = jnp.arange(T, dtype=jnp.float32)
            rel = pos[:, None] - pos[None, :]
            threshold = jnp.abs(L_multiplier * INIT_L)
            pos_norm = jnp.maximum(pos, threshold)[:, None]
            rel = jnp.log(jnp.abs(c * rel) + 1.0)
            pos_norm = jnp.log(jnp.abs(c * pos_norm) + 1.0) + EPS
            nd = rel / pos_norm
            h = jax.nn.relu(nd[..., None] * w1[0] + b1)
            bias = jnp.einsum('tsw,wh->hts', h, w2) + b2[:, None, None]
            causal = jnp.tril(jnp.ones((T, T), dtype=bool))
            bias = jnp.where(causal[None], bias, -jnp.inf)
            return bias[None]
        key = jax.random.key(seed)
        ks = jax.random.split(key, 8)
        B, T, C, H, W = (2, 256, 128, 16, 32)
        s = 0.02
        return {'x': jax.random.normal(ks[0], (B, T, C), jnp.float32), 'Wqkv': jax.random.normal(ks[1], (C, 3 * C), jnp.float32) * s, 'bqkv': jnp.zeros((3 * C,), jnp.float32), 'Wproj': jax.random.normal(ks[2], (C, C), jnp.float32) * s, 'bproj': jnp.zeros((C,), jnp.float32), 'w1': jax.random.normal(ks[3], (1, W), jnp.float32), 'b1': jnp.zeros((W,), jnp.float32), 'w2': jax.random.normal(ks[4], (W, H), jnp.float32) * 0.1, 'b2': jnp.zeros((H,), jnp.float32), 'c_param': jnp.float32(0.1), 'L_multiplier': jnp.float32(1.0)}
    _L0_attn_in = _L0_attn_setup()

    def _L0_ffn_setup():
        import jax, jax.numpy as jnp
        import numpy as np
        E = 16
        H = 128
        F = 256
        TOP_K = 1
        B, S = (2, 128)
        key = jax.random.key(seed)
        ks = jax.random.split(key, 7)
        s = 0.02
        return {'hidden_states': jax.random.normal(ks[0], (B, S, H), jnp.float32), 'w_router': jax.random.normal(ks[1], (E, H), jnp.float32) * s, 'gate_up_proj': jax.random.normal(ks[2], (E, H, 2 * F), jnp.float32) * s, 'down_proj': jax.random.normal(ks[3], (E, F, H), jnp.float32) * s, 'w_gate': jax.random.normal(ks[4], (F, H), jnp.float32) * s, 'w_up': jax.random.normal(ks[5], (F, H), jnp.float32) * s, 'w_down': jax.random.normal(ks[6], (H, F), jnp.float32) * s}
    _L0_ffn_in = _L0_ffn_setup()
    _L0_c = _w((lambda *s: np.random.randn(*s).astype(np.float32) * 0.05)(8, 128))
    _L0_wmod = _w((lambda *s: np.random.randn(*s).astype(np.float32) * 0.05)(128, 6 * 128) * 128 ** (-0.5))
    _d = {'L0_attn_x': _L0_attn_in['x'], 'L0_attn_Wqkv': _L0_attn_in['Wqkv'], 'L0_attn_bqkv': _L0_attn_in['bqkv'], 'L0_attn_Wproj': _L0_attn_in['Wproj'], 'L0_attn_bproj': _L0_attn_in['bproj'], 'L0_attn_w1': _L0_attn_in['w1'], 'L0_attn_b1': _L0_attn_in['b1'], 'L0_attn_w2': _L0_attn_in['w2'], 'L0_attn_b2': _L0_attn_in['b2'], 'L0_attn_c_param': _L0_attn_in['c_param'], 'L0_attn_L_multiplier': _L0_attn_in['L_multiplier'], 'L0_ffn_w_router': _L0_ffn_in['w_router'], 'L0_ffn_gate_up_proj': _L0_ffn_in['gate_up_proj'], 'L0_ffn_down_proj': _L0_ffn_in['down_proj'], 'L0_ffn_w_gate': _L0_ffn_in['w_gate'], 'L0_ffn_w_up': _L0_ffn_in['w_up'], 'L0_ffn_w_down': _L0_ffn_in['w_down'], 'L0_c': _L0_c, 'L0_wmod': _L0_wmod}
    _x0 = _d['L0_attn_x']
    _d['L0_attn_x'] = jax.random.normal(jax.random.fold_in(jax.random.key(seed), 1), (8, 512, 128), dtype=_x0.dtype)
    del _x0
    return _d

def reference(L0_attn_x, L0_attn_Wqkv, L0_attn_bqkv, L0_attn_Wproj, L0_attn_bproj, L0_attn_w1, L0_attn_b1, L0_attn_w2, L0_attn_b2, L0_attn_c_param, L0_attn_L_multiplier, L0_ffn_w_router, L0_ffn_gate_up_proj, L0_ffn_down_proj, L0_ffn_w_gate, L0_ffn_w_up, L0_ffn_w_down, L0_c, L0_wmod):

    def _L0_attn_ref(x, Wqkv, bqkv, Wproj, bproj, w1, b1, w2, b2, c_param, L_multiplier):
        import jax, jax.numpy as jnp
        import numpy as np
        INIT_L = 512.0
        EPS = 1e-06
        N_HEAD = 16

        def fire_bias(T, w1, b1, w2, b2, c, L_multiplier):
            pos = jnp.arange(T, dtype=jnp.float32)
            rel = pos[:, None] - pos[None, :]
            threshold = jnp.abs(L_multiplier * INIT_L)
            pos_norm = jnp.maximum(pos, threshold)[:, None]
            rel = jnp.log(jnp.abs(c * rel) + 1.0)
            pos_norm = jnp.log(jnp.abs(c * pos_norm) + 1.0) + EPS
            nd = rel / pos_norm
            h = jax.nn.relu(nd[..., None] * w1[0] + b1)
            bias = jnp.einsum('tsw,wh->hts', h, w2) + b2[:, None, None]
            causal = jnp.tril(jnp.ones((T, T), dtype=bool))
            bias = jnp.where(causal[None], bias, -jnp.inf)
            return bias[None]
        B, T, C = x.shape
        H = N_HEAD
        hd = C // H
        qkv = x @ Wqkv + bqkv
        q, k, v = jnp.split(qkv, 3, axis=-1)
        q = q.reshape(B, T, H, hd).transpose(0, 2, 1, 3)
        k = k.reshape(B, T, H, hd).transpose(0, 2, 1, 3)
        v = v.reshape(B, T, H, hd).transpose(0, 2, 1, 3)
        bias = fire_bias(T, w1, b1, w2, b2, c_param, L_multiplier)
        scale = 1.0 / jnp.sqrt(jnp.float32(hd))
        att = jnp.einsum('bhqd,bhkd->bhqk', q, k) * scale + bias
        att = jax.nn.softmax(att, axis=-1)
        y = jnp.einsum('bhqk,bhkd->bhqd', att, v)
        y = y.transpose(0, 2, 1, 3).reshape(B, T, C)
        return y @ Wproj + bproj

    def _L0_ffn_ref(hidden_states, w_router, gate_up_proj, down_proj, w_gate, w_up, w_down):
        import jax, jax.numpy as jnp
        import numpy as np
        E = 16
        H = 128
        F = 256
        TOP_K = 1
        B, S = (2, 128)
        b, s, h = hidden_states.shape
        x = hidden_states.reshape(-1, h)
        logits = x @ w_router.T
        _, top_idx = jax.lax.top_k(logits, TOP_K)
        mask = jax.nn.one_hot(top_idx, E, dtype=logits.dtype).sum(axis=1)
        scores = jax.nn.sigmoid(logits) * mask
        masked_inputs = scores.T[:, :, None] * x[None, :, :]
        gate_up = jnp.einsum('eth,ehf->etf', masked_inputs, gate_up_proj)
        gate, up = jnp.split(gate_up, 2, axis=-1)
        expert_out = jnp.einsum('etf,efh->eth', up * jax.nn.silu(gate), down_proj)
        shared = jax.nn.silu(x @ w_gate.T) * (x @ w_up.T) @ w_down.T
        out = shared + expert_out.sum(axis=0)
        return out.reshape(b, s, h)
    x = L0_attn_x
    mod = (_silu(L0_c) @ L0_wmod).reshape(L0_c.shape[0], 6, 1, -1)
    sa, ca, ga, sb, cb, gb = (mod[:, 0], mod[:, 1], mod[:, 2], mod[:, 3], mod[:, 4], mod[:, 5])
    ga = (2 * (ga >= 0) - 1) * jnp.maximum(jnp.abs(ga), 0.25)
    gb = (2 * (gb >= 0) - 1) * jnp.maximum(jnp.abs(gb), 0.25)
    h = _layernorm(x, axis=-1) * (1 + ca) + sa
    x = x + ga * _L0_attn_ref(h, L0_attn_Wqkv, L0_attn_bqkv, L0_attn_Wproj, L0_attn_bproj, L0_attn_w1, L0_attn_b1, L0_attn_w2, L0_attn_b2, L0_attn_c_param, L0_attn_L_multiplier)
    h = _layernorm(x, axis=-1) * (1 + cb) + sb
    x = x + gb * _L0_ffn_ref(h, L0_ffn_w_router, L0_ffn_gate_up_proj, L0_ffn_down_proj, L0_ffn_w_gate, L0_ffn_w_up, L0_ffn_w_down)
    return x

_drawn_inputs = setup_inputs


def setup_inputs(seed=0):
    import zlib

    import numpy as np

    out = dict(_drawn_inputs(seed))
    spreads = {'L0_attn_bqkv': (0.0, 0.8),
     'L0_attn_bproj': (0.0, 0.302),
     'L0_attn_b1': (0.0, 0.8),
     'L0_attn_b2': (0.0, 0.8)}
    factors = {'L0_attn_Wqkv': 8.0,
     'L0_attn_Wproj': 8.0,
     'L0_attn_w1': 8.0,
     'L0_attn_w2': 8.0,
     'L0_ffn_w_router': 8.0,
     'L0_ffn_gate_up_proj': 8.0,
     'L0_ffn_down_proj': 8.0,
     'L0_ffn_w_gate': 8.0,
     'L0_ffn_w_up': 8.0,
     'L0_ffn_w_down': 8.0}
    for name, (base, spread) in spreads.items():
        noise = np.random.default_rng([zlib.crc32(name.encode()), seed]).standard_normal(out[name].shape)
        drawn = base * np.exp(spread * noise) if base else spread * noise
        out[name] = jnp.asarray(drawn.astype(out[name].dtype))
    for name, factor in factors.items():
        out[name] = (out[name] * factor).astype(out[name].dtype)
    return out
```

```python
import concourse.bass as bass
from concourse import mybir
from contextlib import ExitStack

B, T, C, H = 8, 512, 128, 16
HD = C // H
P = 128
NQ = T // P
W = 32
E, F = 16, 256
TOK = B * T // P
SORTED = 48
SLOTS = TOK + SORTED
OFF = [i * (i + 1) // 2 * P for i in range(NQ + 1)]
CAUSAL = OFF[NQ]
MASKED = -1.0e30
TERMS_Q = (0, 0, 1, 1, 0, 2)
TERMS_K = (0, 1, 0, 1, 2, 0)
KR = HD * len(TERMS_Q)
FEAT = 16 * 2 * len(TERMS_Q)
BANKS = [[(0, 0, 0)], [(1, 1, 0), (3, 3, 3 * P)], [(2, 2, 0)]]
BANK_COLS = [4 * P, 4 * P, 2 * P]
PCOL = {0: 0, 1: 4 * P, 3: 7 * P, 2: 8 * P}

POST = ("den3", "mod", "proj", "h2T", "logits")
PREP = ("xT", "q", "k")
ORDER = ("V", "den3", "mod", "proj", "den0", "xT", "q", "k", "den1", "h2T", "logits", "den2")


def jobs(post, prep):
    return [j for j in ORDER if (post or j not in POST) and (prep or j not in PREP)]


def first_job(b, last=False):
    if isinstance(b, int) and b == 0:
        return len(PREP)
    return (b - 1) * len(ORDER) + (len(PREP) + len(jobs(False, True)))


EPILOGUE = first_job(B - 1) + len(jobs(True, False))


def bass_adaln_block(nc, x_d, Wqkv_d, bqkv_d, Wproj_d, bproj_d, w1_d, b1_d, w2_d, b2_d, c_param_d, L_mult_d,
                     w_router_d, gate_up_d, down_d, w_gate_d, w_up_d, w_down_d, cond_d, wmod_d, out_d):
    f32, bf16, i32 = mybir.dt.float32, mybir.dt.bfloat16, mybir.dt.int32
    ALU, ACT, AX = mybir.AluOpType, mybir.ActivationFunctionType, mybir.AxisListType
    ds = bass.ds
    ctx = ExitStack()
    with ctx:
        ctx.enter_context(nc.allow_non_contiguous_dma(reason="small parameter loads"))

        def sb(name, shape, dt=f32):
            return ctx.enter_context(nc.sbuf_tensor(name, shape, dt))

        def sem(name):
            return ctx.enter_context(nc.semaphore(name))

        x1_d = nc.dram_tensor("x1_scratch", (B * T, C), f32, kind="Internal").ap()
        rows_d = nc.dram_tensor("ffn_rows", (SLOTS * P, C), f32, kind="Internal").ap()
        ffn_d = nc.dram_tensor("ffn_out", (SLOTS * P, C), f32, kind="Internal").ap()

        ident = sb("ident", [P, P])
        neg_ident = sb("neg_ident", [P, P], bf16)
        ones_bf = sb("ones_bf", [P, P], bf16)
        pick_den = sb("pick_den", [P, P])
        zeros = sb("zeros", [P, P])
        neg_half = sb("neg_half", [P, NQ])
        Wv = sb("Wv", [P, C])
        Wqk = sb("Wqk", [P, 2, C])
        Wproj = sb("Wproj", [P, 4, C])
        wmod_bc = sb("wmod_bc", [P, 4 * C])
        bq = sb("bq", [P, 2])
        bv_bc = sb("bv_bc", [P, C])
        bproj_bc = sb("bproj_bc", [P, C])
        modT = sb("modT", [P, B, 2])
        siluT = sb("siluT", [P, B])
        routerT = sb("routerT", [P, E])
        bias = sb("bias", [P, H * CAUSAL])
        bias_v = bias[:, :].rearrange("p (h s) -> p h s", h=H)
        qf = sb("qf", [KR, 2, 4, T], bf16)
        kf = sb("kf", [KR, 2, 4, T], bf16)
        probs = sb("probs", [P, 8 * CAUSAL])
        biased = sb("biased", [P, 2, CAUSAL])
        rowmax = sb("rowmax", [P, 2, NQ])
        negmax = sb("negmax", [P, 2, NQ, P], bf16)
        vaug = sb("vaug", [P, NQ, H, 2 * HD])
        yT = sb("yT", [P, 4, T])
        rden = sb("rden", [P, T])
        hT = sb("hT", [P, T])
        xt = sb("xt", [P, NQ, C])
        xr = sb("xr", [P, NQ, C])
        x1 = sb("x1", [P, NQ, C])
        h2T = sb("h2T", [P, T])
        qk32 = sb("qk32", [P, 2, T])
        rest = sb("rest", [P, T])
        parts = sb("parts", [P, 2, 3, T], bf16)
        stats = sb("stats", [P, NQ, 6])
        mv = sb("mv", [P, NQ, 2])
        var_eps = sb("var_eps", [P, NQ])
        rstd = sb("rstd", [P, NQ])
        stats2 = sb("stats2", [P, NQ, 6])
        mv2 = sb("mv2", [P, NQ, 2])
        var_eps2 = sb("var_eps2", [P, NQ])
        rstd2 = sb("rstd2", [P, NQ])
        modbc = sb("modbc", [P, 4, C])
        absg = sb("absg", [P, 2, C])
        sgn = sb("sgn", [P, 2, C])
        silu_col = sb("silu_col", [P, P])
        gb_all = sb("gb_all", [P, B, C])
        logits = sb("logits", [P, TOK, E])
        at = 0

        def setup_view(cols):
            nonlocal at
            at += cols
            return probs[:, at - cols:at]

        YW = 2 * T - 4
        hidden = setup_view(4 * T).rearrange("p (r n) -> p r n", r=4)
        stage = setup_view(4 * T).rearrange("p (r n) -> p r n", r=4)
        dist = setup_view(YW)
        dist_i = setup_view(YW).bitcast(i32)
        pos_i = setup_view(P).bitcast(i32)
        pnorm = setup_view(P)
        slope = setup_view(P)
        w2_bd = setup_view(4 * H)
        fire = setup_view(8)
        wmod_cols = setup_view(2 * C)
        condT = setup_view(B)
        sig = setup_view(B)
        Wqk_raw = setup_view(2 * C)
        at2 = 0

        def ffn_view(cols):
            nonlocal at2
            at2 += cols
            return bias[:, at2 - cols:at2]

        w_up_all = ffn_view((E + 1) * 2 * F).rearrange("p (e n) -> p e n", e=E + 1)
        w_dn_all = ffn_view((E + 1) * 2 * C).rearrange("p (e n) -> p e n", e=E + 1)
        rows_all = ffn_view(TOK * C).rearrange("p (t c) -> p t c", t=TOK)
        row_in = ffn_view(2 * C).rearrange("p (k c) -> p k c", k=2)
        rowT = ffn_view(2 * P).rearrange("p (k c) -> p k c", k=2)
        gated = ffn_view(2 * F).rearrange("p (k c) -> p k c", k=2)
        act_h = ffn_view(2 * F).rearrange("p (k c) -> p k c", k=2)
        act_hT = ffn_view(2 * F).rearrange("p (k c) -> p k c", k=2)
        row_out = ffn_view(2 * C).rearrange("p (k c) -> p k c", k=2)
        raw_shared = ffn_view(6 * C).rearrange("p (k c) -> p k c", k=6)
        at = 0
        x1_all = setup_view(TOK * C).rearrange("p (t c) -> p t c", t=TOK)
        sh_all = setup_view(TOK * C).rearrange("p (t c) -> p t c", t=TOK)
        top = setup_view(TOK)
        top_e = setup_view(TOK)
        score = setup_view(TOK)
        wide = yT[:, 0, :].rearrange("p (t e) -> p t e", e=E)
        wide2 = yT[:, 1, :].rearrange("p (t e) -> p t e", e=E)
        sq = yT[:, 2, 0:E * E].rearrange("p (a b) -> p a b", b=E)
        wide3 = yT[:, 3, :].rearrange("p (e k) -> p e k", e=E)
        iota_e = sb("iota_e", [P, E])
        iota_e1 = sb("iota_e1", [P, E])
        iota_k = sb("iota_k", [P, TOK])
        iota_t = sb("iota_t", [P, SORTED])
        iota_i = sb("iota_i", [P, SORTED], i32)
        one_hot = sb("one_hot", [P, TOK, E], bf16)
        before = sb("before", [P, P], bf16)
        lower = sb("lower", [P, E, E])
        tiles_of = sb("tiles_of", [P, E])
        first_tile = sb("first_tile", [P, E])
        base_row = sb("base_row", [P, E])
        end_tile = sb("end_tile", [P, E])
        dest_f = sb("dest_f", [P, TOK])
        dest = sb("dest", [P, TOK], i32)
        expert_f = sb("expert_f", [P, SLOTS])
        expert = sb("expert", [P, SLOTS], i32)
        cmp_t = xt[:, :, :].rearrange("p a b -> p (a b)")
        cmp_t2 = xr[:, :, :].rearrange("p a b -> p (a b)")

        def bank(name):
            return ctx.enter_context(nc.psum_tensor(name, [P, T], f32))

        score_bank = [bank(f"score_bank{k}") for k in range(3)]
        turned_bank = [bank(f"turned_bank{k}") for k in range(3)]
        y_bank = bank("y_bank")
        misc = bank("misc")

        fire_loaded = sem("fire_loaded")
        params_loaded = sem("params_loaded")
        consts_made = sem("consts_made")
        pool_step = sem("pool_step")
        dve_step = sem("dve_step")
        dist_made = sem("dist_made")
        logs_taken = sem("logs_taken")
        slopes_made = sem("slopes_made")
        hidden_ready = sem("hidden_ready")
        hidden_used = sem("hidden_used")
        stage_ready = sem("stage_ready")
        stage_sent = [sem(f"stage_sent{r}") for r in range(4)]
        bias_masked = sem("bias_masked")
        cond_exp = sem("cond_exp")
        silu_made = sem("silu_made")
        modT_ready = sem("modT_ready")
        modT_copied = sem("modT_copied")
        setup_T = sem("setup_T")

        xt_loaded = sem("xt_loaded")
        xr_loaded = sem("xr_loaded")
        var_ready = sem("var_ready")
        rstd_ready = sem("rstd_ready")
        xn_ready = sem("xn_ready")
        var2_ready = sem("var2_ready")
        rstd2_ready = sem("rstd2_ready")
        parts_step = sem("parts_step")
        feat_ready = [sem(f"feat_ready{s}") for s in range(2)]
        scores_ready = sem("scores_ready")
        scores_free = sem("scores_free")
        negmax_ready = sem("negmax_ready")
        turned_ready = sem("turned_ready")
        turned_free = sem("turned_free")
        av_done = sem("av_done")
        y_copied = sem("y_copied")
        yn_ready = sem("yn_ready")
        misc_ready = sem("misc_ready")
        misc_used = sem("misc_used")
        waits_passed = sem("waits_passed")
        prep_step = sem("prep_step")
        norm_step = sem("norm_step")
        silu_col_made = sem("silu_col_made")
        x1_ready = sem("x1_ready")
        h2_ready = sem("h2_ready")
        x1_stored = sem("x1_stored")
        h2_stored = sem("h2_stored")
        rows_zeroed = sem("rows_zeroed")

        w_loaded = sem("w_loaded")
        shared_loaded = sem("shared_loaded")
        shared_T = sem("shared_T")
        shared_copied = sem("shared_copied")
        rows_loaded = sem("rows_loaded")
        one_hot_made = sem("one_hot_made")
        ranks_ready = sem("ranks_ready")
        score_exp = sem("score_exp")
        top_ready = sem("top_ready")
        dest_ready = sem("dest_ready")
        expert_ready = sem("expert_ready")
        masked_ready = sem("masked_ready")
        scattered = sem("scattered")
        row_loaded = [sem(f"row_loaded{k}") for k in range(2)]
        rowT_ready = sem("rowT_ready")
        rowT_copied = sem("rowT_copied")
        up_ready = sem("up_ready")
        gate_done = sem("gate_done")
        act_ready = sem("act_ready")
        actT_ready = sem("actT_ready")
        actT_copied = sem("actT_copied")
        down_ready = sem("down_ready")
        out_copied = sem("out_copied")
        row_stored = [sem(f"row_stored{k}") for k in range(2)]
        all_loaded = sem("all_loaded")
        gathered = sem("gathered")
        final_step = sem("final_step")
        out_stored = sem("out_stored")

        block = ctx.enter_context(nc.Block())

        @block.sync
        def _(sp):
            sp.dma_start(fire[:, 0:1], c_param_d.partition_broadcast(P)).then_inc(fire_loaded, 16)
            sp.dma_start(fire[:, 1:2], L_mult_d.partition_broadcast(P)).then_inc(fire_loaded, 16)
            for r in range(4):
                rows = slice(W * r, W * r + W)
                sp.dma_start(fire[rows, 2:3], w1_d.rearrange("a w -> w a")).then_inc(fire_loaded, 16)
                sp.dma_start(fire[rows, 3:4], b1_d.rearrange("(w a) -> w a", a=1)).then_inc(fire_loaded, 16)
                for n in range(2):
                    part = slice(W * r + H * n, W * r + H * n + H)
                    sp.dma_start(fire[part, 4:5], b2_d.rearrange("(h a) -> h a", a=1)).then_inc(fire_loaded, 16)
            sp.wait_ge(consts_made, 1)
            for r in range(4):
                sp.dma_start(w2_bd[W * r:W * r + W, H * r:H * r + H], w2_d).then_inc(fire_loaded, 16)
            sp.dma_start(xt[:, :, :], x_d[0, :, :].rearrange("(i p) c -> p i c", p=P)).then_inc(xt_loaded, 16)
            for n in range(T // 8):
                i, q = n // 16, 8 * (n % 16)
                sp.wait_ge(stage_ready, n + 1)
                sp.dma_start(bias_v[q:q + 8, :, OFF[i]:OFF[i + 1]], stage[:, n % 4, 0:P * (i + 1)])\
                  .then_inc(stage_sent[n % 4], 16)

            def features(b, g):
                s = g % 2
                for mat, terms, dst in ((0, TERMS_Q, qf), (1, TERMS_K, kf)):
                    for t, part in enumerate(terms):
                        sp.dma_start(dst[HD * t:HD * t + HD, s, :, :], parts[W * g:W * g + W, mat, part, :]).then_inc(feat_ready[s], 16)

            def batch(b, post, prep):
                if prep:
                    sp.dma_start(xt[:, :, :], x_d[ds(b + 1, 1), :, :].rearrange("b (i p) c -> p (b i) c", p=P))\
                      .then_inc(xt_loaded, 16)
                if post:
                    load_residual(b - 1)
                for g in (2, 3):
                    sp.wait_ge(scores_ready, (b * 16 + 4 * g - 4) * 3)
                    features(b, g)
                if post:
                    store_post(b - 1)
                if prep:
                    sp.wait_ge(parts_step, (b + 2) * 8)
                    for g in (0, 1):
                        sp.wait_ge(scores_ready, (b * 16 + 4 * g + 12) * 3)
                        features(b + 1, g)

            def load_residual(b):
                sp.dma_start(xr[:, :, :], x_d[ds(b, 1), :, :].rearrange("b (i p) c -> p (b i) c", p=P))\
                  .then_inc(xr_loaded, 16)

            def store_post(b):
                sp.wait_ge(x1_ready, b + 1)
                sp.dma_start(x1_d[ds(b * T, T), :].rearrange("(i p) c -> p i c", p=P), x1[:, :, :])\
                  .then_inc(x1_stored, 16)
                sp.wait_ge(h2_ready, b + 1)
                sp.dma_start(rows_d[ds(b * T, T), :].rearrange("(i p) c -> p i c", p=P), xr[:, :, :])\
                  .then_inc(h2_stored, 16)
                sp.wait_ge(h2_stored, (b + 1) * 16)

            sp.wait_ge(parts_step, 8)
            features(0, 0)
            features(0, 1)
            sp.wait_ge(misc_ready, 1)
            batch(0, False, True)
            with sp.Fori(1, B - 1) as b:
                sp.wait_ge(misc_ready, first_job(b))
                batch(b, True, True)
            sp.wait_ge(misc_ready, first_job(B - 1))
            batch(B - 1, True, False)
            sp.wait_ge(misc_ready, EPILOGUE)
            load_residual(B - 1)
            store_post(B - 1)
            sp.wait_ge(scores_free, 3 + 3 * 16 * B)
            for k, src in enumerate((w_gate_d[0:P, :], w_gate_d[P:F, :], w_up_d[0:P, :], w_up_d[P:F, :],
                                     w_down_d[:, 0:P], w_down_d[:, P:F])):
                sp.dma_start(raw_shared[:, k, :], src).then_inc(shared_loaded, 16)
            sp.dma_start(rows_all, rows_d[0:B * T, :].rearrange("(t p) c -> p t c", p=P)).then_inc(rows_loaded, 16)
            for e in range(0, E, 4):
                sp.dma_start(w_up_all[:, e:e + 4, :], gate_up_d[e:e + 4, :, :].rearrange("e k n -> k e n"))\
                  .then_inc(w_loaded, 16)
                for e1 in range(e, e + 4):
                    sp.dma_start(w_dn_all[:, e1, :].rearrange("p (a n) -> p a n", a=2),
                                 down_d[e1, :, :].rearrange("(a p) n -> p a n", p=P)).then_inc(w_loaded, 16)
            sp.wait_ge(scattered, 16 * TOK)

            def load_row(t, k):
                sp.dma_start(row_in[:, k, :], rows_d[ds(t * P, P), :]).then_inc(row_loaded[k], 16)

            load_row(0, 0)
            load_row(1, 1)
            with sp.Fori(0, SLOTS // 2 - 1) as n:
                for k in range(2):
                    sp.wait_ge(rowT_ready, n * 2 + k + 1)
                    load_row(n * 2 + k + 2, k)
            sp.dma_start(x1_all, x1_d.rearrange("(t p) c -> p t c", p=P)).then_inc(all_loaded, 16)
            for k in range(2):
                sp.wait_ge(row_stored[k], 16 * (SLOTS // 2 + 1))
            sp.dma_start(sh_all, ffn_d[0:B * T, :].rearrange("(t p) c -> p t c", p=P)).then_inc(all_loaded, 16)
            with sp.Fori(0, B) as b:
                sp.wait_ge(final_step, b * 3 + 3)
                sp.dma_start(out_d[ds(b, 1), :, :].rearrange("b (i p) c -> p (b i) c", p=P),
                             x1_all[:, ds(b * NQ, NQ), :]).then_inc(out_stored, 16)
            sp.wait_ge(out_stored, 16 * B)
            sp.wait_ge(x1_stored, 16 * B)
            sp.wait_ge(rows_zeroed, 16)

        @block.gpsimd
        def _(pool):
            step = [0]

            def chain(ins):
                step[0] += 1
                ins.then_inc(pool_step, 1)
                pool.wait_ge(pool_step, step[0])

            pool.memset(w2_bd, 0.0).then_inc(consts_made, 1)
            pool.wait_ge(consts_made, 1)
            for r in range(4):
                rows = slice(W * r, W * r + W)
                pool.iota(dist_i[rows, :], pattern=[[-1, YW]], base=r + T - 4, channel_multiplier=0)
                last = pool.iota(pos_i[rows, :], pattern=[[4, P]], base=r, channel_multiplier=0)
            last.then_inc(consts_made, 1)
            pool.wait_ge(consts_made, 2)
            chain(pool.memset(ident[:, :], 0.0))
            chain(pool.memset(neg_ident[:, :], 0.0))
            chain(pool.memset(pick_den[:, :], 0.0))
            chain(pool.memset(Wproj[:, :, :], 0.0))
            chain(pool.memset(before[:, :], 1.0))
            chain(pool.memset(lower[:, :, :], 1.0))
            pool.memset(ones_bf[:, :], 1.0)
            pool.memset(zeros[:, :], 0.0)
            pool.memset(neg_half[:, :], -0.5)
            pool.memset(vaug[:, :, :, :], 1.0)
            pool.affine_select(out=ident[:, :], in_=ident[:, :], compare_op=ALU.not_equal, fill=1.0, base=0,
                               pattern=[[-1, P]], channel_multiplier=1)
            pool.affine_select(out=neg_ident[:, :], in_=neg_ident[:, :], compare_op=ALU.not_equal, fill=-1.0,
                               base=0, pattern=[[-1, P]], channel_multiplier=1)
            pick_v = pick_den[:, :].rearrange("p (a c) -> p a c", a=4)
            pool.affine_select(out=pick_v, in_=pick_v, compare_op=ALU.not_equal, fill=1.0, base=-HD,
                               pattern=[[-W, 4], [0, W]], channel_multiplier=1)
            pool.affine_select(out=before[:, :], in_=before[:, :], compare_op=ALU.is_gt, fill=0.0, base=0,
                               pattern=[[1, P]], channel_multiplier=-1)
            pool.affine_select(out=lower[:, :, :], in_=lower[:, :, :], compare_op=ALU.is_gt, fill=0.0, base=0,
                               pattern=[[1, E], [-1, E]], channel_multiplier=0)
            chain(pool.iota(iota_i[:, :], pattern=[[1, SORTED]], base=0, channel_multiplier=0))
            pool.tensor_copy(iota_t[:, :], iota_i[:, :])
            pool.tensor_copy(iota_e[:, :], iota_i[:, 0:E])
            chain(pool.tensor_copy(iota_k[:, :], iota_i[:, 0:TOK]))
            pool.tensor_scalar(iota_k[:, :], iota_k[:, :], float(P), 0.0, ALU.mult, ALU.add)
            pool.memset(expert_f[:, 0:TOK], float(E)).then_inc(consts_made, 1)
            pool.wait_ge(consts_made, 3)
            pool.dma_start(rows_d[B * T:SLOTS * P, :].rearrange("(t p) c -> p t c", p=P),
                           zeros[:, :].unsqueeze(1).to_broadcast([P, SORTED, C])).then_inc(rows_zeroed, 16)
            zero_row = zeros[:, 0:1].to_broadcast([P, T])

            def split(b, job):
                for mat in range(2):
                    x32, n0 = qk32[:, mat, :], b * 8 + 4 * mat
                    pool.wait_ge(misc_used, job + mat + 1)
                    if mat == 0 and not (isinstance(b, int) and b == 0):
                        for s in range(2):
                            pool.wait_ge(feat_ready[s], b * 2 * FEAT)
                    pool.tensor_tensor(parts[:, mat, 0, :], x32, zero_row, ALU.add).then_inc(parts_step, 1)
                    pool.wait_ge(parts_step, n0 + 1)
                    pool.tensor_tensor(rest[:, :], x32, parts[:, mat, 0, :], ALU.subtract).then_inc(parts_step, 1)
                    pool.wait_ge(parts_step, n0 + 2)
                    pool.tensor_tensor(parts[:, mat, 1, :], rest[:, :], zero_row, ALU.add).then_inc(parts_step, 1)
                    pool.wait_ge(parts_step, n0 + 3)
                    pool.tensor_tensor(parts[:, mat, 2, :], rest[:, :], parts[:, mat, 1, :], ALU.subtract)\
                        .then_inc(parts_step, 1)
                    pool.wait_ge(parts_step, n0 + 4)

            def power(b, var, out, ready, done):
                pool.wait_ge(ready, b + 1)
                pool.tensor_tensor(out[:, :], var[:, :], neg_half[:, :], ALU.pow).then_inc(done, 1)

            power(0, var_eps, rstd, var_ready, rstd_ready)
            split(0, 1)
            for r in range(4):
                pool.wait_ge(stage_sent[r], 16 * (T // 8 // 4))
            for i in range(NQ):
                d = bias_v[:, :, OFF[i] + P * i:OFF[i] + P * i + P]
                pool.affine_select(out=d, in_=d, compare_op=ALU.is_ge, fill=MASKED, base=0,
                                   pattern=[[0, H], [-1, P]], channel_multiplier=1).then_inc(bias_masked, 1)
            power(1, var_eps, rstd, var_ready, rstd_ready)
            split(1, first_job(0) + jobs(False, True).index("q"))
            with pool.Fori(1, B - 1) as b:
                power(b - 1, var_eps2, rstd2, var2_ready, rstd2_ready)
                power(b + 1, var_eps, rstd, var_ready, rstd_ready)
                split(b + 1, first_job(b) + ORDER.index("q"))
            for b in (B - 2, B - 1):
                power(b, var_eps2, rstd2, var2_ready, rstd2_ready)
            pool.wait_ge(dest_ready, 1)
            pool.wait_ge(masked_ready, 1)
            pool.wait_ge(rows_zeroed, 16)
            for t in range(TOK):
                pool.indirect_dma_start(rows_d, bass.IndirectOffsetOnAxis(ap=dest[:, t:t + 1], axis=0),
                                        rows_all[:, t, :], None).then_inc(scattered, 16)
            for k in range(2):
                pool.wait_ge(row_stored[k], 16 * (SLOTS // 2 + 1))
            pool.wait_ge(scattered, 16 * TOK)
            for t in range(TOK):
                pool.indirect_dma_start(rows_all[:, t, :], None, ffn_d,
                                        bass.IndirectOffsetOnAxis(ap=dest[:, t:t + 1], axis=0))\
                    .then_inc(gathered, 16)

        @block.scalar
        def _(act):
            for k in range(2):
                act.sem_inc(row_stored[k], 16)
            act.dma_start(condT, cond_d.rearrange("b k -> k b")).then_inc(params_loaded, 16)
            act.dma_start(wmod_cols, wmod_d[:, 0:2 * C]).then_inc(params_loaded, 16)
            act.dma_start(wmod_bc[:, :], wmod_d[:, 2 * C:6 * C]).then_inc(params_loaded, 16)
            act.dma_start(Wv[:, :], Wqkv_d[:, 2 * C:3 * C]).then_inc(params_loaded, 16)
            act.dma_start(Wqk_raw, Wqkv_d[:, 0:2 * C]).then_inc(params_loaded, 16)
            for m in range(2):
                for g in range(4):
                    part = bqkv_d[m * C + W * g:m * C + W * g + W].rearrange("(h d a) -> d h a", h=4, a=1)
                    act.dma_start(bq[W * g:W * g + W, m:m + 1], part).then_inc(params_loaded, 16)
            act.dma_start(bv_bc[:, :], bqkv_d[2 * C:3 * C].partition_broadcast(P)).then_inc(params_loaded, 16)
            act.dma_start(bproj_bc[:, :], bproj_d.partition_broadcast(P)).then_inc(params_loaded, 16)
            act.dma_start(routerT[:, :], w_router_d.rearrange("e k -> k e")).then_inc(params_loaded, 16)
            act.wait_ge(pool_step, 4)
            for hh in range(4):
                act.dma_start(Wproj[W * hh:W * hh + HD, :, :],
                              Wproj_d.rearrange("(g h d) n -> d g h n", h=4, d=HD)[:, :, hh, :])\
                   .then_inc(params_loaded, 16)
            act.wait_ge(dist_made, 2)
            act.activation(dist, dist, ACT.Ln, bias=1.0).then_inc(logs_taken, 1)
            act.activation(pnorm, pnorm, ACT.Ln, bias=1.0).then_inc(logs_taken, 1)
            act.wait_ge(params_loaded, 16 * 20)
            act.activation(sig, condT, ACT.Exp, scale=-1.0).then_inc(cond_exp, 1)
            def exps(b, h):
                u = b * 16 + h
                if h % 4 == 0:
                    act.wait_ge(av_done, b * 4 + h // 4 + 1)
                for k in range(3):
                    act.wait_ge(turned_ready, u * 3 + 6 + k + 1)
                    c0, n = (h % 8) * CAUSAL + 4 * P * k, BANK_COLS[k]
                    act.activation(probs[:, c0:c0 + n], turned_bank[k][:, 0:n], ACT.Exp).then_inc(turned_free, 1)

            def y_copy(b, g):
                act.wait_ge(av_done, b * 4 + g + 1 + 2)
                act.activation(yT[:, g, :], y_bank[:, :], ACT.Copy).then_inc(y_copied, 1)

            def modulate(b, job):
                act.wait_ge(misc_ready, job + 1)
                act.activation(hT[:, :], misc[:, :], ACT.Identity, bias=modT[:, ds(b, 1), 0],
                               scale=modT[:, ds(b, 1), 1]).then_inc(misc_used, 1)

            def copy_h2T(job):
                act.wait_ge(misc_ready, job + 1)
                act.activation(h2T[:, :], misc[:, :], ACT.Copy).then_inc(misc_used, 1)

            def batch(b, post, prep):
                job = {j: first_job(b) + n for n, j in enumerate(jobs(post, prep))}
                for h in range(H):
                    exps(b, h)
                    if h == 0 and post:
                        y_copy(b - 1, 3)
                    if h == 4 and post:
                        act.wait_ge(misc_ready, job["proj"] + 1)
                    if h in (4, 8, 12):
                        y_copy(b, h // 4 - 1)
                    if h == 6 and prep:
                        modulate(b + 1, job["xT"])
                    if h == 10 and post:
                        copy_h2T(job["h2T"])

            act.wait_ge(modT_copied, 1)
            modulate(0, 0)
            act.wait_ge(slopes_made, 1)
            for n in range(T // 4):
                i = n // 32
                if n >= 4:
                    act.wait_ge(hidden_used, n - 3)
                act.activation(hidden[:, n % 4, 0:P * (i + 1)], dist[:, T - 4 - 4 * n:T - 4 - 4 * n + P * (i + 1)],
                               ACT.Relu, bias=fire[:, 3:4], scale=slope[:, n:n + 1]).then_inc(hidden_ready, 1)
            act.wait_ge(hidden_used, T // 4)
            act.wait_ge(bias_masked, NQ)
            batch(0, False, True)
            with act.Fori(1, B - 1) as b:
                batch(b, True, True)
            batch(B - 1, True, False)
            y_copy(B - 1, 3)
            copy_h2T(EPILOGUE + POST.index("h2T"))
            act.wait_ge(top_ready, 1)
            act.activation(score, top, ACT.Exp, scale=-1.0).then_inc(score_exp, 1)
            with act.Fori(0, SLOTS // 2) as n:
                for k in range(2):
                    t = n * 2 + k
                    act.wait_ge(up_ready, t + 1)
                    act.activation(gated[:, k, :], turned_bank[k][:, 0:F], ACT.Silu).then_inc(gate_done, 1)
                    act.wait_ge(actT_ready, t + 1)
                    act.activation(act_hT[:, k, :], [score_bank[2], turned_bank[2]][k][:, 0:F], ACT.Copy)\
                       .then_inc(actT_copied, 1)
                    act.wait_ge(out_copied, t + 1)
                    act.dma_start(ffn_d[ds(t * P, P), :], row_out[:, k, :]).then_inc(row_stored[k], 16)

        @block.vector
        def _(dve):
            step = [0]

            def chain(ins):
                step[0] += 1
                ins.then_inc(dve_step, 1)
                dve.wait_ge(dve_step, step[0])

            V = nc.vector

            def carry_wait():
                dve.sem_inc(waits_passed)

            dve.wait_ge(fire_loaded, 16 * 22)
            dve.wait_ge(consts_made, 2)

            def absolute(x):
                return V.scalar_tensor_tensor(x, x, -1.0, x, ALU.mult, ALU.max)

            chain(V.tensor_scalar(fire[:, 5:6], fire[:, 1:2], float(T), None, ALU.mult))
            chain(V.tensor_scalar(dist, dist_i, fire[:, 0:1], None, ALU.mult))
            chain(absolute(fire[:, 5:6]))
            chain(V.tensor_scalar(pnorm, pos_i, fire[:, 5:6], fire[:, 0:1], ALU.max, ALU.mult))
            absolute(dist)
            absolute(pnorm).then_inc(dist_made, 2)
            dve.wait_ge(logs_taken, 2)
            chain(V.tensor_scalar(pnorm, pnorm, 1e-6, None, ALU.add))
            chain(V.reciprocal(slope, pnorm))
            V.tensor_scalar(slope, slope, fire[:, 2:3], None, ALU.mult).then_inc(slopes_made, 1)
            dve.wait_ge(cond_exp, 1)
            chain(V.tensor_scalar(sig, sig, 1.0, None, ALU.add))
            chain(V.reciprocal(sig, sig))
            V.tensor_tensor(siluT[:, :], condT, sig, ALU.mult).then_inc(silu_made, 1)
            dve.wait_ge(params_loaded, 16 * 20)
            for m in range(2):
                V.tensor_copy(Wqk[:, m, :].rearrange("p (g d h) -> p g d h", g=4, d=HD),
                              Wqk_raw[:, m * C:m * C + C].rearrange("p (g h d) -> p g d h", g=4, d=HD))
            dve.wait_ge(modT_ready, 1)
            V.tensor_copy(modT[:, :, 0], misc[:, 0:B])
            V.tensor_scalar(modT[:, :, 1], misc[:, B:2 * B], 1.0, None, ALU.add).then_inc(modT_copied, 1)
            V.memset(y_bank[:, :], 0.0)
            dve.sem_inc(scores_free, 3)

            def norm_stats(src, st, m, ve, ready, steps, base):
                for i in range(NQ):
                    last = V.bn_stats(st[:, i, :], src[:, i, :])
                last.then_inc(steps, 1)
                dve.wait_ge(steps, base + 1)
                carry_wait()
                for i in range(NQ):
                    last = V.bn_aggr(m[:, i, :], st[:, i, :])
                last.then_inc(steps, 1)
                dve.wait_ge(steps, base + 2)
                V.tensor_scalar(ve[:, :], m[:, :, 1], 1e-5, None, ALU.add).then_inc(ready, 1)

            def normalize(b, dst, src, m, r, rstd_sem):
                dve.wait_ge(rstd_sem, b + 1)
                for i in range(NQ):
                    last = V.tensor_scalar(dst[:, i, :], src[:, i, :], m[:, i, 0:1], r[:, i:i + 1],
                                           ALU.subtract, ALU.mult)
                return last

            GATE_STEPS, RESIDUAL_STEPS, NORM2_STEPS = 4, 3, 2

            def post_base(b):
                return b * (GATE_STEPS + RESIDUAL_STEPS + NORM2_STEPS)

            def norm1_stats(b):
                dve.wait_ge(xt_loaded, (b + 1) * 16)
                norm_stats(xt, stats, mv, var_eps, var_ready, prep_step, b * 2)

            def norm1_apply(b):
                normalize(b, xt, xt, mv, rstd, rstd_ready).then_inc(xn_ready, 1)

            def take_qk(mat, job):
                dve.wait_ge(misc_ready, job + 1)
                s = float(HD) ** -0.5 if mat == 0 else 1.0
                V.tensor_scalar(qk32[:, mat, :], misc[:, :], bq[:, mat:mat + 1], s, ALU.add, ALU.mult)\
                 .then_inc(misc_used, 1)

            def take_v(b, job):
                dve.wait_ge(misc_ready, job + 1)
                V.tensor_tensor(vaug[:, :, :, 0:HD], misc[:, :].rearrange("p (i h d) -> p i h d", i=NQ, d=HD),
                                bv_bc[:, :].rearrange("p (h d) -> p h d", d=HD).unsqueeze(1)
                                .to_broadcast([P, NQ, H, HD]), ALU.add).then_inc(misc_used, 1)

            def maxima(b, h):
                u, s = b * 16 + h, h % 2
                dve.wait_ge(turned_ready, u * 3 + 3)
                for i in range(NQ):
                    k, c0 = (0, i * P) if i < 2 else (i - 1, 0)
                    if i != 1:
                        dve.wait_ge(scores_ready, u * 3 + k + 1)
                        carry_wait()
                    n = P * (i + 1)
                    last = V.tensor_tensor_reduce(
                        out=biased[:, s, OFF[i]:OFF[i] + n], in0=score_bank[k][:, c0:c0 + n],
                        in1=bias_v[:, h, OFF[i]:OFF[i] + n], scale=1.0, scalar=MASKED, op0=ALU.add, op1=ALU.max,
                        accum_out=rowmax[:, s, i:i + 1])
                    if i:
                        last.then_inc(scores_free, 1)
                dve.wait_ge(scores_free, u * 3 + 6)
                V.tensor_tensor(negmax[:, s, :, :], neg_ident[:, :].unsqueeze(1).to_broadcast([P, NQ, P]),
                                rowmax[:, s, :].unsqueeze(2).to_broadcast([P, NQ, P]), ALU.mult)\
                 .then_inc(negmax_ready, 1)

            def normalize_y(b, g, job):
                dve.wait_ge(misc_ready, job + 1)
                V.reciprocal(rden[:, :], misc[:, :]).then_inc(misc_used, 1)
                dve.wait_ge(misc_used, job + 1)
                V.tensor_tensor(yT[:, g, :], yT[:, g, :], rden[:, :], ALU.mult).then_inc(yn_ready, 1)

            def make_silu_col(b):
                V.tensor_copy(silu_col[:, :], siluT[:, ds(b, 1)].to_broadcast([P, P])).then_inc(silu_col_made, 1)

            def gates(b, job):
                n0 = post_base(b)
                dve.wait_ge(misc_ready, job + 1)
                V.tensor_copy(modbc[:, :, :], misc[:, :].rearrange("p (m c) -> p m c", m=4)).then_inc(misc_used, 1)
                dve.wait_ge(misc_used, job + 1)
                g2 = modbc[:, 0:4:3, :]
                V.tensor_scalar(sgn[:, :, :], g2, 0.0, 2.0, ALU.is_ge, ALU.mult)
                V.tensor_scalar(modbc[:, 2, :], modbc[:, 2, :], 1.0, None, ALU.add)
                V.scalar_tensor_tensor(absg[:, :, :], g2, -1.0, g2, ALU.mult, ALU.max).then_inc(norm_step, 1)
                dve.wait_ge(norm_step, n0 + 1)
                V.tensor_scalar(absg[:, :, :], absg[:, :, :], 0.25, None, ALU.max).then_inc(norm_step, 1)
                dve.wait_ge(norm_step, n0 + 2)
                V.scalar_tensor_tensor(g2, sgn[:, :, :], -1.0, absg[:, :, :], ALU.add, ALU.mult)\
                 .then_inc(norm_step, 1)
                dve.wait_ge(norm_step, n0 + 3)
                V.tensor_copy(gb_all[:, ds(b, 1), :], modbc[:, 3:4, :]).then_inc(norm_step, 1)

            def bc4(ap):
                return ap.unsqueeze(1).to_broadcast([P, NQ, C])

            def residual(b, job):
                n0 = post_base(b) + GATE_STEPS
                dve.wait_ge(misc_ready, job + 1)
                if not (isinstance(b, int) and b == 0):
                    dve.wait_ge(x1_stored, b * 16)
                V.tensor_tensor(x1[:, :, :], misc[:, :].rearrange("p (i c) -> p i c", i=NQ), bc4(bproj_bc[:, :]),
                                ALU.add).then_inc(misc_used, 1)
                dve.wait_ge(misc_used, job + 1)
                V.tensor_tensor(x1[:, :, :], x1[:, :, :], bc4(modbc[:, 0, :]), ALU.mult).then_inc(norm_step, 1)
                dve.wait_ge(norm_step, n0 + 1)
                dve.wait_ge(xr_loaded, (b + 1) * 16)
                V.tensor_tensor(x1[:, :, :], x1[:, :, :], xr[:, :, :], ALU.add).then_inc(x1_ready, 1)
                dve.wait_ge(x1_ready, b + 1)
                norm_stats(x1, stats2, mv2, var_eps2, var2_ready, norm_step, n0 + 1)

            def norm2(b):
                n0 = post_base(b) + GATE_STEPS + RESIDUAL_STEPS
                normalize(b, xr, x1, mv2, rstd2, rstd2_ready).then_inc(norm_step, 1)
                dve.wait_ge(norm_step, n0 + 1)
                V.tensor_tensor(xr[:, :, :], xr[:, :, :], bc4(modbc[:, 2, :]), ALU.mult).then_inc(norm_step, 1)
                dve.wait_ge(norm_step, n0 + 2)
                V.tensor_tensor(xr[:, :, :], xr[:, :, :], bc4(modbc[:, 1, :]), ALU.add).then_inc(h2_ready, 1)

            def take_logits(b, job):
                dve.wait_ge(misc_ready, job + 1)
                V.tensor_copy(logits[:, ds(b * NQ, NQ), :], misc[:, 0:NQ * E].rearrange("p (i e) -> p i e", i=NQ))\
                 .then_inc(misc_used, 1)

            def batch(b, post, prep):
                job = {j: first_job(b) + n for n, j in enumerate(jobs(post, prep))}
                for h in range(H):
                    maxima(b, h)
                    if h == 1:
                        if post:
                            dve.wait_ge(av_done, b * 4 + 2)
                        take_v(b, job["V"])
                        if post:
                            make_silu_col(b - 1)
                    if h == 2 and post:
                        normalize_y(b - 1, 3, job["den3"])
                    if h == 3:
                        if post:
                            gates(b - 1, job["mod"])
                    if h == 4 and post:
                        residual(b - 1, job["proj"])
                    if h == 5:
                        if prep:
                            norm1_stats(b + 1)
                    if h == 6:
                        normalize_y(b, 0, job["den0"])
                        if prep:
                            norm1_apply(b + 1)
                    if h == 7 and post:
                        norm2(b - 1)
                    if h == 8 and prep:
                        take_qk(0, job["q"])
                    if h == 9 and prep:
                        take_qk(1, job["k"])
                    if h == 10:
                        normalize_y(b, 1, job["den1"])
                    if h == 12 and post:
                        take_logits(b - 1, job["logits"])
                    if h == 14:
                        normalize_y(b, 2, job["den2"])

            norm1_stats(0)
            norm1_apply(0)
            take_qk(0, 1)
            take_qk(1, 2)
            for n in range(T // 8):
                i = n // 16
                dve.wait_ge(hidden_used, 2 * n + 2)
                if n >= 4:
                    dve.wait_ge(stage_sent[n % 4], 16 * (n // 4))
                V.tensor_scalar(stage[:, n % 4, 0:P * (i + 1)], turned_bank[n % 3][:, 0:P * (i + 1)],
                                fire[:, 4:5], None, ALU.add).then_inc(stage_ready, 1)
            dve.wait_ge(bias_masked, NQ)
            batch(0, False, True)
            with dve.Fori(1, B - 1) as b:
                batch(b, True, True)
            batch(B - 1, True, False)
            make_silu_col(B - 1)
            e0 = EPILOGUE
            normalize_y(B - 1, 3, e0)
            gates(B - 1, e0 + 1)
            residual(B - 1, e0 + 2)
            norm2(B - 1)
            take_logits(B - 1, e0 + 4)

            dve.wait_ge(misc_used, e0 + 5)
            te = [P, TOK, E]

            def e_bc(ap):
                return ap.unsqueeze(1).to_broadcast(te)

            def t_bc(ap):
                return ap.unsqueeze(2).to_broadcast(te)

            V.tensor_scalar(iota_e1[:, :], iota_e[:, :], -float(E), None, ALU.add)
            V.tensor_reduce(top, logits[:, :, :], AX.X, ALU.max).then_inc(top_ready, 1)
            dve.wait_ge(top_ready, 1)
            chain(V.tensor_tensor(wide, logits[:, :, :], t_bc(top), ALU.is_equal))
            chain(V.tensor_tensor(wide2, wide, e_bc(iota_e1[:, :]), ALU.mult))
            chain(V.tensor_reduce(top_e, wide2, AX.X, ALU.min))
            V.tensor_tensor(one_hot[:, :, :], e_bc(iota_e1[:, :]), t_bc(top_e), ALU.is_equal)\
             .then_inc(one_hot_made, 1)
            dve.wait_ge(score_exp, 1)
            chain(V.tensor_scalar(score, score, 1.0, None, ALU.add))
            chain(V.reciprocal(score, score))
            dve.wait_ge(rows_loaded, 16)
            V.tensor_tensor(rows_all, rows_all, score.unsqueeze(2).to_broadcast([P, TOK, C]), ALU.mult)\
             .then_inc(masked_ready, 1)
            dve.wait_ge(ranks_ready, 1)
            tot = score_bank[1][:, 0:E]
            chain(V.tensor_tensor(wide3, iota_k[:, :].unsqueeze(1).to_broadcast([P, E, TOK]),
                                  tot.unsqueeze(2).to_broadcast([P, E, TOK]), ALU.is_lt))
            chain(V.tensor_reduce(tiles_of[:, :], wide3, AX.X, ALU.add))
            chain(V.tensor_tensor(sq, lower[:, :, :], tiles_of[:, :].unsqueeze(1).to_broadcast([P, E, E]),
                                  ALU.mult))
            chain(V.tensor_reduce(first_tile[:, :], sq, AX.X, ALU.add))
            chain(V.tensor_tensor(end_tile[:, :], first_tile[:, :], tiles_of[:, :], ALU.add))
            chain(V.tensor_scalar(base_row[:, :], first_tile[:, :], float(TOK), float(P), ALU.add, ALU.mult))
            chain(V.tensor_tensor(wide, score_bank[0][:, :].rearrange("p (t e) -> p t e", e=E),
                                  e_bc(base_row[:, :]), ALU.add))
            chain(V.tensor_tensor(wide2, wide, one_hot[:, :, :], ALU.mult))
            chain(V.tensor_reduce(dest_f[:, :], wide2, AX.X, ALU.add))
            V.tensor_copy(dest[:, :], dest_f[:, :]).then_inc(dest_ready, 1)
            half = SORTED // 2
            for q, buf in ((0, cmp_t), (1, cmp_t2)):
                v = buf[:, 0:half * E].rearrange("p (t e) -> p t e", e=E)
                chain(V.tensor_tensor(v, end_tile[:, :].unsqueeze(1).to_broadcast([P, half, E]),
                                      iota_t[:, half * q:half * q + half].unsqueeze(2).to_broadcast([P, half, E]),
                                      ALU.is_le))
                chain(V.tensor_reduce(expert_f[:, TOK + half * q:TOK + half * q + half], v, AX.X, ALU.add))
            chain(V.tensor_scalar(expert_f[:, TOK:SLOTS], expert_f[:, TOK:SLOTS], float(E - 1), None, ALU.min))
            V.tensor_copy(expert[:, :], expert_f[:, :]).then_inc(expert_ready, 1)
            for k in range(6):
                dst = w_up_all[:, E, k * P:k * P + P] if k < 4 else w_dn_all[:, E, (k - 4) * P:(k - 4) * P + P]
                dve.wait_ge(shared_T, k + 1)
                V.tensor_copy(dst, score_bank[2][:, 0:P]).then_inc(shared_copied, 1)
            with dve.Fori(0, SLOTS // 2) as n:
                for k in range(2):
                    t = n * 2 + k
                    dve.wait_ge(rowT_ready, t + 1)
                    V.tensor_copy(rowT[:, k, :], score_bank[k][:, 0:P]).then_inc(rowT_copied, 1)
                    dve.wait_ge(gate_done, t + 1)
                    V.tensor_tensor(act_h[:, k, :], gated[:, k, :], turned_bank[k][:, F:2 * F], ALU.mult)\
                     .then_inc(act_ready, 1)
                    dve.wait_ge(down_ready, t + 1)
                    dve.wait_ge(row_stored[k], n * 16 + 16)
                    V.tensor_copy(row_out[:, k, :], [y_bank, misc][k][:, 0:C]).then_inc(out_copied, 1)
            dve.wait_ge(all_loaded, 32)
            dve.wait_ge(gathered, 16 * TOK)
            with dve.Fori(0, B) as b:
                r = ds(b * NQ, NQ)
                V.tensor_tensor(sh_all[:, r, :], sh_all[:, r, :], rows_all[:, r, :], ALU.add)\
                 .then_inc(final_step, 1)
                dve.wait_ge(final_step, b * 3 + 1)
                V.tensor_tensor(sh_all[:, r, :], sh_all[:, r, :], gb_all[:, ds(b, 1), :].to_broadcast([P, NQ, C]),
                                ALU.mult).then_inc(final_step, 1)
                dve.wait_ge(final_step, b * 3 + 2)
                V.tensor_tensor(x1_all[:, r, :], x1_all[:, r, :], sh_all[:, r, :], ALU.add)\
                 .then_inc(final_step, 1)

        @block.tensor
        def _(pe):
            mm = nc.tensor.matmul
            pe.sem_inc(turned_ready, 6)
            pe.sem_inc(turned_free, 3)
            pe.sem_inc(av_done, 2)
            pe.sem_inc(y_copied, 1)
            pe.wait_ge(consts_made, 3)
            pe.wait_ge(silu_made, 1)
            for m in range(2):
                last = mm(misc[:, m * B:m * B + B], wmod_cols[:, m * C:m * C + C], siluT[:, :], start=True, stop=True)
            last.then_inc(modT_ready, 1)

            def transpose4(src, job):
                for i in range(NQ):
                    last = mm(misc[:, i * P:i * P + P], src[:, i, :], ident[:, :], is_transpose=True,
                              start=True, stop=True)
                last.then_inc(misc_ready, 1)

            def xT(b, job):
                pe.wait_ge(xn_ready, b + 1)
                if not (isinstance(job, int) and job == 0):
                    pe.wait_ge(misc_used, job)
                transpose4(xt, job)

            def qk_of(mat, job):
                pe.wait_ge(misc_used, job)
                mm(misc[:, :], Wqk[:, mat, :], hT[:, :], start=True, stop=True).then_inc(misc_ready, 1)

            def v_of(b, job):
                pe.wait_ge(misc_used, job)
                for i in range(NQ):
                    last = mm(misc[:, i * C:i * C + C], hT[:, i * P:i * P + P], Wv[:, :],
                              start=True, stop=True)
                last.then_inc(misc_ready, 1)

            def scores(b, h):
                u, g = b * 16 + h, h // 4
                if h % 4 == 0:
                    pe.wait_ge(feat_ready[g % 2], b * 2 * FEAT + FEAT * (g // 2 + 1))
                for i in range(NQ):
                    k, c0 = (0, i * P) if i < 2 else (i - 1, 0)
                    if i != 1:
                        pe.wait_ge(scores_free, u * 3 + k + 1)
                    n = P * (i + 1)
                    last = mm(score_bank[k][:, c0:c0 + n], qf[:, g % 2, h % 4, i * P:i * P + P],
                              kf[:, g % 2, h % 4, 0:n], start=True, stop=True)
                    if i:
                        last.then_inc(scores_ready, 1)

            def turn(b, h):
                u, s = b * 16 + h, h % 2
                pe.wait_ge(negmax_ready, u + 1)
                for k, blocks in enumerate(BANKS):
                    pe.wait_ge(turned_free, u * 3 + k + 1)
                    for j, i0, c0 in blocks:
                        for i in range(i0, NQ):
                            dst = turned_bank[k][:, c0 + (i - i0) * P:c0 + (i - i0) * P + P]
                            mm(dst, biased[:, s, OFF[i] + j * P:OFF[i] + j * P + P], ident[:, :],
                               is_transpose=True, start=True, stop=False)
                            last = mm(dst, ones_bf[:, :], negmax[:, s, i, :], start=False, stop=True)
                    last.then_inc(turned_ready, 1)

            def values(b, g):
                pe.wait_ge(turned_free, b * 48 + 12 * g + 12 + 3)
                pe.wait_ge(y_copied, b * 4 + g + 1)
                for j in range(NQ):
                    n = P * (NQ - j)
                    for hh in range(4):
                        h = 4 * g + hh
                        c0 = (h % 8) * CAUSAL + PCOL[j]
                        last = mm(y_bank[W * hh:W * hh + 2 * HD, j * P:T], vaug[:, j, h, :], probs[:, c0:c0 + n],
                                  start=(j == 0), stop=(j == NQ - 1))
                last.then_inc(av_done, 1)

            def denominators(b, g, job):
                pe.wait_ge(y_copied, b * 4 + g + 2)
                pe.wait_ge(misc_used, job)
                mm(misc[:, :], pick_den[:, :], yT[:, g, :], start=True, stop=True).then_inc(misc_ready, 1)

            def modulation(b, job):
                pe.wait_ge(silu_col_made, b + 1)
                pe.wait_ge(misc_used, job)
                mm(misc[:, :], silu_col[:, :], wmod_bc[:, :], start=True, stop=True).then_inc(misc_ready, 1)

            def project(b, job):
                pe.wait_ge(yn_ready, b * 4 + 4)
                pe.wait_ge(misc_used, job)
                for i in range(NQ):
                    for g in range(4):
                        last = mm(misc[:, i * C:i * C + C], yT[:, g, i * P:i * P + P], Wproj[:, g, :],
                                  start=(g == 0), stop=(g == 3))
                last.then_inc(misc_ready, 1)

            def turn_h2(b, job):
                pe.wait_ge(h2_ready, b + 1)
                pe.wait_ge(misc_used, job)
                transpose4(xr, job)

            def router(b, job):
                pe.wait_ge(misc_used, job)
                for i in range(NQ):
                    last = mm(misc[:, i * E:i * E + E], h2T[:, i * P:i * P + P], routerT[:, :], start=True, stop=True)
                last.then_inc(misc_ready, 1)

            def batch(b, post, prep):
                job = {j: first_job(b) + n for n, j in enumerate(jobs(post, prep))}
                for h in range(H):
                    if h < H - 1:
                        scores(b, h + 1)
                    elif prep:
                        scores(b + 1, 0)
                    turn(b, h)
                    if h == 0:
                        if post:
                            values(b - 1, 3)
                        v_of(b, job["V"])
                    if h == 1 and post:
                        denominators(b - 1, 3, job["den3"])
                    if h == 2 and post:
                        modulation(b - 1, job["mod"])
                    if h == 3 and post:
                        project(b - 1, job["proj"])
                    if h == 4:
                        pe.wait_ge(misc_used, job["V"] + 1)
                        values(b, 0)
                    if h == 5:
                        denominators(b, 0, job["den0"])
                    if h == 6 and prep:
                        xT(b + 1, job["xT"])
                    if h == 7 and prep:
                        qk_of(0, job["q"])
                    if h == 8:
                        values(b, 1)
                        if prep:
                            qk_of(1, job["k"])
                    if h == 9:
                        denominators(b, 1, job["den1"])
                    if h == 10 and post:
                        turn_h2(b - 1, job["h2T"])
                    if h == 11 and post:
                        router(b - 1, job["logits"])
                    if h == 12:
                        values(b, 2)
                    if h == 13:
                        denominators(b, 2, job["den2"])

            pe.wait_ge(params_loaded, 16 * 20)
            pe.wait_ge(modT_copied, 1)
            xT(0, 0)
            qk_of(0, 1)
            qk_of(1, 2)
            for n in range(T // 4):
                i, pair = n // 32, n // 2
                pe.wait_ge(hidden_ready, n + 1)
                if n % 2 == 0 and pair >= 3:
                    pe.wait_ge(stage_ready, pair - 2)
                mm(turned_bank[pair % 3][64 * (n % 2):64 * (n % 2) + 64, 0:P * (i + 1)], w2_bd,
                   hidden[:, n % 4, 0:P * (i + 1)], start=True, stop=True).then_inc(hidden_used, 1)
            pe.wait_ge(stage_ready, T // 8)
            scores(0, 0)
            batch(0, False, True)
            with pe.Fori(1, B - 1) as b:
                batch(b, True, True)
            batch(B - 1, True, False)
            values(B - 1, 3)
            e0 = EPILOGUE
            denominators(B - 1, 3, e0)
            modulation(B - 1, e0 + 1)
            project(B - 1, e0 + 2)
            turn_h2(B - 1, e0 + 3)
            router(B - 1, e0 + 4)
            pe.wait_ge(one_hot_made, 1)
            hot = one_hot[:, :, :].rearrange("p t e -> p (t e)")
            rank = score_bank[0][:, :]
            mm(rank, before[:, :], hot, start=True, stop=False)
            for t in range(TOK - 1):
                left = TOK - 1 - t
                mm(rank[:, (t + 1) * E:TOK * E].rearrange("p (t e) -> p t e", e=E), ones_bf[:, :],
                   one_hot[:, t:t + 1, :].to_broadcast([P, left, E]), start=False, stop=(t == TOK - 2))
            for t in range(TOK):
                last = mm(score_bank[1][:, 0:E], ones_bf[:, :], one_hot[:, t, :], start=(t == 0), stop=(t == TOK - 1))
            last.then_inc(ranks_ready, 1)
            pe.wait_ge(shared_loaded, 16 * 6)
            for k in range(6):
                if k:
                    pe.wait_ge(shared_copied, k)
                mm(score_bank[2][:, 0:P], raw_shared[:, k, :], ident[:, :], is_transpose=True,
                   start=True, stop=True).then_inc(shared_T, 1)
            pe.wait_ge(shared_copied, 6)
            pe.wait_ge(expert_ready, 1)
            pe.wait_ge(w_loaded, 16 * (E + 4))

            def turn_row(t, k, n):
                pe.wait_ge(row_loaded[k], n * 16 + 16)
                mm(score_bank[k][:, 0:P], row_in[:, k, :], ident[:, :], is_transpose=True, start=True, stop=True)\
                    .then_inc(rowT_ready, 1)

            def pick(t):
                return pe.value_load(expert[0:1, ds(t, 1)], min_val=0, max_val=E)

            def up(t, k, e):
                pe.wait_ge(rowT_copied, t + 1)
                mm(turned_bank[k][:, :], rowT[:, k, :],
                   w_up_all[:, ds(e, 1), :].rearrange("p a n -> p (a n)"), start=True, stop=True).then_inc(up_ready, 1)

            def down(t, k, e):
                pe.wait_ge(act_ready, t + 1)
                tb = [score_bank[2], turned_bank[2]][k]
                for a in range(2):
                    last = mm(tb[:, a * P:a * P + P], act_h[:, k, a * P:a * P + P], ident[:, :],
                              is_transpose=True, start=True, stop=True)
                last.then_inc(actT_ready, 1)
                pe.wait_ge(actT_copied, t + 1)
                for a in range(2):
                    last = mm([y_bank, misc][k][:, 0:C], act_hT[:, k, a * P:a * P + P],
                              w_dn_all[:, ds(e, 1), a * C:a * C + C].rearrange("p a n -> p (a n)"),
                              start=(a == 0), stop=(a == 1))
                last.then_inc(down_ready, 1)

            with pe.Fori(0, SLOTS // 2) as n:
                for k in range(2):
                    t = n * 2 + k
                    e = pick(t)
                    turn_row(t, k, n)
                    up(t, k, e)
                    down(t, k, e)


_INS = ['L0_attn_x', 'L0_attn_Wqkv', 'L0_attn_bqkv', 'L0_attn_Wproj', 'L0_attn_bproj', 'L0_attn_w1', 'L0_attn_b1',
        'L0_attn_w2', 'L0_attn_b2', 'L0_attn_c_param', 'L0_attn_L_multiplier', 'L0_ffn_w_router',
        'L0_ffn_gate_up_proj', 'L0_ffn_down_proj', 'L0_ffn_w_gate', 'L0_ffn_w_up', 'L0_ffn_w_down', 'L0_c', 'L0_wmod']


def kernel(**inputs):
    import numpy as _np
    import concourse.bacc as _bacc
    from concourse import mybir as _mybir
    from concourse.bass_utils import run_bass_kernel_spmd as _run

    nc = _bacc.Bacc("TRN2", target_bir_lowering=False, num_devices=1)
    arrays, args = {}, []
    for name in _INS:
        a = _np.ascontiguousarray(inputs[name])
        if a.ndim == 0:
            a = a.reshape(1)
        arrays[f"in_{name}_dram"] = a
        args.append(nc.dram_tensor(f"in_{name}_dram", a.shape, _mybir.dt.from_np(a.dtype), kind="ExternalInput").ap())
    args.append(nc.dram_tensor("out_0_dram", (B, T, C), _mybir.dt.float32, kind="ExternalOutput").ap())
    bass_adaln_block(nc, *args)
    r = _run(nc, [arrays], core_ids=[0])
    return r.results[0]["out_0_dram"]
```

```python
import concourse.bass as bass
from concourse import mybir
from contextlib import ExitStack

B, T, C, H = 8, 512, 128, 16
HD = C // H
P = 128
NQ = T // P
W = 32
E, F = 16, 256
TOK = B * T // P
SORTED = 48
SLOTS = TOK + SORTED
OFF = [i * (i + 1) // 2 * P for i in range(NQ + 1)]
CAUSAL = OFF[NQ]
MASKED = -1.0e30
ROW = C + 1
NOBODY = 1 << 20
DEEP = 4
TERMS_Q = (0, 0, 1, 1, 0, 2)
TERMS_K = (0, 1, 0, 1, 2, 0)
KR = HD * len(TERMS_Q)
FEAT = 16 * 2 * len(TERMS_Q)
BANKS = [[(0, 0, 0)], [(1, 1, 0), (3, 3, 3 * P)], [(2, 2, 0)]]
BANK_COLS = [4 * P, 4 * P, 2 * P]
PCOL = {0: 0, 1: 4 * P, 3: 7 * P, 2: 8 * P}

POST = ("den3", "mod", "proj", "h2T", "logits")
PREP = ("xT", "q", "k")
ORDER = ("V", "den3", "mod", "proj", "den0", "xT", "q", "k", "den1", "h2T", "logits", "den2")


def jobs(post, prep):
    return [j for j in ORDER if (post or j not in POST) and (prep or j not in PREP)]


def first_job(b, last=False):
    if isinstance(b, int) and b == 0:
        return len(PREP)
    return (b - 1) * len(ORDER) + (len(PREP) + len(jobs(False, True)))


EPILOGUE = first_job(B - 1) + len(jobs(True, False))


def bass_adaln_block(nc, x_d, Wqkv_d, bqkv_d, Wproj_d, bproj_d, w1_d, b1_d, w2_d, b2_d, c_param_d, L_mult_d,
                     w_router_d, gate_up_d, down_d, w_gate_d, w_up_d, w_down_d, cond_d, wmod_d, out_d):
    f32, bf16, i32 = mybir.dt.float32, mybir.dt.bfloat16, mybir.dt.int32
    ALU, ACT, AX = mybir.AluOpType, mybir.ActivationFunctionType, mybir.AxisListType
    ds = bass.ds
    ctx = ExitStack()
    with ctx:
        ctx.enter_context(nc.allow_non_contiguous_dma(reason="small parameter loads"))

        def sb(name, shape, dt=f32):
            return ctx.enter_context(nc.sbuf_tensor(name, shape, dt))

        def sem(name):
            return ctx.enter_context(nc.semaphore(name))

        x1_d = nc.dram_tensor("x1_scratch", (B * T, C), f32, kind="Internal").ap()
        rows_d = nc.dram_tensor("ffn_rows", (B * T, C), f32, kind="Internal").ap()
        sorted_d = nc.dram_tensor("sorted_rows", (SORTED * P, ROW), f32, kind="Internal").ap()
        routed_d = nc.dram_tensor("routed_out", (B * T, C), f32, kind="Internal").ap()

        ident = sb("ident", [P, P])
        neg_ident = sb("neg_ident", [P, P], bf16)
        ones_bf = sb("ones_bf", [P, P], bf16)
        pick_den = sb("pick_den", [P, P])
        empty_row = sb("empty_row", [P, ROW])
        neg_half = sb("neg_half", [P, NQ])
        Wv = sb("Wv", [P, C])
        Wqk = sb("Wqk", [P, 2, C])
        Wproj = sb("Wproj", [P, 4, C])
        wmod_bc = sb("wmod_bc", [P, 4 * C])
        bq = sb("bq", [P, 2])
        bv_bc = sb("bv_bc", [P, C])
        bproj_bc = sb("bproj_bc", [P, C])
        modT = sb("modT", [P, B, 2])
        siluT = sb("siluT", [P, B])
        routerT = sb("routerT", [P, E])
        bias = sb("bias", [P, H * CAUSAL])
        bias_v = bias[:, :].rearrange("p (h s) -> p h s", h=H)
        qf = sb("qf", [KR, 2, 4, T], bf16)
        kf = sb("kf", [KR, 2, 4, T], bf16)
        probs = sb("probs", [P, 8 * CAUSAL])
        biased = sb("biased", [P, 2, CAUSAL])
        rowmax = sb("rowmax", [P, 2, NQ], bf16)
        vaug = sb("vaug", [P, NQ, H, 2 * HD])
        yT = sb("yT", [P, 4, T])
        den = sb("den", [P, T])
        hT = sb("hT", [P, T])
        xt = sb("xt", [P, NQ, C])
        xr = sb("xr", [P, NQ, C])
        x1 = sb("x1", [P, NQ, C])
        h2T = sb("h2T", [P, T])
        qk32 = sb("qk32", [P, 2, T])
        rest = sb("rest", [P, T])
        parts = sb("parts", [P, 2, 3, T], bf16)
        stats = sb("stats", [P, NQ, 6])
        mv = sb("mv", [P, NQ, 2])
        var_eps = sb("var_eps", [P, NQ])
        rstd = sb("rstd", [P, NQ])
        stats2 = sb("stats2", [P, NQ, 6])
        mv2 = sb("mv2", [P, NQ, 2])
        var_eps2 = sb("var_eps2", [P, NQ])
        rstd2 = sb("rstd2", [P, NQ])
        modbc = sb("modbc", [P, 4, C])
        absg = sb("absg", [P, 2, C])
        sgn = sb("sgn", [P, 2, C])
        silu_col = sb("silu_col", [P, P])
        gb_all = sb("gb_all", [P, B, C])
        logits = sb("logits", [P, TOK, E])
        at = 0

        def setup_view(cols):
            nonlocal at
            at += cols
            return probs[:, at - cols:at]

        YW = 2 * T - 4
        hidden = setup_view(4 * T).rearrange("p (r n) -> p r n", r=4)
        stage = setup_view(4 * T).rearrange("p (r n) -> p r n", r=4)
        dist = setup_view(YW)
        dist_i = setup_view(YW).bitcast(i32)
        pos_i = setup_view(P).bitcast(i32)
        pnorm = setup_view(P)
        slope = setup_view(P)
        w2_bd = setup_view(4 * H)
        fire = setup_view(8)
        wmod_cols = setup_view(2 * C)
        condT = setup_view(B)
        sig = setup_view(B)
        Wqk_raw = setup_view(2 * C)
        at2 = 0

        def ffn_view(cols):
            nonlocal at2
            at2 += cols
            return bias[:, at2 - cols:at2]

        w_up_all = ffn_view((E + 1) * 2 * F).rearrange("p (e n) -> p e n", e=E + 1)
        w_dn_all = ffn_view((E + 1) * 2 * C).rearrange("p (e n) -> p e n", e=E + 1)
        rows_all = ffn_view(TOK * ROW).rearrange("p (t c) -> p t c", t=TOK)
        row_in = ffn_view(DEEP * ROW).rearrange("p (k c) -> p k c", k=DEEP)
        rowT = ffn_view(2 * P).rearrange("p (k c) -> p k c", k=2)
        gated = ffn_view(2 * F).rearrange("p (k c) -> p k c", k=2)
        act_h = ffn_view(2 * F).rearrange("p (k c) -> p k c", k=2)
        act_hT = ffn_view(2 * F).rearrange("p (k c) -> p k c", k=2)
        row_out = ffn_view(DEEP * C).rearrange("p (k c) -> p k c", k=DEEP)
        at = 0
        x1_all = setup_view(TOK * C).rearrange("p (t c) -> p t c", t=TOK)
        routed = setup_view(TOK * C).rearrange("p (t c) -> p t c", t=TOK)
        top = setup_view(TOK)
        top_e = setup_view(TOK)
        score = setup_view(TOK)
        raw_shared = setup_view(6 * C).rearrange("p (k c) -> p k c", k=6)
        wide = yT[:, 0, :].rearrange("p (t e) -> p t e", e=E)
        wide2 = yT[:, 1, :].rearrange("p (t e) -> p t e", e=E)
        sq = yT[:, 2, 0:E * E].rearrange("p (a b) -> p a b", b=E)
        wide3 = yT[:, 3, :].rearrange("p (e k) -> p e k", e=E)
        token = sb("token", [P, 8], i32)
        iota_e = sb("iota_e", [P, E])
        iota_e1 = sb("iota_e1", [P, E])
        iota_k = sb("iota_k", [P, TOK])
        iota_t = sb("iota_t", [P, SORTED])
        iota_i = sb("iota_i", [P, SORTED], i32)
        one_hot = sb("one_hot", [P, TOK, E], bf16)
        before = sb("before", [P, P], bf16)
        lower = sb("lower", [P, E, E])
        tiles_of = sb("tiles_of", [P, E])
        first_tile = sb("first_tile", [P, E])
        base_row = sb("base_row", [P, E])
        end_tile = sb("end_tile", [P, E])
        dest_f = sb("dest_f", [P, TOK])
        dest = sb("dest", [P, TOK], i32)
        expert_f = sb("expert_f", [P, SLOTS])
        expert = sb("expert", [P, SLOTS], i32)
        cmp_t = xt[:, :, :].rearrange("p a b -> p (a b)")
        cmp_t2 = xr[:, :, :].rearrange("p a b -> p (a b)")

        def bank(name):
            return ctx.enter_context(nc.psum_tensor(name, [P, T], f32))

        score_bank = [bank(f"score_bank{k}") for k in range(3)]
        turned_bank = [bank(f"turned_bank{k}") for k in range(3)]
        y_bank = bank("y_bank")
        misc = bank("misc")

        fire_loaded = sem("fire_loaded")
        params_loaded = sem("params_loaded")
        consts_made = sem("consts_made")
        pool_step = sem("pool_step")
        dve_step = sem("dve_step")
        dist_made = sem("dist_made")
        logs_taken = sem("logs_taken")
        slopes_made = sem("slopes_made")
        hidden_ready = sem("hidden_ready")
        hidden_used = sem("hidden_used")
        stage_ready = sem("stage_ready")
        stage_sent = [sem(f"stage_sent{r}") for r in range(4)]
        bias_masked = sem("bias_masked")
        cond_exp = sem("cond_exp")
        silu_made = sem("silu_made")
        modT_ready = sem("modT_ready")
        modT_copied = sem("modT_copied")
        setup_T = sem("setup_T")

        xt_loaded = sem("xt_loaded")
        xr_loaded = sem("xr_loaded")
        var_ready = sem("var_ready")
        rstd_ready = sem("rstd_ready")
        xn_ready = sem("xn_ready")
        var2_ready = sem("var2_ready")
        rstd2_ready = sem("rstd2_ready")
        parts_step = sem("parts_step")
        feat_ready = [sem(f"feat_ready{s}") for s in range(2)]
        scores_ready = sem("scores_ready")
        scores_free = sem("scores_free")
        turned_ready = sem("turned_ready")
        turned_free = sem("turned_free")
        av_done = sem("av_done")
        y_copied = sem("y_copied")
        den_ready = sem("den_ready")
        y_divided = sem("y_divided")
        misc_ready = sem("misc_ready")
        misc_used = sem("misc_used")
        waits_passed = sem("waits_passed")
        prep_step = sem("prep_step")
        norm_step = sem("norm_step")
        silu_col_made = sem("silu_col_made")
        x1_ready = sem("x1_ready")
        h2_ready = sem("h2_ready")
        x1_stored = sem("x1_stored")
        h2_stored = sem("h2_stored")
        rows_zeroed = sem("rows_zeroed")

        w_loaded = sem("w_loaded")
        shared_loaded = sem("shared_loaded")
        shared_T = sem("shared_T")
        shared_copied = sem("shared_copied")
        rows_loaded = sem("rows_loaded")
        one_hot_made = sem("one_hot_made")
        ranks_ready = sem("ranks_ready")
        score_exp = sem("score_exp")
        top_ready = sem("top_ready")
        dest_ready = sem("dest_ready")
        expert_ready = sem("expert_ready")
        numbers_made = sem("numbers_made")
        masked_ready = sem("masked_ready")
        scattered = sem("scattered")
        row_loaded = [sem(f"row_loaded{k}") for k in range(DEEP)]
        rowT_ready = sem("rowT_ready")
        rowT_copied = sem("rowT_copied")
        up_ready = sem("up_ready")
        gate_done = sem("gate_done")
        act_ready = sem("act_ready")
        actT_ready = sem("actT_ready")
        actT_copied = sem("actT_copied")
        down_ready = sem("down_ready")
        shared_added = sem("shared_added")
        out_copied = sem("out_copied")
        row_sent = [sem(f"row_sent{k}") for k in range(8)]
        scatters_issued = sem("scatters_issued")
        x1_loaded = sem("x1_loaded")
        routed_loaded = sem("routed_loaded")
        final_step = sem("final_step")
        out_stored = sem("out_stored")

        block = ctx.enter_context(nc.Block())

        @block.sync
        def _(sp):
            sp.dma_start(fire[:, 0:1], c_param_d.partition_broadcast(P)).then_inc(fire_loaded, 16)
            sp.dma_start(fire[:, 1:2], L_mult_d.partition_broadcast(P)).then_inc(fire_loaded, 16)
            for r in range(4):
                rows = slice(W * r, W * r + W)
                sp.dma_start(fire[rows, 2:3], w1_d.rearrange("a w -> w a")).then_inc(fire_loaded, 16)
                sp.dma_start(fire[rows, 3:4], b1_d.rearrange("(w a) -> w a", a=1)).then_inc(fire_loaded, 16)
                for n in range(2):
                    part = slice(W * r + H * n, W * r + H * n + H)
                    sp.dma_start(fire[part, 4:5], b2_d.rearrange("(h a) -> h a", a=1)).then_inc(fire_loaded, 16)
            sp.wait_ge(consts_made, 1)
            for r in range(4):
                sp.dma_start(w2_bd[W * r:W * r + W, H * r:H * r + H], w2_d).then_inc(fire_loaded, 16)
            sp.dma_start(xt[:, :, :], x_d[0, :, :].rearrange("(i p) c -> p i c", p=P)).then_inc(xt_loaded, 16)
            for n in range(T // 8):
                i, q = n // 16, 8 * (n % 16)
                sp.wait_ge(stage_ready, n + 1)
                sp.dma_start(bias_v[q:q + 8, :, OFF[i]:OFF[i + 1]], stage[:, n % 4, 0:P * (i + 1)])\
                  .then_inc(stage_sent[n % 4], 16)

            def features(b, g):
                s = g % 2
                for mat, terms, dst in ((0, TERMS_Q, qf), (1, TERMS_K, kf)):
                    for t, part in enumerate(terms):
                        sp.dma_start(dst[HD * t:HD * t + HD, s, :, :], parts[W * g:W * g + W, mat, part, :]).then_inc(feat_ready[s], 16)

            def batch(b, post, prep):
                if prep:
                    sp.dma_start(xt[:, :, :], x_d[ds(b + 1, 1), :, :].rearrange("b (i p) c -> p (b i) c", p=P))\
                      .then_inc(xt_loaded, 16)
                if post:
                    load_residual(b - 1)
                for g in (2, 3):
                    sp.wait_ge(scores_ready, (b * 16 + 4 * g - 4) * 3)
                    features(b, g)
                if post:
                    store_post(b - 1)
                if prep:
                    sp.wait_ge(parts_step, (b + 2) * 8)
                    for g in (0, 1):
                        sp.wait_ge(scores_ready, (b * 16 + 4 * g + 12) * 3)
                        features(b + 1, g)

            def load_residual(b):
                sp.dma_start(xr[:, :, :], x_d[ds(b, 1), :, :].rearrange("b (i p) c -> p (b i) c", p=P))\
                  .then_inc(xr_loaded, 16)

            def store_post(b):
                sp.wait_ge(x1_ready, b + 1)
                sp.dma_start(x1_d[ds(b * T, T), :].rearrange("(i p) c -> p i c", p=P), x1[:, :, :])\
                  .then_inc(x1_stored, 16)
                sp.wait_ge(h2_ready, b + 1)
                sp.dma_start(rows_d[ds(b * T, T), :].rearrange("(i p) c -> p i c", p=P), xr[:, :, :])\
                  .then_inc(h2_stored, 16)
                sp.wait_ge(h2_stored, (b + 1) * 16)

            sp.wait_ge(parts_step, 8)
            features(0, 0)
            features(0, 1)
            sp.wait_ge(misc_ready, 1)
            batch(0, False, True)
            with sp.Fori(1, B - 1) as b:
                sp.wait_ge(misc_ready, first_job(b))
                batch(b, True, True)
            sp.wait_ge(misc_ready, first_job(B - 1))
            batch(B - 1, True, False)
            sp.wait_ge(misc_ready, EPILOGUE)
            load_residual(B - 1)
            store_post(B - 1)
            sp.wait_ge(scores_free, 3 + 3 * 16 * B)
            for k, src in enumerate((w_gate_d[0:P, :], w_gate_d[P:F, :], w_up_d[0:P, :], w_up_d[P:F, :],
                                     w_down_d[:, 0:P], w_down_d[:, P:F])):
                sp.dma_start(raw_shared[:, k, :], src).then_inc(shared_loaded, 16)
            sp.dma_start(rows_all[:, :, 0:C], rows_d.rearrange("(t p) c -> p t c", p=P)).then_inc(rows_loaded, 16)
            sp.dma_start(w_up_all[:, 0:4, :], gate_up_d[0:4, :, :].rearrange("e k n -> k e n")).then_inc(w_loaded, 16)

            def load_shared(t, k):
                sp.dma_start(row_in[:, k, 0:C], rows_d[ds(t * P, P), :]).then_inc(row_loaded[k], 16)

            def load_sorted(t, k):
                sp.dma_start(row_in[:, k, :], sorted_d[ds((t - TOK) * P, P), :]).then_inc(row_loaded[k], 16)

            for k in range(DEEP):
                load_shared(k, k)
            sp.dma_start(x1_all, x1_d.rearrange("(t p) c -> p t c", p=P)).then_inc(x1_loaded, 16)
            for e in range(0, E, 4):
                if e:
                    sp.dma_start(w_up_all[:, e:e + 4, :], gate_up_d[e:e + 4, :, :].rearrange("e k n -> k e n"))\
                      .then_inc(w_loaded, 16)
                for e1 in range(e, e + 4):
                    sp.dma_start(w_dn_all[:, e1, :].rearrange("p (a n) -> p a n", a=2),
                                 down_d[e1, :, :].rearrange("(a p) n -> p a n", p=P)).then_inc(w_loaded, 16)
            with sp.Fori(1, TOK // DEEP) as n:
                for k in range(DEEP):
                    sp.wait_ge(rowT_copied, (n - 1) * DEEP + k + 1)
                    load_shared(n * DEEP + k, k)
            sp.wait_ge(scattered, 16 * TOK)
            with sp.Fori(TOK // DEEP, SLOTS // DEEP) as n:
                for k in range(DEEP):
                    sp.wait_ge(rowT_copied, (n - 1) * DEEP + k + 1)
                    load_sorted(n * DEEP + k, k)
            for k in range(8):
                sp.wait_ge(row_sent[k], 16 * (SORTED // 8))
            for b in range(B):
                sp.dma_start(routed[:, b * NQ:b * NQ + NQ, :],
                             routed_d[b * T:b * T + T, :].rearrange("(i p) c -> p i c", p=P))\
                  .then_inc(routed_loaded, 16)
            with sp.Fori(0, B) as b:
                sp.wait_ge(final_step, b * 2 + 2)
                sp.dma_start(out_d[ds(b, 1), :, :].rearrange("b (i p) c -> p (b i) c", p=P),
                             x1_all[:, ds(b * NQ, NQ), :]).then_inc(out_stored, 16)
            sp.wait_ge(out_stored, 16 * B)
            sp.wait_ge(x1_stored, 16 * B)
            sp.wait_ge(rows_zeroed, 16)

        @block.gpsimd
        def _(pool):
            step = [0]

            def chain(ins):
                step[0] += 1
                ins.then_inc(pool_step, 1)
                pool.wait_ge(pool_step, step[0])

            pool.sem_inc(y_divided, 1)
            pool.memset(w2_bd, 0.0).then_inc(consts_made, 1)
            pool.wait_ge(consts_made, 1)
            for r in range(4):
                rows = slice(W * r, W * r + W)
                pool.iota(dist_i[rows, :], pattern=[[-1, YW]], base=r + T - 4, channel_multiplier=0)
                last = pool.iota(pos_i[rows, :], pattern=[[4, P]], base=r, channel_multiplier=0)
            last.then_inc(consts_made, 1)
            pool.wait_ge(consts_made, 2)
            chain(pool.memset(ident[:, :], 0.0))
            chain(pool.memset(neg_ident[:, :], 0.0))
            chain(pool.memset(pick_den[:, :], 0.0))
            chain(pool.memset(Wproj[:, :, :], 0.0))
            chain(pool.memset(before[:, :], 1.0))
            chain(pool.memset(lower[:, :, :], 1.0))
            pool.memset(ones_bf[:, :], 1.0)
            pool.memset(empty_row[:, 0:C], 0.0)
            pool.memset(empty_row[:, C:ROW].bitcast(i32), NOBODY)
            pool.memset(neg_half[:, :], -0.5)
            pool.memset(vaug[:, :, :, :], 1.0)
            pool.affine_select(out=ident[:, :], in_=ident[:, :], compare_op=ALU.not_equal, fill=1.0, base=0,
                               pattern=[[-1, P]], channel_multiplier=1)
            pool.affine_select(out=neg_ident[:, :], in_=neg_ident[:, :], compare_op=ALU.not_equal, fill=-1.0,
                               base=0, pattern=[[-1, P]], channel_multiplier=1)
            pick_v = pick_den[:, :].rearrange("p (a c) -> p a c", a=4)
            pool.affine_select(out=pick_v, in_=pick_v, compare_op=ALU.not_equal, fill=1.0, base=-HD,
                               pattern=[[-W, 4], [0, W]], channel_multiplier=1)
            pool.affine_select(out=before[:, :], in_=before[:, :], compare_op=ALU.is_gt, fill=0.0, base=0,
                               pattern=[[1, P]], channel_multiplier=-1)
            pool.affine_select(out=lower[:, :, :], in_=lower[:, :, :], compare_op=ALU.is_gt, fill=0.0, base=0,
                               pattern=[[1, E], [-1, E]], channel_multiplier=0)
            chain(pool.iota(iota_i[:, :], pattern=[[1, SORTED]], base=0, channel_multiplier=0))
            pool.tensor_copy(iota_t[:, :], iota_i[:, :])
            pool.tensor_copy(iota_e[:, :], iota_i[:, 0:E])
            chain(pool.tensor_copy(iota_k[:, :], iota_i[:, 0:TOK]))
            pool.tensor_scalar(iota_k[:, :], iota_k[:, :], float(P), 0.0, ALU.mult, ALU.add)
            pool.memset(expert_f[:, 0:TOK], float(E)).then_inc(consts_made, 1)
            pool.wait_ge(consts_made, 3)
            pool.dma_start(sorted_d.rearrange("(t p) c -> p t c", p=P),
                           empty_row[:, :].unsqueeze(1).to_broadcast([P, SORTED, ROW])).then_inc(rows_zeroed, 16)
            zero_row = empty_row[:, 0:1].to_broadcast([P, T])

            def split(b, job):
                for mat in range(2):
                    x32, n0 = qk32[:, mat, :], b * 8 + 4 * mat
                    pool.wait_ge(misc_used, job + mat + 1)
                    if mat == 0 and not (isinstance(b, int) and b == 0):
                        for s in range(2):
                            pool.wait_ge(feat_ready[s], b * 2 * FEAT)
                    pool.tensor_tensor(parts[:, mat, 0, :], x32, zero_row, ALU.add).then_inc(parts_step, 1)
                    pool.wait_ge(parts_step, n0 + 1)
                    pool.tensor_tensor(rest[:, :], x32, parts[:, mat, 0, :], ALU.subtract).then_inc(parts_step, 1)
                    pool.wait_ge(parts_step, n0 + 2)
                    pool.tensor_tensor(parts[:, mat, 1, :], rest[:, :], zero_row, ALU.add).then_inc(parts_step, 1)
                    pool.wait_ge(parts_step, n0 + 3)
                    pool.tensor_tensor(parts[:, mat, 2, :], rest[:, :], parts[:, mat, 1, :], ALU.subtract)\
                        .then_inc(parts_step, 1)
                    pool.wait_ge(parts_step, n0 + 4)

            def divide(b, g):
                pool.wait_ge(den_ready, b * 4 + g + 1)
                pool.tensor_tensor(yT[:, g, :], yT[:, g, :], den[:, :], ALU.mult).then_inc(y_divided, 1)

            def power(b, var, out, ready, done):
                pool.wait_ge(ready, b + 1)
                pool.tensor_tensor(out[:, :], var[:, :], neg_half[:, :], ALU.pow).then_inc(done, 1)

            power(0, var_eps, rstd, var_ready, rstd_ready)
            split(0, 1)
            for r in range(4):
                pool.wait_ge(stage_sent[r], 16 * (T // 8 // 4))
            for i in range(NQ):
                d = bias_v[:, :, OFF[i] + P * i:OFF[i] + P * i + P]
                pool.affine_select(out=d, in_=d, compare_op=ALU.is_ge, fill=MASKED, base=0,
                                   pattern=[[0, H], [-1, P]], channel_multiplier=1).then_inc(bias_masked, 1)
            def batch(b, post, prep):
                job = {j: first_job(b) + n for n, j in enumerate(jobs(post, prep))}
                if post:
                    divide(b - 1, 3)
                    power(b - 1, var_eps2, rstd2, var2_ready, rstd2_ready)
                if prep:
                    power(b + 1, var_eps, rstd, var_ready, rstd_ready)
                divide(b, 0)
                if prep:
                    split(b + 1, job["q"])
                divide(b, 1)
                divide(b, 2)

            batch(0, False, True)
            with pool.Fori(1, B - 1) as b:
                batch(b, True, True)
            batch(B - 1, True, False)
            divide(B - 1, 3)
            power(B - 1, var_eps2, rstd2, var2_ready, rstd2_ready)
            pool.wait_ge(rows_loaded, 16)
            pool.iota(rows_all[:, :, C:ROW].bitcast(i32).rearrange("p t a -> p (t a)"), pattern=[[P, TOK]], base=0,
                      channel_multiplier=1).then_inc(numbers_made, 1)
            pool.wait_ge(numbers_made, 1)
            pool.wait_ge(dest_ready, 1)
            pool.wait_ge(masked_ready, 1)
            pool.wait_ge(rows_zeroed, 16)
            for t in range(TOK):
                pool.indirect_dma_start(sorted_d, bass.IndirectOffsetOnAxis(ap=dest[:, t:t + 1], axis=0),
                                        rows_all[:, t, :], None).then_inc(scattered, 16)
            with pool.Fori(0, SORTED // 8) as m:
                for k in range(8):
                    pool.wait_ge(out_copied, m * 8 + TOK + k + 1)
                    pool.sem_inc(scatters_issued)
                    pool.indirect_dma_start(routed_d, bass.IndirectOffsetOnAxis(ap=token[:, k:k + 1], axis=0),
                                            row_out[:, k % DEEP, :], None, bounds_check=B * T - 1,
                                            oob_is_err=False).then_inc(row_sent[k], 16)

        @block.scalar
        def _(act):
            act.dma_start(condT, cond_d.rearrange("b k -> k b")).then_inc(params_loaded, 16)
            act.dma_start(wmod_cols, wmod_d[:, 0:2 * C]).then_inc(params_loaded, 16)
            act.dma_start(wmod_bc[:, :], wmod_d[:, 2 * C:6 * C]).then_inc(params_loaded, 16)
            act.dma_start(Wv[:, :], Wqkv_d[:, 2 * C:3 * C]).then_inc(params_loaded, 16)
            act.dma_start(Wqk_raw, Wqkv_d[:, 0:2 * C]).then_inc(params_loaded, 16)
            for m in range(2):
                for g in range(4):
                    part = bqkv_d[m * C + W * g:m * C + W * g + W].rearrange("(h d a) -> d h a", h=4, a=1)
                    act.dma_start(bq[W * g:W * g + W, m:m + 1], part).then_inc(params_loaded, 16)
            act.dma_start(bv_bc[:, :], bqkv_d[2 * C:3 * C].partition_broadcast(P)).then_inc(params_loaded, 16)
            act.dma_start(bproj_bc[:, :], bproj_d.partition_broadcast(P)).then_inc(params_loaded, 16)
            act.dma_start(routerT[:, :], w_router_d.rearrange("e k -> k e")).then_inc(params_loaded, 16)
            act.wait_ge(pool_step, 4)
            for hh in range(4):
                act.dma_start(Wproj[W * hh:W * hh + HD, :, :],
                              Wproj_d.rearrange("(g h d) n -> d g h n", h=4, d=HD)[:, :, hh, :])\
                   .then_inc(params_loaded, 16)
            act.wait_ge(dist_made, 2)
            act.activation(dist, dist, ACT.Ln, bias=1.0).then_inc(logs_taken, 1)
            act.activation(pnorm, pnorm, ACT.Ln, bias=1.0).then_inc(logs_taken, 1)
            act.wait_ge(params_loaded, 16 * 20)
            act.activation(sig, condT, ACT.Exp, scale=-1.0).then_inc(cond_exp, 1)
            def exps(b, h):
                u = b * 16 + h
                if h % 4 == 0:
                    act.wait_ge(av_done, b * 4 + h // 4 + 1)
                for k in range(3):
                    act.wait_ge(turned_ready, u * 3 + 6 + k + 1)
                    c0, n = (h % 8) * CAUSAL + 4 * P * k, BANK_COLS[k]
                    act.activation(probs[:, c0:c0 + n], turned_bank[k][:, 0:n], ACT.Exp).then_inc(turned_free, 1)

            def y_copy(b, g):
                act.wait_ge(av_done, b * 4 + g + 1 + 2)
                act.activation(yT[:, g, :], y_bank[:, :], ACT.Copy).then_inc(y_copied, 1)

            def modulate(b, job):
                act.wait_ge(misc_ready, job + 1)
                act.activation(hT[:, :], misc[:, :], ACT.Identity, bias=modT[:, ds(b, 1), 0],
                               scale=modT[:, ds(b, 1), 1]).then_inc(misc_used, 1)

            def take_qk(mat, job):
                act.wait_ge(misc_ready, job + 1)
                act.activation(qk32[:, mat, :], misc[:, :], ACT.Identity, bias=bq[:, mat:mat + 1],
                               scale=float(HD) ** -0.5 if mat == 0 else 1.0).then_inc(misc_used, 1)

            def take_den(b, g, job):
                act.wait_ge(misc_ready, job + 1)
                act.wait_ge(y_divided, b * 4 + g + 1)
                act.activation(den[:, :], misc[:, :], ACT.Ln).then_inc(misc_used, 1)
                act.wait_ge(misc_used, job + 1)
                act.activation(den[:, :], den[:, :], ACT.Exp, scale=-1.0).then_inc(den_ready, 1)

            def take_mod(b, job):
                act.wait_ge(misc_ready, job + 1)
                act.activation(modbc[:, :, :], misc[:, :].rearrange("p (m c) -> p m c", m=4), ACT.Copy)\
                   .then_inc(misc_used, 1)

            def take_logits(b, job):
                act.wait_ge(misc_ready, job + 1)
                act.activation(logits[:, ds(b * NQ, NQ), :],
                               misc[:, 0:NQ * E].rearrange("p (i e) -> p i e", i=NQ), ACT.Copy)\
                   .then_inc(misc_used, 1)

            def copy_h2T(job):
                act.wait_ge(misc_ready, job + 1)
                act.activation(h2T[:, :], misc[:, :], ACT.Copy).then_inc(misc_used, 1)

            def batch(b, post, prep):
                job = {j: first_job(b) + n for n, j in enumerate(jobs(post, prep))}
                for h in range(H):
                    exps(b, h)
                    if h == 0 and post:
                        y_copy(b - 1, 3)
                    if h == 4 and post:
                        act.wait_ge(misc_ready, job["proj"] + 1)
                    if h in (4, 8, 12):
                        y_copy(b, h // 4 - 1)
                    if h == 1 and post:
                        take_den(b - 1, 3, job["den3"])
                    if h == 2 and post:
                        take_mod(b - 1, job["mod"])
                    if h in (5, 9, 13):
                        take_den(b, h // 4 - 1, job[f"den{h // 4 - 1}"])
                    if h == 6 and prep:
                        modulate(b + 1, job["xT"])
                    if h == 7 and prep:
                        take_qk(0, job["q"])
                    if h == 8 and prep:
                        take_qk(1, job["k"])
                    if h == 10 and post:
                        copy_h2T(job["h2T"])
                    if h == 11 and post:
                        take_logits(b - 1, job["logits"])

            act.wait_ge(modT_copied, 1)
            modulate(0, 0)
            take_qk(0, 1)
            take_qk(1, 2)
            act.wait_ge(slopes_made, 1)
            for n in range(T // 4):
                i = n // 32
                if n >= 4:
                    act.wait_ge(hidden_used, n - 3)
                act.activation(hidden[:, n % 4, 0:P * (i + 1)], dist[:, T - 4 - 4 * n:T - 4 - 4 * n + P * (i + 1)],
                               ACT.Relu, bias=fire[:, 3:4], scale=slope[:, n:n + 1]).then_inc(hidden_ready, 1)
            act.wait_ge(hidden_used, T // 4)
            act.wait_ge(bias_masked, NQ)
            batch(0, False, True)
            with act.Fori(1, B - 1) as b:
                batch(b, True, True)
            batch(B - 1, True, False)
            y_copy(B - 1, 3)
            take_den(B - 1, 3, EPILOGUE)
            take_mod(B - 1, EPILOGUE + 1)
            copy_h2T(EPILOGUE + 3)
            take_logits(B - 1, EPILOGUE + 4)
            act.wait_ge(top_ready, 1)
            act.activation(score, top, ACT.Exp, scale=-1.0).then_inc(score_exp, 1)

            def gate(t, k):
                act.wait_ge(up_ready, t + 1)
                act.activation(gated[:, k % 2, :], turned_bank[k % 2][:, 0:F], ACT.Silu).then_inc(gate_done, 1)

            def copy_actT(t, k):
                act.wait_ge(actT_ready, t + 1)
                act.activation(act_hT[:, k % 2, :], [score_bank[2], turned_bank[2]][k % 2][:, 0:F], ACT.Copy)\
                   .then_inc(actT_copied, 1)

            gate(0, 0)
            gate(1, 1)
            copy_actT(0, 0)
            with act.Fori(0, SLOTS // 2 - 1) as n:
                for k in range(2):
                    gate(n * 2 + k + 2, k)
                    copy_actT(n * 2 + k + 1, k + 1)
            copy_actT(SLOTS - 1, 1)

        @block.vector
        def _(dve):
            step = [0]

            def chain(ins):
                step[0] += 1
                ins.then_inc(dve_step, 1)
                dve.wait_ge(dve_step, step[0])

            V = nc.vector

            def carry_wait():
                dve.sem_inc(waits_passed)

            dve.wait_ge(fire_loaded, 16 * 22)
            dve.wait_ge(consts_made, 2)

            def absolute(x):
                return V.scalar_tensor_tensor(x, x, -1.0, x, ALU.mult, ALU.max)

            chain(V.tensor_scalar(fire[:, 5:6], fire[:, 1:2], float(T), None, ALU.mult))
            chain(V.tensor_scalar(dist, dist_i, fire[:, 0:1], None, ALU.mult))
            chain(absolute(fire[:, 5:6]))
            chain(V.tensor_scalar(pnorm, pos_i, fire[:, 5:6], fire[:, 0:1], ALU.max, ALU.mult))
            absolute(dist)
            absolute(pnorm).then_inc(dist_made, 2)
            dve.wait_ge(logs_taken, 2)
            chain(V.tensor_scalar(pnorm, pnorm, 1e-6, None, ALU.add))
            chain(V.reciprocal(slope, pnorm))
            V.tensor_scalar(slope, slope, fire[:, 2:3], None, ALU.mult).then_inc(slopes_made, 1)
            dve.wait_ge(cond_exp, 1)
            chain(V.tensor_scalar(sig, sig, 1.0, None, ALU.add))
            chain(V.reciprocal(sig, sig))
            V.tensor_tensor(siluT[:, :], condT, sig, ALU.mult).then_inc(silu_made, 1)
            dve.wait_ge(params_loaded, 16 * 20)
            for m in range(2):
                V.tensor_copy(Wqk[:, m, :].rearrange("p (g d h) -> p g d h", g=4, d=HD),
                              Wqk_raw[:, m * C:m * C + C].rearrange("p (g h d) -> p g d h", g=4, d=HD))
            V.tensor_scalar(bq[:, 0:1], bq[:, 0:1], float(HD) ** -0.5, None, ALU.mult)
            dve.wait_ge(modT_ready, 1)
            V.tensor_copy(modT[:, :, 0], misc[:, 0:B])
            V.tensor_scalar(modT[:, :, 1], misc[:, B:2 * B], 1.0, None, ALU.add).then_inc(modT_copied, 1)
            V.memset(y_bank[:, :], 0.0)
            dve.sem_inc(scores_free, 3)

            def norm_stats(src, st, m, ve, ready, steps, base):
                for i in range(NQ):
                    last = V.bn_stats(st[:, i, :], src[:, i, :])
                last.then_inc(steps, 1)
                dve.wait_ge(steps, base + 1)
                carry_wait()
                for i in range(NQ):
                    last = V.bn_aggr(m[:, i, :], st[:, i, :])
                last.then_inc(steps, 1)
                dve.wait_ge(steps, base + 2)
                V.tensor_scalar(ve[:, :], m[:, :, 1], 1e-5, None, ALU.add).then_inc(ready, 1)

            def normalize(b, dst, src, m, r, rstd_sem):
                dve.wait_ge(rstd_sem, b + 1)
                for i in range(NQ):
                    last = V.tensor_scalar(dst[:, i, :], src[:, i, :], m[:, i, 0:1], r[:, i:i + 1],
                                           ALU.subtract, ALU.mult)
                return last

            GATE_STEPS, RESIDUAL_STEPS, NORM2_STEPS = 4, 3, 2

            def post_base(b):
                return b * (GATE_STEPS + RESIDUAL_STEPS + NORM2_STEPS)

            def norm1_stats(b):
                dve.wait_ge(xt_loaded, (b + 1) * 16)
                norm_stats(xt, stats, mv, var_eps, var_ready, prep_step, b * 2)

            def norm1_apply(b):
                normalize(b, xt, xt, mv, rstd, rstd_ready).then_inc(xn_ready, 1)

            def take_v(b, job):
                dve.wait_ge(misc_ready, job + 1)
                V.tensor_tensor(vaug[:, :, :, 0:HD], misc[:, :].rearrange("p (i h d) -> p i h d", i=NQ, d=HD),
                                bv_bc[:, :].rearrange("p (h d) -> p h d", d=HD).unsqueeze(1)
                                .to_broadcast([P, NQ, H, HD]), ALU.add).then_inc(misc_used, 1)

            def maxima(b, h):
                u, s = b * 16 + h, h % 2
                dve.wait_ge(turned_ready, u * 3 + 3)
                for i in range(NQ):
                    k, c0 = (0, i * P) if i < 2 else (i - 1, 0)
                    if i != 1:
                        dve.wait_ge(scores_ready, u * 3 + k + 1)
                        carry_wait()
                    n = P * (i + 1)
                    last = V.tensor_tensor_reduce(
                        out=biased[:, s, OFF[i]:OFF[i] + n], in0=score_bank[k][:, c0:c0 + n],
                        in1=bias_v[:, h, OFF[i]:OFF[i] + n], scale=1.0, scalar=MASKED, op0=ALU.add, op1=ALU.max,
                        accum_out=rowmax[:, s, i:i + 1])
                    if i:
                        last.then_inc(scores_free, 1)

            def make_silu_col(b):
                V.tensor_copy(silu_col[:, :], siluT[:, ds(b, 1)].to_broadcast([P, P])).then_inc(silu_col_made, 1)

            def gates(b, job):
                n0 = post_base(b)
                dve.wait_ge(misc_used, job + 1)
                g2 = modbc[:, 0:4:3, :]
                V.tensor_scalar(sgn[:, :, :], g2, 0.0, 2.0, ALU.is_ge, ALU.mult)
                V.tensor_scalar(modbc[:, 2, :], modbc[:, 2, :], 1.0, None, ALU.add)
                V.scalar_tensor_tensor(absg[:, :, :], g2, -1.0, g2, ALU.mult, ALU.max).then_inc(norm_step, 1)
                dve.wait_ge(norm_step, n0 + 1)
                V.tensor_scalar(absg[:, :, :], absg[:, :, :], 0.25, None, ALU.max).then_inc(norm_step, 1)
                dve.wait_ge(norm_step, n0 + 2)
                V.scalar_tensor_tensor(g2, sgn[:, :, :], -1.0, absg[:, :, :], ALU.add, ALU.mult)\
                 .then_inc(norm_step, 1)
                dve.wait_ge(norm_step, n0 + 3)
                V.tensor_copy(gb_all[:, ds(b, 1), :], modbc[:, 3:4, :]).then_inc(norm_step, 1)

            def bc4(ap):
                return ap.unsqueeze(1).to_broadcast([P, NQ, C])

            def residual(b, job):
                n0 = post_base(b) + GATE_STEPS
                dve.wait_ge(misc_ready, job + 1)
                if not (isinstance(b, int) and b == 0):
                    dve.wait_ge(x1_stored, b * 16)
                V.tensor_tensor(x1[:, :, :], misc[:, :].rearrange("p (i c) -> p i c", i=NQ), bc4(bproj_bc[:, :]),
                                ALU.add).then_inc(misc_used, 1)
                dve.wait_ge(misc_used, job + 1)
                V.tensor_tensor(x1[:, :, :], x1[:, :, :], bc4(modbc[:, 0, :]), ALU.mult).then_inc(norm_step, 1)
                dve.wait_ge(norm_step, n0 + 1)
                dve.wait_ge(xr_loaded, (b + 1) * 16)
                V.tensor_tensor(x1[:, :, :], x1[:, :, :], xr[:, :, :], ALU.add).then_inc(x1_ready, 1)
                dve.wait_ge(x1_ready, b + 1)
                norm_stats(x1, stats2, mv2, var_eps2, var2_ready, norm_step, n0 + 1)

            def norm2(b):
                n0 = post_base(b) + GATE_STEPS + RESIDUAL_STEPS
                normalize(b, xr, x1, mv2, rstd2, rstd2_ready).then_inc(norm_step, 1)
                dve.wait_ge(norm_step, n0 + 1)
                V.tensor_tensor(xr[:, :, :], xr[:, :, :], bc4(modbc[:, 2, :]), ALU.mult).then_inc(norm_step, 1)
                dve.wait_ge(norm_step, n0 + 2)
                V.tensor_tensor(xr[:, :, :], xr[:, :, :], bc4(modbc[:, 1, :]), ALU.add).then_inc(h2_ready, 1)

            def batch(b, post, prep):
                job = {j: first_job(b) + n for n, j in enumerate(jobs(post, prep))}
                for h in range(H):
                    maxima(b, h)
                    if h == 1:
                        if post:
                            dve.wait_ge(av_done, b * 4 + 2)
                        take_v(b, job["V"])
                        if post:
                            make_silu_col(b - 1)
                    if h == 3 and post:
                        gates(b - 1, job["mod"])
                    if h == 4 and post:
                        residual(b - 1, job["proj"])
                    if h == 5:
                        if prep:
                            norm1_stats(b + 1)
                    if h == 6:
                        if prep:
                            norm1_apply(b + 1)
                    if h == 7 and post:
                        norm2(b - 1)

            norm1_stats(0)
            norm1_apply(0)
            for n in range(T // 8):
                i = n // 16
                dve.wait_ge(hidden_used, 2 * n + 2)
                if n >= 4:
                    dve.wait_ge(stage_sent[n % 4], 16 * (n // 4))
                V.tensor_scalar(stage[:, n % 4, 0:P * (i + 1)], turned_bank[n % 3][:, 0:P * (i + 1)],
                                fire[:, 4:5], None, ALU.add).then_inc(stage_ready, 1)
            dve.wait_ge(bias_masked, NQ)
            batch(0, False, True)
            with dve.Fori(1, B - 1) as b:
                batch(b, True, True)
            batch(B - 1, True, False)
            make_silu_col(B - 1)
            e0 = EPILOGUE
            gates(B - 1, e0 + 1)
            residual(B - 1, e0 + 2)
            norm2(B - 1)

            dve.wait_ge(misc_used, e0 + 5)
            te = [P, TOK, E]

            def e_bc(ap):
                return ap.unsqueeze(1).to_broadcast(te)

            def t_bc(ap):
                return ap.unsqueeze(2).to_broadcast(te)

            V.tensor_scalar(iota_e1[:, :], iota_e[:, :], -float(E), None, ALU.add)
            V.tensor_reduce(top, logits[:, :, :], AX.X, ALU.max).then_inc(top_ready, 1)
            dve.wait_ge(top_ready, 1)
            chain(V.tensor_tensor(wide, logits[:, :, :], t_bc(top), ALU.is_equal))
            chain(V.tensor_tensor(wide2, wide, e_bc(iota_e1[:, :]), ALU.mult))
            chain(V.tensor_reduce(top_e, wide2, AX.X, ALU.min))
            V.tensor_tensor(one_hot[:, :, :], e_bc(iota_e1[:, :]), t_bc(top_e), ALU.is_equal)\
             .then_inc(one_hot_made, 1)
            dve.wait_ge(score_exp, 1)
            chain(V.tensor_scalar(score, score, 1.0, None, ALU.add))
            chain(V.reciprocal(score, score))
            dve.wait_ge(rows_loaded, 16)
            V.tensor_tensor(rows_all[:, :, 0:C], rows_all[:, :, 0:C], score.unsqueeze(2).to_broadcast([P, TOK, C]),
                            ALU.mult)\
             .then_inc(masked_ready, 1)
            dve.wait_ge(ranks_ready, 1)
            tot = score_bank[1][:, 0:E]
            chain(V.tensor_tensor(wide3, iota_k[:, :].unsqueeze(1).to_broadcast([P, E, TOK]),
                                  tot.unsqueeze(2).to_broadcast([P, E, TOK]), ALU.is_lt))
            chain(V.tensor_reduce(tiles_of[:, :], wide3, AX.X, ALU.add))
            chain(V.tensor_tensor(sq, lower[:, :, :], tiles_of[:, :].unsqueeze(1).to_broadcast([P, E, E]),
                                  ALU.mult))
            chain(V.tensor_reduce(first_tile[:, :], sq, AX.X, ALU.add))
            chain(V.tensor_tensor(end_tile[:, :], first_tile[:, :], tiles_of[:, :], ALU.add))
            chain(V.tensor_scalar(base_row[:, :], first_tile[:, :], float(P), None, ALU.mult))
            chain(V.tensor_tensor(wide, score_bank[0][:, :].rearrange("p (t e) -> p t e", e=E),
                                  e_bc(base_row[:, :]), ALU.add))
            chain(V.tensor_tensor(wide2, wide, one_hot[:, :, :], ALU.mult))
            chain(V.tensor_reduce(dest_f[:, :], wide2, AX.X, ALU.add))
            V.tensor_copy(dest[:, :], dest_f[:, :]).then_inc(dest_ready, 1)
            half = SORTED // 2
            for q, buf in ((0, cmp_t), (1, cmp_t2)):
                v = buf[:, 0:half * E].rearrange("p (t e) -> p t e", e=E)
                chain(V.tensor_tensor(v, end_tile[:, :].unsqueeze(1).to_broadcast([P, half, E]),
                                      iota_t[:, half * q:half * q + half].unsqueeze(2).to_broadcast([P, half, E]),
                                      ALU.is_le))
                chain(V.tensor_reduce(expert_f[:, TOK + half * q:TOK + half * q + half], v, AX.X, ALU.add))
            chain(V.tensor_scalar(expert_f[:, TOK:SLOTS], expert_f[:, TOK:SLOTS], float(E - 1), None, ALU.min))
            V.tensor_copy(expert[:, :], expert_f[:, :]).then_inc(expert_ready, 1)
            for k in range(6):
                dst = w_up_all[:, E, k * P:k * P + P] if k < 4 else w_dn_all[:, E, (k - 4) * P:(k - 4) * P + P]
                dve.wait_ge(shared_T, k + 1)
                V.tensor_copy(dst, score_bank[2][:, 0:P]).then_inc(shared_copied, 1)
            def row_t(t, k):
                dve.wait_ge(rowT_ready, t + 1)
                V.tensor_copy(rowT[:, k % 2, :], score_bank[k % 2][:, 0:P]).then_inc(rowT_copied, 1)

            def first_eight(m):
                return isinstance(m, int) and m == 0

            def row_t_sorted(t, k, m):
                dve.wait_ge(rowT_ready, t + 1)
                V.tensor_copy(rowT[:, k % 2, :], score_bank[k % 2][:, 0:P])
                if not first_eight(m):
                    dve.wait_ge(row_sent[k], m * 16)
                V.tensor_copy(token[:, k:k + 1], row_in[:, k % DEEP, C:ROW].bitcast(i32)).then_inc(rowT_copied, 1)

            def gate_up(t, k):
                dve.wait_ge(gate_done, t + 1)
                V.tensor_tensor(act_h[:, k % 2, :], gated[:, k % 2, :], turned_bank[k % 2][:, F:2 * F], ALU.mult)\
                 .then_inc(act_ready, 1)

            def out_shared(t, k, b):
                dve.wait_ge(down_ready, t + 1)
                V.tensor_tensor(row_out[:, k % DEEP, :], [y_bank, misc][k % 2][:, 0:C],
                                gb_all[:, ds(b, 1), :].rearrange("p a c -> p (a c)"), ALU.mult)\
                 .then_inc(out_copied, 1)
                dve.wait_ge(out_copied, t + 1)
                here = x1_all[:, ds(t, 1), :].rearrange("p a c -> p (a c)")
                V.tensor_tensor(here, here, row_out[:, k % DEEP, :], ALU.add).then_inc(shared_added, 1)

            def out_sorted(t, k, m):
                dve.wait_ge(down_ready, t + 1)
                if k >= 4:
                    dve.wait_ge(row_sent[k - 4], m * 16 + 16)
                elif not first_eight(m):
                    dve.wait_ge(row_sent[k + 4], m * 16)
                V.tensor_copy(row_out[:, k % DEEP, :], [y_bank, misc][k % 2][:, 0:C]).then_inc(out_copied, 1)

            row_t(0, 0)
            row_t(1, 1)
            row_t(2, 2)
            gate_up(0, 0)
            gate_up(1, 1)
            dve.wait_ge(x1_loaded, 16)
            with dve.Fori(0, TOK // 8 - 1) as m:
                for k in range(8):
                    t = m * 8 + k
                    row_t(t + 3, (k + 3) % 8)
                    gate_up(t + 2, k + 2)
                    out_shared(t, k, m * 2 + k // 4)
            for k in range(8):
                t = TOK - 8 + k
                if k < 5:
                    row_t(t + 3, (k + 3) % 8)
                else:
                    row_t_sorted(t + 3, (k + 3) % 8, 0)
                gate_up(t + 2, k + 2)
                out_shared(t, k, t // 4)

            def eight_sorted(m, last=False):
                for k in range(8):
                    t = m * 8 + TOK + k
                    if not (last and k >= 5):
                        row_t_sorted(t + 3, (k + 3) % 8, m if k < 5 else m + 1)
                    if not (last and k >= 6):
                        gate_up(t + 2, k + 2)
                    out_sorted(t, k, m)

            eight_sorted(0)
            with dve.Fori(1, SORTED // 8 - 1) as m:
                eight_sorted(m)
            eight_sorted(SORTED // 8 - 1, last=True)
            dve.wait_ge(shared_added, TOK)
            for b in range(B):
                r = slice(b * NQ, b * NQ + NQ)
                if b == 0:
                    dve.wait_ge(routed_loaded, 16 * B)
                V.tensor_tensor(routed[:, r, :], routed[:, r, :], gb_all[:, b:b + 1, :].to_broadcast([P, NQ, C]),
                                ALU.mult).then_inc(final_step, 1)
                dve.wait_ge(final_step, b * 2 + 1)
                V.tensor_tensor(x1_all[:, r, :], x1_all[:, r, :], routed[:, r, :], ALU.add).then_inc(final_step, 1)

        @block.tensor
        def _(pe):
            mm = nc.tensor.matmul
            pe.sem_inc(turned_ready, 6)
            pe.sem_inc(turned_free, 3)
            pe.sem_inc(av_done, 2)
            pe.sem_inc(y_copied, 1)
            pe.wait_ge(consts_made, 3)
            pe.wait_ge(silu_made, 1)
            for m in range(2):
                last = mm(misc[:, m * B:m * B + B], wmod_cols[:, m * C:m * C + C], siluT[:, :], start=True, stop=True)
            last.then_inc(modT_ready, 1)

            def transpose4(src, job):
                for i in range(NQ):
                    last = mm(misc[:, i * P:i * P + P], src[:, i, :], ident[:, :], is_transpose=True,
                              start=True, stop=True)
                last.then_inc(misc_ready, 1)

            def xT(b, job):
                pe.wait_ge(xn_ready, b + 1)
                if not (isinstance(job, int) and job == 0):
                    pe.wait_ge(misc_used, job)
                transpose4(xt, job)

            def qk_of(mat, job):
                pe.wait_ge(misc_used, job)
                mm(misc[:, :], Wqk[:, mat, :], hT[:, :], start=True, stop=True).then_inc(misc_ready, 1)

            def v_of(b, job):
                pe.wait_ge(misc_used, job)
                for i in range(NQ):
                    last = mm(misc[:, i * C:i * C + C], hT[:, i * P:i * P + P], Wv[:, :],
                              start=True, stop=True)
                last.then_inc(misc_ready, 1)

            def scores(b, h):
                u, g = b * 16 + h, h // 4
                if h % 4 == 0:
                    pe.wait_ge(feat_ready[g % 2], b * 2 * FEAT + FEAT * (g // 2 + 1))
                for i in range(NQ):
                    k, c0 = (0, i * P) if i < 2 else (i - 1, 0)
                    if i != 1:
                        pe.wait_ge(scores_free, u * 3 + k + 1)
                    n = P * (i + 1)
                    last = mm(score_bank[k][:, c0:c0 + n], qf[:, g % 2, h % 4, i * P:i * P + P],
                              kf[:, g % 2, h % 4, 0:n], start=True, stop=True)
                    if i:
                        last.then_inc(scores_ready, 1)

            def turn(b, h):
                u, s = b * 16 + h, h % 2
                pe.wait_ge(scores_free, u * 3 + 6)
                for k, blocks in enumerate(BANKS):
                    pe.wait_ge(turned_free, u * 3 + k + 1)
                    for j, i0, c0 in blocks:
                        for i in range(i0, NQ):
                            dst = turned_bank[k][:, c0 + (i - i0) * P:c0 + (i - i0) * P + P]
                            mm(dst, biased[:, s, OFF[i] + j * P:OFF[i] + j * P + P], ident[:, :],
                               is_transpose=True, start=True, stop=False)
                            last = mm(dst, rowmax[:, s, i:i + 1].to_broadcast([P, P]), neg_ident[:, :], start=False, stop=True)
                    last.then_inc(turned_ready, 1)

            def values(b, g):
                pe.wait_ge(turned_free, b * 48 + 12 * g + 12 + 3)
                pe.wait_ge(y_copied, b * 4 + g + 1)
                for j in range(NQ):
                    n = P * (NQ - j)
                    for hh in range(4):
                        h = 4 * g + hh
                        c0 = (h % 8) * CAUSAL + PCOL[j]
                        last = mm(y_bank[W * hh:W * hh + 2 * HD, j * P:T], vaug[:, j, h, :], probs[:, c0:c0 + n],
                                  start=(j == 0), stop=(j == NQ - 1))
                last.then_inc(av_done, 1)

            def denominators(b, g, job):
                pe.wait_ge(y_copied, b * 4 + g + 2)
                pe.wait_ge(misc_used, job)
                mm(misc[:, :], pick_den[:, :], yT[:, g, :], start=True, stop=True).then_inc(misc_ready, 1)

            def modulation(b, job):
                pe.wait_ge(silu_col_made, b + 1)
                pe.wait_ge(misc_used, job)
                mm(misc[:, :], silu_col[:, :], wmod_bc[:, :], start=True, stop=True).then_inc(misc_ready, 1)

            def project(b, job):
                pe.wait_ge(y_divided, b * 4 + 5)
                pe.wait_ge(misc_used, job)
                for i in range(NQ):
                    for g in range(4):
                        last = mm(misc[:, i * C:i * C + C], yT[:, g, i * P:i * P + P], Wproj[:, g, :],
                                  start=(g == 0), stop=(g == 3))
                last.then_inc(misc_ready, 1)

            def turn_h2(b, job):
                pe.wait_ge(h2_ready, b + 1)
                pe.wait_ge(misc_used, job)
                transpose4(xr, job)

            def router(b, job):
                pe.wait_ge(misc_used, job)
                for i in range(NQ):
                    last = mm(misc[:, i * E:i * E + E], h2T[:, i * P:i * P + P], routerT[:, :], start=True, stop=True)
                last.then_inc(misc_ready, 1)

            def batch(b, post, prep):
                job = {j: first_job(b) + n for n, j in enumerate(jobs(post, prep))}
                for h in range(H):
                    if h < H - 1:
                        scores(b, h + 1)
                    elif prep:
                        scores(b + 1, 0)
                    turn(b, h)
                    if h == 0:
                        if post:
                            values(b - 1, 3)
                        v_of(b, job["V"])
                    if h == 1 and post:
                        denominators(b - 1, 3, job["den3"])
                    if h == 2 and post:
                        modulation(b - 1, job["mod"])
                    if h == 3 and post:
                        project(b - 1, job["proj"])
                    if h == 4:
                        pe.wait_ge(misc_used, job["V"] + 1)
                        values(b, 0)
                    if h == 5:
                        denominators(b, 0, job["den0"])
                    if h == 6 and prep:
                        xT(b + 1, job["xT"])
                    if h == 7 and prep:
                        qk_of(0, job["q"])
                    if h == 8:
                        values(b, 1)
                        if prep:
                            qk_of(1, job["k"])
                    if h == 9:
                        denominators(b, 1, job["den1"])
                    if h == 10 and post:
                        turn_h2(b - 1, job["h2T"])
                    if h == 11 and post:
                        router(b - 1, job["logits"])
                    if h == 12:
                        values(b, 2)
                    if h == 13:
                        denominators(b, 2, job["den2"])

            pe.wait_ge(params_loaded, 16 * 20)
            pe.wait_ge(modT_copied, 1)
            xT(0, 0)
            qk_of(0, 1)
            qk_of(1, 2)
            for n in range(T // 4):
                i, pair = n // 32, n // 2
                pe.wait_ge(hidden_ready, n + 1)
                if n % 2 == 0 and pair >= 3:
                    pe.wait_ge(stage_ready, pair - 2)
                mm(turned_bank[pair % 3][64 * (n % 2):64 * (n % 2) + 64, 0:P * (i + 1)], w2_bd,
                   hidden[:, n % 4, 0:P * (i + 1)], start=True, stop=True).then_inc(hidden_used, 1)
            pe.wait_ge(stage_ready, T // 8)
            scores(0, 0)
            batch(0, False, True)
            with pe.Fori(1, B - 1) as b:
                batch(b, True, True)
            batch(B - 1, True, False)
            values(B - 1, 3)
            e0 = EPILOGUE
            denominators(B - 1, 3, e0)
            modulation(B - 1, e0 + 1)
            project(B - 1, e0 + 2)
            turn_h2(B - 1, e0 + 3)
            router(B - 1, e0 + 4)
            pe.wait_ge(one_hot_made, 1)
            hot = one_hot[:, :, :].rearrange("p t e -> p (t e)")
            rank = score_bank[0][:, :]
            mm(rank, before[:, :], hot, start=True, stop=False)
            for t in range(TOK - 1):
                left = TOK - 1 - t
                mm(rank[:, (t + 1) * E:TOK * E].rearrange("p (t e) -> p t e", e=E), ones_bf[:, :],
                   one_hot[:, t:t + 1, :].to_broadcast([P, left, E]), start=False, stop=(t == TOK - 2))
            for t in range(TOK):
                last = mm(score_bank[1][:, 0:E], ones_bf[:, :], one_hot[:, t, :], start=(t == 0), stop=(t == TOK - 1))
            last.then_inc(ranks_ready, 1)
            pe.wait_ge(shared_loaded, 16 * 6)
            for k in range(6):
                if k:
                    pe.wait_ge(shared_copied, k)
                mm(score_bank[2][:, 0:P], raw_shared[:, k, :], ident[:, :], is_transpose=True,
                   start=True, stop=True).then_inc(shared_T, 1)
            pe.wait_ge(shared_copied, 6)
            pe.wait_ge(expert_ready, 1)
            pe.wait_ge(w_loaded, 16 * (E + 4))

            def turn_row(t, k, n):
                pe.wait_ge(row_loaded[k], n * 16 + 16)
                mm(score_bank[k % 2][:, 0:P], row_in[:, k, 0:C], ident[:, :], is_transpose=True, start=True, stop=True)\
                    .then_inc(rowT_ready, 1)

            def weights_of(t, count):
                return nc.values_load_multi_w_load_instructions(
                    expert[0:1, ds(t, count)], engines=[mybir.EngineType.PE], min_val=0, max_val=E,
                    skip_runtime_bounds_check_because="a count of experts, cut to E - 1, or the constant E")[1]

            def up(t, k, e):
                pe.wait_ge(rowT_copied, t + 1)
                mm(turned_bank[k % 2][:, :], rowT[:, k % 2, :],
                   w_up_all[:, ds(e, 1), :].rearrange("p a n -> p (a n)"), start=True, stop=True).then_inc(up_ready, 1)

            def turn_act(t, k):
                pe.wait_ge(act_ready, t + 1)
                tb = [score_bank[2], turned_bank[2]][k % 2]
                for a in range(2):
                    last = mm(tb[:, a * P:a * P + P], act_h[:, k % 2, a * P:a * P + P], ident[:, :],
                              is_transpose=True, start=True, stop=True)
                last.then_inc(actT_ready, 1)

            def down(t, k, e):
                pe.wait_ge(actT_copied, t + 1)
                for a in range(2):
                    last = mm([y_bank, misc][k % 2][:, 0:C], act_hT[:, k % 2, a * P:a * P + P],
                              w_dn_all[:, ds(e, 1), a * C:a * C + C].rearrange("p a n -> p (a n)"),
                              start=(a == 0), stop=(a == 1))
                last.then_inc(down_ready, 1)

            turn_row(0, 0, 0)
            turn_row(1, 1, 0)
            up(0, 0, E)
            turn_row(2, 2, 0)
            up(1, 1, E)
            turn_act(0, 0)
            with pe.Fori(0, SLOTS // DEEP - 1) as n:
                e = weights_of(n * DEEP, DEEP + 2)
                for k in range(DEEP):
                    t = n * DEEP + k
                    up(t + 2, k + 2, e[k + 2])
                    turn_row(t + 3, (k + 3) % DEEP, n if k < 1 else n + 1)
                    turn_act(t + 1, k + 1)
                    down(t, k, e[k])
            e = weights_of(SLOTS - DEEP, DEEP)
            for k in range(DEEP):
                t, n = SLOTS - DEEP + k, SLOTS // DEEP - 1
                if k < 2:
                    up(t + 2, k + 2, e[k + 2])
                if k < 1:
                    turn_row(t + 3, k + 3, n)
                if k < 3:
                    turn_act(t + 1, k + 1)
                if k >= 2:
                    pe.wait_ge(out_copied, t - 1)
                down(t, k, e[k])


_INS = ['L0_attn_x', 'L0_attn_Wqkv', 'L0_attn_bqkv', 'L0_attn_Wproj', 'L0_attn_bproj', 'L0_attn_w1', 'L0_attn_b1',
        'L0_attn_w2', 'L0_attn_b2', 'L0_attn_c_param', 'L0_attn_L_multiplier', 'L0_ffn_w_router',
        'L0_ffn_gate_up_proj', 'L0_ffn_down_proj', 'L0_ffn_w_gate', 'L0_ffn_w_up', 'L0_ffn_w_down', 'L0_c', 'L0_wmod']


def kernel(**inputs):
    import numpy as _np
    import concourse.bacc as _bacc
    from concourse import mybir as _mybir
    from concourse.bass_utils import run_bass_kernel_spmd as _run

    nc = _bacc.Bacc("TRN2", target_bir_lowering=False, num_devices=1)
    arrays, args = {}, []
    for name in _INS:
        a = _np.ascontiguousarray(inputs[name])
        if a.ndim == 0:
            a = a.reshape(1)
        arrays[f"in_{name}_dram"] = a
        args.append(nc.dram_tensor(f"in_{name}_dram", a.shape, _mybir.dt.from_np(a.dtype), kind="ExternalInput").ap())
    args.append(nc.dram_tensor("out_0_dram", (B, T, C), _mybir.dt.float32, kind="ExternalOutput").ap())
    bass_adaln_block(nc, *args)
    r = _run(nc, [arrays], core_ids=[0])
    return r.results[0]["out_0_dram"]
```

```python
import concourse.bass as bass
from concourse import mybir
from contextlib import ExitStack

B, T, C, H = 8, 512, 128, 16
HD = C // H
P = 128
NQ = T // P
W = 32
E, F = 16, 256
TOK = B * T // P
SORTED = 48
SLOTS = TOK + SORTED
OFF = [i * (i + 1) // 2 * P for i in range(NQ + 1)]
CAUSAL = OFF[NQ]
MASKED = -1.0e30
ROW = C + 1
NOBODY = 1 << 20
DEEP = 4
TERMS_Q = (0, 0, 1, 1, 0, 2)
TERMS_K = (0, 1, 0, 1, 2, 0)
OCTETS = P // 8
BY_POOL = (2, 6)
KR = HD * len(TERMS_Q)
FEAT = 16 * len(TERMS_Q)
BANKS = [[(0, 0, 0)], [(1, 1, 0), (3, 3, 3 * P)], [(2, 2, 0)]]
BANK_COLS = [4 * P, 4 * P, 2 * P]
PCOL = {0: 0, 1: 4 * P, 3: 7 * P, 2: 8 * P}

POST = ("den1", "mod", "proj", "h2T", "logits")
PREP = ("xT", "q", "k")
ORDER = ("V", "den1", "mod", "xT", "proj", "q", "k", "den0", "h2T", "logits")


def jobs(post, prep):
    return [j for j in ORDER if (post or j not in POST) and (prep or j not in PREP)]


def first_job(b, last=False):
    if isinstance(b, int) and b == 0:
        return len(PREP)
    return (b - 1) * len(ORDER) + (len(PREP) + len(jobs(False, True)))


EPILOGUE = first_job(B - 1) + len(jobs(True, False))


def bass_adaln_block(nc, x_d, Wqkv_d, bqkv_d, Wproj_d, bproj_d, w1_d, b1_d, w2_d, b2_d, c_param_d, L_mult_d,
                     w_router_d, gate_up_d, down_d, w_gate_d, w_up_d, w_down_d, cond_d, wmod_d, out_d):
    f32, bf16, i32 = mybir.dt.float32, mybir.dt.bfloat16, mybir.dt.int32
    ALU, ACT, AX = mybir.AluOpType, mybir.ActivationFunctionType, mybir.AxisListType
    ds = bass.ds
    ctx = ExitStack()
    with ctx:
        ctx.enter_context(nc.allow_non_contiguous_dma(reason="small parameter loads"))

        def sb(name, shape, dt=f32):
            return ctx.enter_context(nc.sbuf_tensor(name, shape, dt))

        def sem(name):
            return ctx.enter_context(nc.semaphore(name))

        x1_d = nc.dram_tensor("x1_scratch", (B * T, C), f32, kind="Internal").ap()
        rows_d = nc.dram_tensor("ffn_rows", (B * T, C), f32, kind="Internal").ap()
        sorted_d = nc.dram_tensor("sorted_rows", (SORTED * P, ROW), f32, kind="Internal").ap()
        routed_d = nc.dram_tensor("routed_out", (B * T, C), f32, kind="Internal").ap()

        ident = sb("ident", [P, P])
        neg_ident = sb("neg_ident", [P, P], bf16)
        ones_bf = sb("ones_bf", [P, P], bf16)
        pick_den = sb("pick_den", [P, P])
        empty_row = sb("empty_row", [P, ROW])
        neg_half = sb("neg_half", [P, NQ])
        two = sb("two", [P, 1])
        Wv = sb("Wv", [P, C])
        Wqk = sb("Wqk", [P, 2, C])
        Wproj = sb("Wproj", [P, 2, C])
        wmod_bc = sb("wmod_bc", [P, 4 * C])
        bq = sb("bq", [P, 2])
        bv_bc = sb("bv_bc", [P, C])
        bproj_bc = sb("bproj_bc", [P, C])
        modT = sb("modT", [P, B, 2])
        siluT = sb("siluT", [P, B])
        routerT = sb("routerT", [P, E])
        bias = sb("bias", [P, H * CAUSAL])
        bias_v = bias[:, :].rearrange("p (h s) -> p h s", h=H)
        qf = sb("qf", [KR, 2, 4, T], bf16)
        kf = sb("kf", [KR, 2, 4, T], bf16)
        probs = sb("probs", [P, 8 * CAUSAL])
        biased = sb("biased", [P, 2, CAUSAL])
        rowmax = sb("rowmax", [P, 2, NQ], bf16)
        last_max = sb("last_max", [P, 2, 1])
        neg_max = sb("neg_max", [P, 2, 1])
        vaug = sb("vaug", [P, NQ, H, W])
        yT = sb("yT", [P, 2, T])
        den = sb("den", [P, T])
        inv_den = sb("inv_den", [P, T])
        hT = sb("hT", [P, T])
        xt = sb("xt", [P, NQ, C])
        xr = sb("xr", [P, NQ, C])
        x1 = sb("x1", [P, NQ, C])
        h2T = sb("h2T", [P, T])
        qk32 = sb("qk32", [P, 2, T])
        rest = sb("rest", [P, T])
        parts = sb("parts", [P, 2, 3, T], bf16)
        stats = sb("stats", [P, NQ, 6])
        mv = sb("mv", [P, NQ, 2])
        var_eps = sb("var_eps", [P, NQ])
        rstd = sb("rstd", [P, NQ])
        stats2 = sb("stats2", [P, NQ, 6])
        mv2 = sb("mv2", [P, NQ, 2])
        var_eps2 = sb("var_eps2", [P, NQ])
        rstd2 = sb("rstd2", [P, NQ])
        modbc = sb("modbc", [P, 4, C])
        absg = sb("absg", [P, 2, C])
        sgn = sb("sgn", [P, 2, C])
        silu_col = sb("silu_col", [P, P])
        gb_all = sb("gb_all", [P, B, C])
        logits = sb("logits", [P, TOK, E])
        at = 0

        def setup_view(cols):
            nonlocal at
            at += cols
            return probs[:, at - cols:at]

        YW = 2 * T - 4
        hidden = setup_view(2 * 2 * CAUSAL).rearrange("p (s n) -> p s n", s=2)
        third_stage = setup_view(CAUSAL)
        dist = setup_view(YW)
        dist_i = setup_view(YW).bitcast(i32)
        pos_i = setup_view(P).bitcast(i32)
        pnorm = setup_view(P)
        slope = setup_view(P)
        w2_bd = setup_view(4 * H)
        w2_rep = setup_view(H)
        fire = setup_view(8)
        c_col, L_col, w1_col, b1_col, b2_col, threshold, b12_col, neg_b1 = (fire[:, k:k + 1] for k in range(8))
        r_col = setup_view(1)
        wmod_cols = setup_view(2 * C)
        condT = setup_view(B)
        sig = setup_view(B)
        Wqk_raw = setup_view(2 * C)
        at2 = 0

        def ffn_view(cols):
            nonlocal at2
            at2 += cols
            return bias[:, at2 - cols:at2]

        w_up_all = ffn_view((E + 1) * 2 * F).rearrange("p (e n) -> p e n", e=E + 1)
        w_dn_all = ffn_view((E + 1) * 2 * C).rearrange("p (e n) -> p e n", e=E + 1)
        rows_all = ffn_view(TOK * ROW).rearrange("p (t c) -> p t c", t=TOK)
        row_in = ffn_view(DEEP * ROW).rearrange("p (k c) -> p k c", k=DEEP)
        rowT = ffn_view(2 * P).rearrange("p (k c) -> p k c", k=2)
        gated = ffn_view(2 * F).rearrange("p (k c) -> p k c", k=2)
        act_h = ffn_view(2 * F).rearrange("p (k c) -> p k c", k=2)
        act_hT = ffn_view(2 * F).rearrange("p (k c) -> p k c", k=2)
        row_out = ffn_view(DEEP * C).rearrange("p (k c) -> p k c", k=DEEP)
        at = 0
        x1_all = setup_view(TOK * C).rearrange("p (t c) -> p t c", t=TOK)
        routed = setup_view(TOK * C).rearrange("p (t c) -> p t c", t=TOK)
        top = setup_view(TOK)
        top_e = setup_view(TOK)
        score = setup_view(TOK)
        raw_up, raw_down = xt, rest[:, 0:2 * P].rearrange("p (k c) -> p k c", k=2)
        wide = yT[:, 0, :].rearrange("p (t e) -> p t e", e=E)
        wide2 = yT[:, 1, :].rearrange("p (t e) -> p t e", e=E)
        sq = h2T[:, 0:E * E].rearrange("p (a b) -> p a b", b=E)
        wide3 = den[:, :].rearrange("p (e k) -> p e k", e=E)
        token = sb("token", [P, 8], i32)
        iota_e = sb("iota_e", [P, E])
        iota_e1 = sb("iota_e1", [P, E])
        iota_k = sb("iota_k", [P, TOK])
        iota_t = sb("iota_t", [P, SORTED])
        iota_i = sb("iota_i", [P, SORTED], i32)
        one_hot = sb("one_hot", [P, TOK, E], bf16)
        before = sb("before", [P, P], bf16)
        lower = sb("lower", [P, E, E])
        tiles_of = sb("tiles_of", [P, E])
        first_tile = sb("first_tile", [P, E])
        base_row = sb("base_row", [P, E])
        end_tile = sb("end_tile", [P, E])
        dest_f = sb("dest_f", [P, TOK])
        dest = sb("dest", [P, TOK], i32)
        expert_f = sb("expert_f", [P, SLOTS])
        expert = sb("expert", [P, SLOTS], i32)
        cmp_t = xt[:, :, :].rearrange("p a b -> p (a b)")
        cmp_t2 = xr[:, :, :].rearrange("p a b -> p (a b)")

        def bank(name):
            return ctx.enter_context(nc.psum_tensor(name, [P, T], f32))

        score_bank = [bank(f"score_bank{k}") for k in range(3)]
        turned_bank = [bank(f"turned_bank{k}") for k in range(3)]
        y_bank = bank("y_bank")
        misc = bank("misc")

        fire_banks = [turned_bank, score_bank]

        BIAS_BANKS = [(0, OFF[2]), (OFF[2], 3 * P), (OFF[3], 4 * P)]

        def bias_bank(i):
            return (0, OFF[i]) if i < 2 else (i - 1, 0)

        def stage_of(j, c0=0, n=CAUSAL):
            return (third_stage if j % 3 == 2 else biased[:, j % 3, :])[:, c0:c0 + n]

        def hidden_of(j, i, a):
            c0 = 2 * OFF[i] + a * P * (i + 1)
            return hidden[:, j % 2, c0:c0 + P * (i + 1)]

        def dist_of(n, i):
            return dist[:, T - 4 - 4 * n:T - 4 - 4 * n + P * (i + 1)]

        fire_loaded = sem("fire_loaded")
        first_params_loaded = sem("first_params_loaded")
        params_loaded = sem("params_loaded")
        consts_made = sem("consts_made")
        pool_step = sem("pool_step")
        dve_step = sem("dve_step")
        dist_made = sem("dist_made")
        logs_taken = sem("logs_taken")
        slopes_made = sem("slopes_made")
        hidden_by_dve = sem("hidden_by_dve")
        hidden_by_act = sem("hidden_by_act")
        hidden_used = sem("hidden_used")
        stage_by_dve = sem("stage_by_dve")
        stage_by_act = sem("stage_by_act")
        stage_ready = sem("stage_ready")
        stage_sent = [sem(f"stage_sent{r}") for r in range(3)]
        w2_made = sem("w2_made")
        b1_products = sem("b1_products")
        cond_loaded = sem("cond_loaded")
        cond_exp = sem("cond_exp")
        silu_made = sem("silu_made")
        modT_ready = sem("modT_ready")
        modT_copied = sem("modT_copied")

        xt_loaded = sem("xt_loaded")
        xr_loaded = sem("xr_loaded")
        var_ready = sem("var_ready")
        rstd_ready = sem("rstd_ready")
        xn_ready = sem("xn_ready")
        var2_ready = sem("var2_ready")
        rstd2_ready = sem("rstd2_ready")
        parts_step = sem("parts_step")
        feat_ready = [[sem(f"{m}_feat_ready{s}") for m in "qk"] for s in range(2)]
        scores_ready = sem("scores_ready")
        scores_free = sem("scores_free")
        max_ready = sem("max_ready")
        shifted = sem("shifted")
        turned_ready = sem("turned_ready")
        turned_free = sem("turned_free")
        av_done = sem("av_done")
        y_copied = sem("y_copied")
        inverse_ready = sem("inverse_ready")
        newton_step = sem("newton_step")
        y_divided = sem("y_divided")
        misc_ready = sem("misc_ready")
        misc_used = sem("misc_used")
        waits_passed = sem("waits_passed")
        prep_step = sem("prep_step")
        norm_step = sem("norm_step")
        silu_col_made = sem("silu_col_made")
        x1_ready = sem("x1_ready")
        h2_ready = sem("h2_ready")
        x1_stored = sem("x1_stored")
        h2_stored = sem("h2_stored")
        rows_zeroed = sem("rows_zeroed")

        w_loaded = sem("w_loaded")
        shared_loaded = sem("shared_loaded")
        shared_T = sem("shared_T")
        rows_loaded = sem("rows_loaded")
        one_hot_made = sem("one_hot_made")
        ranks_ready = sem("ranks_ready")
        score_exp = sem("score_exp")
        top_ready = sem("top_ready")
        dest_ready = sem("dest_ready")
        expert_ready = sem("expert_ready")
        numbers_made = sem("numbers_made")
        masked_ready = sem("masked_ready")
        scattered = sem("scattered")
        row_loaded = [sem(f"row_loaded{k}") for k in range(DEEP)]
        rowT_ready = sem("rowT_ready")
        rowT_copied = sem("rowT_copied")
        up_ready = sem("up_ready")
        gate_done = sem("gate_done")
        act_ready = sem("act_ready")
        actT_ready = sem("actT_ready")
        actT_copied = sem("actT_copied")
        down_ready = sem("down_ready")
        shared_added = sem("shared_added")
        out_copied = sem("out_copied")
        row_sent = [sem(f"row_sent{k}") for k in range(8)]
        scatters_issued = sem("scatters_issued")
        x1_loaded = sem("x1_loaded")
        routed_loaded = [sem(f"routed_loaded{b}") for b in range(B)]
        final_by_dve = sem("final_by_dve")
        final_by_pool = sem("final_by_pool")
        out_stored = sem("out_stored")

        block = ctx.enter_context(nc.Block())

        def finish(eng, ops, rows, step):
            eng.wait_ge(shared_added, TOK)
            for n, b in enumerate(rows):
                r = slice(b * NQ, b * NQ + NQ)
                eng.wait_ge(routed_loaded[b], 16)
                ops.tensor_tensor(routed[:, r, :], routed[:, r, :], gb_all[:, b:b + 1, :].to_broadcast([P, NQ, C]),
                                  ALU.mult).then_inc(step, 1)
                eng.wait_ge(step, n * 2 + 1)
                ops.tensor_tensor(x1_all[:, r, :], x1_all[:, r, :], routed[:, r, :], ALU.add).then_inc(step, 1)

        @block.sync
        def _(sp):
            for col, src in ((c_col, c_param_d.partition_broadcast(P)), (L_col, L_mult_d.partition_broadcast(P)),
                             (w1_col, w1_d.to_broadcast([4, W]).unsqueeze(2)),
                             (b1_col, b1_d.unsqueeze(0).to_broadcast([4, W]).unsqueeze(2)),
                             (b2_col, b2_d.unsqueeze(0).to_broadcast([P // H, H]).unsqueeze(2)),
                             (w2_rep, w2_d.unsqueeze(0).to_broadcast([4, W, H]))):
                sp.dma_start(col, src).then_inc(fire_loaded, 16)
            sp.dma_start(condT, cond_d.rearrange("b k -> k b")).then_inc(cond_loaded, 16)
            sp.dma_start(xt[:, :, :], x_d[0, :, :].rearrange("(i p) c -> p i c", p=P)).then_inc(xt_loaded, 16)
            sp.dma_start(wmod_cols, wmod_d[:, 0:2 * C]).then_inc(first_params_loaded, 16)
            sp.dma_start(Wqk_raw, Wqkv_d[:, 0:2 * C]).then_inc(first_params_loaded, 16)
            for m in range(2):
                for g in range(4):
                    part = bqkv_d[m * C + W * g:m * C + W * g + W].rearrange("(h d a) -> d h a", h=4, a=1)
                    sp.dma_start(bq[W * g:W * g + W, m:m + 1], part).then_inc(first_params_loaded, 16)
            for r in range(2):
                half = slice(r * C // 2, r * C // 2 + C // 2)
                sp.dma_start(Wv[:, half], Wqkv_d[:, 2 * C:3 * C].rearrange("k (g r n) -> k r g n", g=2, r=2)[:, r])\
                  .then_inc(params_loaded, 16)
                sp.dma_start(bv_bc[:, half].rearrange("p (g n) -> p g n", g=2),
                             bqkv_d[2 * C:3 * C].rearrange("(g r n) -> r g n", g=2, r=2)[r].partition_broadcast(P))\
                  .then_inc(params_loaded, 16)
            sp.dma_start(wmod_bc[:, :], wmod_d[:, 2 * C:6 * C]).then_inc(params_loaded, 16)
            sp.dma_start(bproj_bc[:, :], bproj_d.partition_broadcast(P)).then_inc(params_loaded, 16)
            sp.dma_start(routerT[:, :], w_router_d.rearrange("e k -> k e")).then_inc(params_loaded, 16)
            sp.wait_ge(consts_made, 3)
            for hh in range(4):
                for r in range(2):
                    row = W * hh + 2 * HD * r
                    sp.dma_start(Wproj[row:row + HD, :, :],
                                 Wproj_d.rearrange("(g r h d) n -> d g r h n", r=2, h=4, d=HD)[:, :, r, hh, :])\
                      .then_inc(params_loaded, 16)

            def features(b, g, mats=(0, 1)):
                s = g % 2
                for mat in mats:
                    terms, dst = ((TERMS_Q, qf), (TERMS_K, kf))[mat]
                    for t, part in enumerate(terms):
                        sp.dma_start(dst[HD * t:HD * t + HD, s, :, :], parts[W * g:W * g + W, mat, part, :])\
                          .then_inc(feat_ready[s][mat], 16)

            def batch(b, post, prep):
                if prep:
                    sp.dma_start(xt[:, :, :], x_d[ds(b + 1, 1), :, :].rearrange("b (i p) c -> p (b i) c", p=P))\
                      .then_inc(xt_loaded, 16)
                if post:
                    load_residual(b - 1)
                for g in (2, 3):
                    sp.wait_ge(scores_ready, (b * 16 + 4 * g - 4) * 3)
                    features(b, g)
                if post:
                    store_x1(b - 1)
                if prep:
                    sp.wait_ge(scores_ready, (b * 16 + 12) * 3)
                    for mat in range(2):
                        sp.wait_ge(parts_step, (b + 1) * 8 + 4 * mat + 4)
                        features(b + 1, 0, (mat,))
                if post:
                    store_h2(b - 1)
                if prep:
                    sp.wait_ge(scores_ready, (b * 16 + 16) * 3)
                    features(b + 1, 1)

            def load_residual(b):
                sp.dma_start(xr[:, :, :], x_d[ds(b, 1), :, :].rearrange("b (i p) c -> p (b i) c", p=P))\
                  .then_inc(xr_loaded, 16)

            def store_x1(b):
                sp.wait_ge(x1_ready, b + 1)
                sp.dma_start(x1_d[ds(b * T, T), :].rearrange("(i p) c -> p i c", p=P), x1[:, :, :])\
                  .then_inc(x1_stored, 16)

            def store_h2(b):
                sp.wait_ge(h2_ready, b + 1)
                sp.dma_start(rows_d[ds(b * T, T), :].rearrange("(i p) c -> p i c", p=P), xr[:, :, :])\
                  .then_inc(h2_stored, 16)
                sp.wait_ge(h2_stored, (b + 1) * 16)

            for j in range(OCTETS):
                sp.wait_ge(stage_ready, j + 1)
                sp.dma_start(bias_v[8 * j:8 * j + 8, :, :], stage_of(j)).then_inc(stage_sent[j % 3], 16)
                if j in (9, 11):
                    sp.wait_ge(parts_step, 4)
                    features(0, (j - 9) // 2, (0,))
                if j in (13, 15):
                    sp.wait_ge(parts_step, 8)
                    features(0, (j - 13) // 2, (1,))
            sp.wait_ge(misc_ready, 1)
            batch(0, False, True)
            with sp.Fori(1, B - 1) as b:
                sp.wait_ge(misc_ready, first_job(b))
                batch(b, True, True)
            def load_shared(t, k):
                sp.dma_start(row_in[:, k, 0:C], rows_d[ds(t * P, P), :]).then_inc(row_loaded[k], 16)

            def load_sorted(t, k):
                sp.dma_start(row_in[:, k, :], sorted_d[ds((t - TOK) * P, P), :]).then_inc(row_loaded[k], 16)

            def load_expert(e):
                sp.dma_start(w_up_all[:, e, :], gate_up_d[e, :, :]).then_inc(w_loaded, 16)
                sp.dma_start(w_dn_all[:, e, :].rearrange("p (a n) -> p a n", a=2),
                             down_d[e, :, :].rearrange("(a p) n -> p a n", p=P)).then_inc(w_loaded, 16)

            sp.wait_ge(misc_ready, first_job(B - 1))
            for k, src in enumerate((w_gate_d[0:P, :], w_gate_d[P:F, :], w_up_d[0:P, :], w_up_d[P:F, :])):
                sp.dma_start(raw_up[:, k, :], src).then_inc(shared_loaded, 16)
            sp.dma_start(raw_down, w_down_d.rearrange("c (k n) -> c k n", k=2)).then_inc(shared_loaded, 16)
            batch(B - 1, True, False)
            sp.wait_ge(misc_ready, EPILOGUE)
            load_residual(B - 1)
            early = slice(0, TOK - NQ)
            late = slice(TOK - NQ, TOK)
            rows_v = rows_d.rearrange("(t p) c -> p t c", p=P)
            x1_v = x1_d.rearrange("(t p) c -> p t c", p=P)
            sp.wait_ge(av_done, 4 * B - 1 + 2)
            sp.dma_start(x1_all[:, early, :], x1_v[:, early, :]).then_inc(x1_loaded, 16)
            sp.wait_ge(scores_free, 3 + 3 * 16 * B)
            for k in range(DEEP):
                load_shared(k, k)
            sp.dma_start(rows_all[:, early, 0:C], rows_v[:, early, :]).then_inc(rows_loaded, 16)
            store_x1(B - 1)
            store_h2(B - 1)
            sp.dma_start(rows_all[:, late, 0:C], rows_v[:, late, :]).then_inc(rows_loaded, 16)
            sp.wait_ge(x1_stored, 16 * B)
            sp.dma_start(x1_all[:, late, :], x1_v[:, late, :]).then_inc(x1_loaded, 16)
            for n in range(1, TOK // DEEP):
                for k in range(DEEP):
                    sp.wait_ge(rowT_copied, (n - 1) * DEEP + k + 1)
                    load_shared(n * DEEP + k, k)
                for e in range(3 * (n - 1), min(3 * n, E)):
                    load_expert(e)
            sp.wait_ge(scattered, 16 * TOK)
            with sp.Fori(TOK // DEEP, SLOTS // DEEP) as n:
                for k in range(DEEP):
                    sp.wait_ge(rowT_copied, (n - 1) * DEEP + k + 1)
                    load_sorted(n * DEEP + k, k)
            for k in range(8):
                sp.wait_ge(row_sent[k], 16 * (SORTED // 8))
            for b in range(B):
                sp.dma_start(routed[:, b * NQ:b * NQ + NQ, :],
                             routed_d[b * T:b * T + T, :].rearrange("(i p) c -> p i c", p=P))\
                  .then_inc(routed_loaded[b], 16)
            for b in range(B):
                if b in BY_POOL:
                    sp.wait_ge(final_by_pool, 2 * BY_POOL.index(b) + 2)
                else:
                    sp.wait_ge(final_by_dve, 2 * (b - sum(x < b for x in BY_POOL)) + 2)
                sp.dma_start(out_d[b, :, :].rearrange("(i p) c -> p i c", p=P),
                             x1_all[:, b * NQ:b * NQ + NQ, :]).then_inc(out_stored, 16)
            sp.wait_ge(out_stored, 16 * B)
            sp.wait_ge(x1_stored, 16 * B)
            sp.wait_ge(rows_zeroed, 16)

        @block.gpsimd
        def _(pool):
            step = [0]

            def chain(ins):
                step[0] += 1
                ins.then_inc(pool_step, 1)
                pool.wait_ge(pool_step, step[0])

            pool.sem_inc(y_divided, 1)
            for r in range(4):
                last = pool.memset(r_col[W * r:W * r + W, :], float(r))
            chain(last)
            pool.iota(dist_i, pattern=[[-1, YW]], base=T - 4, channel_multiplier=0)
            pool.iota(pos_i, pattern=[[4, P]], base=0, channel_multiplier=0).then_inc(consts_made, 1)
            pool.wait_ge(consts_made, 1)
            pool.memset(w2_bd, 0.0).then_inc(consts_made, 1)
            pool.wait_ge(consts_made, 2)
            chain(pool.memset(ident[:, :], 0.0))
            chain(pool.memset(neg_ident[:, :], 0.0))
            chain(pool.memset(pick_den[:, :], 0.0))
            chain(pool.memset(Wproj[:, :, :], 0.0))
            chain(pool.memset(before[:, :], 1.0))
            chain(pool.memset(lower[:, :, :], 1.0))
            pool.memset(ones_bf[:, :], 1.0)
            pool.memset(empty_row[:, 0:C], 0.0)
            pool.memset(empty_row[:, C:ROW].bitcast(i32), NOBODY)
            pool.memset(neg_half[:, :], -0.5)
            pool.memset(two[:, :], 2.0)
            chain(pool.memset(vaug[:, :, :, :], 0.0))
            for r in range(2):
                c1 = 2 * HD * r + HD
                pool.memset(vaug[:, :, H // 2 * r:H // 2 * r + H // 2, c1:c1 + HD], 1.0)
            pool.affine_select(out=ident[:, :], in_=ident[:, :], compare_op=ALU.not_equal, fill=1.0, base=0,
                               pattern=[[-1, P]], channel_multiplier=1)
            pool.affine_select(out=neg_ident[:, :], in_=neg_ident[:, :], compare_op=ALU.not_equal, fill=-1.0,
                               base=0, pattern=[[-1, P]], channel_multiplier=1)
            pick_v = pick_den[:, :].rearrange("p (a c) -> p a c", a=8)
            pool.affine_select(out=pick_v, in_=pick_v, compare_op=ALU.not_equal, fill=1.0, base=-HD,
                               pattern=[[-2 * HD, 8], [0, 2 * HD]], channel_multiplier=1)
            pool.affine_select(out=before[:, :], in_=before[:, :], compare_op=ALU.is_gt, fill=0.0, base=0,
                               pattern=[[1, P]], channel_multiplier=-1)
            pool.affine_select(out=lower[:, :, :], in_=lower[:, :, :], compare_op=ALU.is_gt, fill=0.0, base=0,
                               pattern=[[1, E], [-1, E]], channel_multiplier=0)
            chain(pool.iota(iota_i[:, :], pattern=[[1, SORTED]], base=0, channel_multiplier=0))
            pool.tensor_copy(iota_t[:, :], iota_i[:, :])
            pool.tensor_copy(iota_e[:, :], iota_i[:, 0:E])
            chain(pool.tensor_copy(iota_k[:, :], iota_i[:, 0:TOK]))
            pool.tensor_scalar(iota_k[:, :], iota_k[:, :], float(P), 0.0, ALU.mult, ALU.add)
            pool.memset(expert_f[:, 0:TOK], float(E)).then_inc(consts_made, 1)
            pool.wait_ge(consts_made, 3)
            zero_row = empty_row[:, 0:1].to_broadcast([P, T])

            def split_step(b, job, n):
                mat, k, n0 = n // 4, n % 4, b * 8 + n
                x32 = qk32[:, mat, :]
                if k == 0:
                    pool.wait_ge(misc_used, job + mat + 1)
                    if not (isinstance(b, int) and b == 0):
                        for s in range(2):
                            pool.wait_ge(feat_ready[s][mat], b * 2 * FEAT)
                dst, x, y, op = ((parts[:, mat, 0, :], x32, zero_row, ALU.add),
                                 (rest[:, :], x32, parts[:, mat, 0, :], ALU.subtract),
                                 (parts[:, mat, 1, :], rest[:, :], zero_row, ALU.add),
                                 (parts[:, mat, 2, :], rest[:, :], parts[:, mat, 1, :], ALU.subtract))[k]
                pool.tensor_tensor(dst, x, y, op).then_inc(parts_step, 1)
                pool.wait_ge(parts_step, n0 + 1)

            def divide(b, pair):
                n0 = b * 4 + pair * 2
                pool.wait_ge(inverse_ready, b * 2 + pair + 1)
                pool.tensor_tensor(yT[:, pair, :], yT[:, pair, :], inv_den[:, :], ALU.mult)
                pool.tensor_tensor(den[:, :], den[:, :], inv_den[:, :], ALU.mult).then_inc(newton_step, 1)
                pool.wait_ge(newton_step, n0 + 1)
                pool.tensor_tensor(den[:, :], two[:, 0:1].to_broadcast([P, T]), den[:, :], ALU.subtract)\
                    .then_inc(newton_step, 1)
                pool.wait_ge(newton_step, n0 + 2)
                pool.tensor_tensor(yT[:, pair, :], yT[:, pair, :], den[:, :], ALU.mult).then_inc(y_divided, 1)

            def power(b, var, out, ready, done):
                pool.wait_ge(ready, b + 1)
                pool.tensor_tensor(out[:, :], var[:, :], neg_half[:, :], ALU.pow).then_inc(done, 1)

            for j in range(OCTETS):
                pool.wait_ge(stage_by_dve, j + 1)
                if j % 2:
                    pool.wait_ge(stage_by_act, j // 2 + 1)
                for i in range(NQ):
                    d = stage_of(j, OFF[i] + P * i, P)
                    last = pool.affine_select(out=d, in_=d, compare_op=ALU.is_ge, fill=MASKED, base=H * 8 * j,
                                              pattern=[[-H, P]], channel_multiplier=1)
                last.then_inc(stage_ready, 1)
                if j == 0:
                    power(0, var_eps, rstd, var_ready, rstd_ready)
                if 5 <= j < 13:
                    split_step(0, 1, j - 5)
            def batch(b, post, prep):
                job = {j: first_job(b) + n for n, j in enumerate(jobs(post, prep))}
                if prep:
                    power(b + 1, var_eps, rstd, var_ready, rstd_ready)
                if post:
                    divide(b - 1, 1)
                for n in range(8):
                    if n == 2 and post:
                        power(b - 1, var_eps2, rstd2, var2_ready, rstd2_ready)
                    if prep:
                        split_step(b + 1, job["q" if n < 4 else "k"] - n // 4, n)
                divide(b, 0)

            batch(0, False, True)
            pool.dma_start(sorted_d.rearrange("(t p) c -> p t c", p=P),
                           empty_row[:, :].unsqueeze(1).to_broadcast([P, SORTED, ROW])).then_inc(rows_zeroed, 16)

            with pool.Fori(1, B - 1) as b:
                batch(b, True, True)
            batch(B - 1, True, False)
            power(B - 1, var_eps2, rstd2, var2_ready, rstd2_ready)
            pool.wait_ge(rows_loaded, 32)
            pool.iota(rows_all[:, :, C:ROW].bitcast(i32).rearrange("p t a -> p (t a)"), pattern=[[P, TOK]], base=0,
                      channel_multiplier=1).then_inc(numbers_made, 1)
            pool.wait_ge(numbers_made, 1)
            pool.wait_ge(dest_ready, 1)
            pool.wait_ge(rows_zeroed, 16)
            for t in range(TOK):
                if t % NQ == 0:
                    pool.wait_ge(masked_ready, t // NQ + 1)
                pool.indirect_dma_start(sorted_d, bass.IndirectOffsetOnAxis(ap=dest[:, t:t + 1], axis=0),
                                        rows_all[:, t, :], None).then_inc(scattered, 16)
            with pool.Fori(0, SORTED // 8) as m:
                for k in range(8):
                    pool.wait_ge(out_copied, m * 8 + TOK + k + 1)
                    pool.sem_inc(scatters_issued)
                    pool.indirect_dma_start(routed_d, bass.IndirectOffsetOnAxis(ap=token[:, k:k + 1], axis=0),
                                            row_out[:, k % DEEP, :], None, bounds_check=B * T - 1,
                                            oob_is_err=False).then_inc(row_sent[k], 16)
            finish(pool, pool, BY_POOL, final_by_pool)

        @block.scalar
        def _(act):
            act.wait_ge(dist_made, 2)
            act.activation(dist, dist, ACT.Ln, bias=1.0).then_inc(logs_taken, 1)
            act.activation(pnorm, pnorm, ACT.Ln, bias=1.0).then_inc(logs_taken, 1)
            act.preload_act_table_set("natural_log_exp_and_others")
            act.wait_ge(cond_loaded, 16)
            act.activation(sig, condT, ACT.Exp, scale=-1.0).then_inc(cond_exp, 1)

            def exps(b, h):
                u = b * 16 + h
                if h % 4 == 0:
                    act.wait_ge(av_done, b * 4 + h // 4 + 1)
                for k in range(3):
                    act.wait_ge(turned_ready, u * 3 + 6 + k + 1)
                    c0, n = (h % 8) * CAUSAL + 4 * P * k, BANK_COLS[k]
                    act.activation(probs[:, c0:c0 + n], turned_bank[k][:, 0:n], ACT.Exp).then_inc(turned_free, 1)

            def shift(b, h):
                u, s = b * 16 + h, h % 2
                act.wait_ge(max_ready, u + 1)
                last = biased[:, s, OFF[NQ - 1]:CAUSAL]
                act.activation(last, last, ACT.Identity, bias=neg_max[:, s, :]).then_inc(shifted, 1)

            def y_copy(b, pair):
                act.wait_ge(av_done, b * 4 + 2 * pair + 2 + 2)
                act.activation(yT[:, pair, :], y_bank[:, :], ACT.Copy).then_inc(y_copied, 1)

            def modulate(b, job):
                act.wait_ge(misc_ready, job + 1)
                act.activation(hT[:, :], misc[:, :], ACT.Identity, bias=modT[:, ds(b, 1), 0],
                               scale=modT[:, ds(b, 1), 1]).then_inc(misc_used, 1)

            def take_qk(mat, job):
                act.wait_ge(misc_ready, job + 1)
                act.activation(qk32[:, mat, :], misc[:, :], ACT.Identity, bias=bq[:, mat:mat + 1],
                               scale=float(HD) ** -0.5 if mat == 0 else 1.0).then_inc(misc_used, 1)

            def take_den(b, pair, job):
                act.wait_ge(misc_ready, job + 1)
                act.wait_ge(y_divided, b * 2 + pair + 1)
                act.activation(den[:, :], misc[:, :], ACT.Copy)
                act.activation(inv_den[:, :], misc[:, :], ACT.Ln).then_inc(misc_used, 1)
                act.wait_ge(misc_used, job + 1)
                act.activation(inv_den[:, :], inv_den[:, :], ACT.Exp, scale=-1.0).then_inc(inverse_ready, 1)

            def take_mod(b, job):
                act.wait_ge(misc_ready, job + 1)
                act.activation(modbc[:, :, :], misc[:, :].rearrange("p (m c) -> p m c", m=4), ACT.Copy)\
                   .then_inc(misc_used, 1)

            def take_logits(b, job):
                act.wait_ge(misc_ready, job + 1)
                act.activation(logits[:, ds(b * NQ, NQ), :],
                               misc[:, 0:NQ * E].rearrange("p (i e) -> p i e", i=NQ), ACT.Copy)\
                   .then_inc(misc_used, 1)

            def copy_h2T(job):
                act.wait_ge(misc_ready, job + 1)
                act.activation(h2T[:, :], misc[:, :], ACT.Copy).then_inc(misc_used, 1)

            def batch(b, post, prep):
                job = {j: first_job(b) + n for n, j in enumerate(jobs(post, prep))}
                for h in range(H):
                    exps(b, h)
                    if h < H - 1:
                        shift(b, h + 1)
                    elif prep:
                        shift(b + 1, 0)
                    if h == 0 and post:
                        y_copy(b - 1, 1)
                    if h == 8:
                        if post:
                            act.wait_ge(misc_ready, job["proj"] + 1)
                        y_copy(b, 0)
                    if h == 1 and post:
                        take_den(b - 1, 1, job["den1"])
                    if h == 3 and post:
                        take_mod(b - 1, job["mod"])
                    if h == 10:
                        take_den(b, 0, job["den0"])
                    if h == 5 and prep:
                        modulate(b + 1, job["xT"])
                    if h == 7 and prep:
                        take_qk(0, job["q"])
                    if h == 9 and prep:
                        take_qk(1, job["k"])
                    if h == 13 and post:
                        copy_h2T(job["h2T"])
                    if h == 14 and post:
                        take_logits(b - 1, job["logits"])

            act.wait_ge(slopes_made, 1)
            def hidden_tiles_2_3(j):
                for i in (2, 3):
                    if j >= 2:
                        act.wait_ge(hidden_used, 4 * (j - 2) + i + 1)
                    for a in range(2):
                        n = P // 4 * i + 2 * j + a
                        last = act.activation(hidden_of(j, i, a), dist_of(n, i), ACT.Relu, bias=b1_col,
                                              scale=slope[:, n:n + 1])
                    last.then_inc(hidden_by_act, 1)

            hidden_tiles_2_3(0)
            for j in range(OCTETS):
                if j + 1 < OCTETS:
                    hidden_tiles_2_3(j + 1)
                if j % 2:
                    if j >= 3:
                        act.wait_ge(stage_sent[j % 3], 16 * (j // 3))
                    act.wait_ge(hidden_used, 4 * j + 4)
                    c0, n = BIAS_BANKS[2]
                    act.activation(stage_of(j, c0, n), fire_banks[1][2][:, 0:n], ACT.Identity, bias=b2_col)\
                       .then_inc(stage_by_act, 1)
                if j == 2:
                    act.wait_ge(modT_copied, 1)
                    modulate(0, 0)
                if j in (3, 4):
                    take_qk(j - 3, j - 2)
            act.wait_ge(hidden_used, 4 * OCTETS)
            shift(0, 0)
            batch(0, False, True)
            with act.Fori(1, B - 1) as b:
                batch(b, True, True)
            batch(B - 1, True, False)
            y_copy(B - 1, 1)
            take_mod(B - 1, EPILOGUE + 1)
            copy_h2T(EPILOGUE + 3)
            take_logits(B - 1, EPILOGUE + 4)
            act.wait_ge(top_ready, 1)
            act.activation(score, top, ACT.Exp, scale=-1.0).then_inc(score_exp, 1)

            def gate(t, k):
                act.wait_ge(up_ready, t + 1)
                act.activation(gated[:, k % 2, :], turned_bank[k % 2][:, 0:F], ACT.Silu).then_inc(gate_done, 1)

            def copy_actT(t, k):
                act.wait_ge(actT_ready, t + 1)
                act.activation(act_hT[:, k % 2, :], score_bank[2][:, 0:F], ACT.Copy)\
                   .then_inc(actT_copied, 1)

            gate(0, 0)
            gate(1, 1)
            copy_actT(0, 0)
            with act.Fori(0, SLOTS // 2 - 1) as n:
                for k in range(2):
                    gate(n * 2 + k + 2, k)
                    copy_actT(n * 2 + k + 1, k + 1)
            copy_actT(SLOTS - 1, 1)

        @block.vector
        def _(dve):
            step = [0]

            def chain(ins):
                step[0] += 1
                ins.then_inc(dve_step, 1)
                dve.wait_ge(dve_step, step[0])

            V = nc.vector

            def carry_wait():
                dve.sem_inc(waits_passed)

            dve.wait_ge(fire_loaded, 16 * 6)
            dve.wait_ge(consts_made, 1)

            def absolute(x):
                return V.scalar_tensor_tensor(x, x, -1.0, x, ALU.mult, ALU.max)

            chain(V.tensor_scalar(threshold, L_col, float(T), None, ALU.mult))
            chain(V.tensor_scalar(dist, dist_i, r_col, c_col, ALU.add, ALU.mult))
            chain(absolute(threshold))
            chain(V.tensor_scalar(pnorm, pos_i, r_col, threshold, ALU.add, ALU.max))
            chain(V.tensor_scalar(pnorm, pnorm, c_col, None, ALU.mult))
            absolute(dist)
            absolute(pnorm).then_inc(dist_made, 2)
            dve.wait_ge(consts_made, 2)
            V.tensor_scalar(neg_b1, b1_col, -1.0, None, ALU.mult)
            for r in range(4):
                last = V.tensor_copy(w2_bd[W * r:W * r + W, H * r:H * r + H], w2_rep[W * r:W * r + W, :])
            last.then_inc(w2_made, 1)
            dve.wait_ge(logs_taken, 2)
            chain(V.tensor_scalar(pnorm, pnorm, 1e-6, None, ALU.add))
            chain(V.reciprocal(slope, pnorm))
            V.tensor_scalar(slope, slope, w1_col, None, ALU.mult).then_inc(slopes_made, 1)
            dve.wait_ge(b1_products, 1)
            V.tensor_tensor(b12_col, y_bank[:, 0:1], b2_col, ALU.add)
            dve.wait_ge(slopes_made, 1)

            def make_silu():
                dve.wait_ge(cond_exp, 1)
                chain(V.tensor_scalar(sig, sig, 1.0, None, ALU.add))
                chain(V.reciprocal(sig, sig))
                V.tensor_tensor(siluT[:, :], condT, sig, ALU.mult).then_inc(silu_made, 1)

            def arrange_parameters():
                dve.wait_ge(first_params_loaded, 16 * 10)
                for m in range(2):
                    V.tensor_copy(Wqk[:, m, :].rearrange("p (g d h) -> p g d h", g=4, d=HD),
                                  Wqk_raw[:, m * C:m * C + C].rearrange("p (g h d) -> p g d h", g=4, d=HD))
                V.tensor_scalar(bq[:, 0:1], bq[:, 0:1], float(HD) ** -0.5, None, ALU.mult)
                dve.wait_ge(modT_ready, 1)
                V.tensor_copy(modT[:, :, 0], misc[:, 0:B])
                V.tensor_scalar(modT[:, :, 1], misc[:, B:2 * B], 1.0, None, ALU.add).then_inc(modT_copied, 1)
                V.memset(y_bank[:, :], 0.0)

            def norm_stats(src, st, m, ve, ready, steps, base):
                for i in range(NQ):
                    last = V.bn_stats(st[:, i, :], src[:, i, :])
                last.then_inc(steps, 1)
                dve.wait_ge(steps, base + 1)
                carry_wait()
                for i in range(NQ):
                    last = V.bn_aggr(m[:, i, :], st[:, i, :])
                last.then_inc(steps, 1)
                dve.wait_ge(steps, base + 2)
                V.tensor_scalar(ve[:, :], m[:, :, 1], 1e-5, None, ALU.add).then_inc(ready, 1)

            def normalize(b, dst, src, m, r, rstd_sem):
                dve.wait_ge(rstd_sem, b + 1)
                for i in range(NQ):
                    last = V.tensor_scalar(dst[:, i, :], src[:, i, :], m[:, i, 0:1], r[:, i:i + 1],
                                           ALU.subtract, ALU.mult)
                return last

            GATE_STEPS, RESIDUAL_STEPS, NORM2_STEPS = 4, 3, 2

            def post_base(b):
                return b * (GATE_STEPS + RESIDUAL_STEPS + NORM2_STEPS)

            def norm1_stats(b):
                dve.wait_ge(xt_loaded, (b + 1) * 16)
                norm_stats(xt, stats, mv, var_eps, var_ready, prep_step, b * 2)

            def norm1_apply(b):
                normalize(b, xt, xt, mv, rstd, rstd_ready).then_inc(xn_ready, 1)

            def take_v(b, job):
                dve.wait_ge(misc_ready, job + 1)
                half = H // 2
                for r in range(2):
                    s = slice(half * r, half * r + half)
                    last = V.tensor_tensor(vaug[:, :, s, 2 * HD * r:2 * HD * r + HD],
                                           misc[:, :].rearrange("p (i h d) -> p i h d", i=NQ, d=HD)[:, :, s, :],
                                           bv_bc[:, :].rearrange("p (h d) -> p h d", d=HD)[:, s, :].unsqueeze(1)
                                           .to_broadcast([P, NQ, half, HD]), ALU.add)
                last.then_inc(misc_used, 1)

            def maxima(b, h):
                u, s = b * 16 + h, h % 2
                dve.wait_ge(turned_ready, u * 3 + 3)
                for i in reversed(range(NQ)):
                    k, c0 = (0, i * P) if i < 2 else (i - 1, 0)
                    if i:
                        dve.wait_ge(scores_ready, u * 3 + 3 - k)
                        carry_wait()
                    n = P * (i + 1)
                    last = V.tensor_tensor_reduce(
                        out=biased[:, s, OFF[i]:OFF[i] + n], in0=score_bank[k][:, c0:c0 + n],
                        in1=bias_v[:, h, OFF[i]:OFF[i] + n], scale=1.0, scalar=MASKED, op0=ALU.add, op1=ALU.max,
                        accum_out=rowmax[:, s, i:i + 1] if i < NQ - 1 else last_max[:, s, :])
                    if i != 1:
                        last.then_inc(scores_free, 1)
                    if i == 2:
                        dve.wait_ge(scores_free, u * 3 + 4)
                        V.tensor_scalar(neg_max[:, s, :], last_max[:, s, :], -1.0, None, ALU.mult)\
                         .then_inc(max_ready, 1)

            def make_silu_col(b):
                V.tensor_copy(silu_col[:, :], siluT[:, ds(b, 1)].to_broadcast([P, P])).then_inc(silu_col_made, 1)

            def gates(b, job):
                n0 = post_base(b)
                dve.wait_ge(misc_used, job + 1)
                g2 = modbc[:, 0:4:3, :]
                V.tensor_scalar(sgn[:, :, :], g2, 0.0, 2.0, ALU.is_ge, ALU.mult)
                V.tensor_scalar(modbc[:, 2, :], modbc[:, 2, :], 1.0, None, ALU.add)
                V.scalar_tensor_tensor(absg[:, :, :], g2, -1.0, g2, ALU.mult, ALU.max).then_inc(norm_step, 1)
                dve.wait_ge(norm_step, n0 + 1)
                V.tensor_scalar(absg[:, :, :], absg[:, :, :], 0.25, None, ALU.max).then_inc(norm_step, 1)

            def finish_gates(b):
                n0 = post_base(b)
                g2 = modbc[:, 0:4:3, :]
                dve.wait_ge(norm_step, n0 + 2)
                V.scalar_tensor_tensor(g2, sgn[:, :, :], -1.0, absg[:, :, :], ALU.add, ALU.mult)\
                 .then_inc(norm_step, 1)
                dve.wait_ge(norm_step, n0 + 3)
                V.tensor_copy(gb_all[:, ds(b, 1), :], modbc[:, 3:4, :]).then_inc(norm_step, 1)

            def bc4(ap):
                return ap.unsqueeze(1).to_broadcast([P, NQ, C])

            def residual(b, job):
                n0 = post_base(b) + GATE_STEPS
                dve.wait_ge(misc_ready, job + 1)
                if not (isinstance(b, int) and b == 0):
                    dve.wait_ge(x1_stored, b * 16)
                V.tensor_tensor(x1[:, :, :], misc[:, :].rearrange("p (i c) -> p i c", i=NQ), bc4(bproj_bc[:, :]),
                                ALU.add).then_inc(misc_used, 1)
                dve.wait_ge(misc_used, job + 1)
                V.tensor_tensor(x1[:, :, :], x1[:, :, :], bc4(modbc[:, 0, :]), ALU.mult).then_inc(norm_step, 1)
                dve.wait_ge(norm_step, n0 + 1)
                dve.wait_ge(xr_loaded, (b + 1) * 16)
                V.tensor_tensor(x1[:, :, :], x1[:, :, :], xr[:, :, :], ALU.add).then_inc(x1_ready, 1)

            def norm2_stats(b):
                n0 = post_base(b) + GATE_STEPS
                dve.wait_ge(x1_ready, b + 1)
                norm_stats(x1, stats2, mv2, var_eps2, var2_ready, norm_step, n0 + 1)

            def norm2(b):
                n0 = post_base(b) + GATE_STEPS + RESIDUAL_STEPS
                normalize(b, xr, x1, mv2, rstd2, rstd2_ready).then_inc(norm_step, 1)

            def modulate2(b):
                n0 = post_base(b) + GATE_STEPS + RESIDUAL_STEPS
                dve.wait_ge(norm_step, n0 + 1)
                V.tensor_tensor(xr[:, :, :], xr[:, :, :], bc4(modbc[:, 2, :]), ALU.mult).then_inc(norm_step, 1)
                dve.wait_ge(norm_step, n0 + 2)
                V.tensor_tensor(xr[:, :, :], xr[:, :, :], bc4(modbc[:, 1, :]), ALU.add).then_inc(h2_ready, 1)

            def batch(b, post, prep):
                job = {j: first_job(b) + n for n, j in enumerate(jobs(post, prep))}
                for h in range(H):
                    maxima(b, h)
                    if h == 1:
                        if post:
                            dve.wait_ge(av_done, b * 4 + 2)
                        take_v(b, job["V"])
                        if post:
                            make_silu_col(b - 1)
                    if h == 3 and prep:
                        norm1_stats(b + 1)
                    if h == 4 and post:
                        gates(b - 1, job["mod"])
                    if h == 4 and prep:
                        norm1_apply(b + 1)
                    if h == 5 and post:
                        finish_gates(b - 1)
                    if h == 8 and post:
                        residual(b - 1, job["proj"])
                    if h == 9 and post:
                        norm2_stats(b - 1)
                    if h == 12 and post:
                        norm2(b - 1)
                        modulate2(b - 1)

            def hidden_tiles_0_1(j):
                for i in (0, 1):
                    if j >= 2:
                        dve.wait_ge(hidden_used, 4 * (j - 2) + i + 1)
                    for a in range(2):
                        n = P // 4 * i + 2 * j + a
                        last = V.tensor_scalar(hidden_of(j, i, a), dist_of(n, i), slope[:, n:n + 1], neg_b1,
                                               ALU.mult, ALU.max)
                    last.then_inc(hidden_by_dve, 1)

            def stage_bias(j):
                if j >= 3:
                    dve.wait_ge(stage_sent[j % 3], 16 * (j // 3))
                for k in range(2 if j % 2 else 3):
                    dve.wait_ge(hidden_used, 4 * j + k + 2)
                    c0, n = BIAS_BANKS[k]
                    last = V.tensor_scalar(stage_of(j, c0, n), fire_banks[j % 2][k][:, 0:n],
                                           b2_col if k else b12_col, None, ALU.add)
                last.then_inc(stage_by_dve, 1)

            hidden_tiles_0_1(0)
            for j in range(OCTETS):
                if j + 1 < OCTETS:
                    hidden_tiles_0_1(j + 1)
                stage_bias(j)
                if j == 0:
                    make_silu()
                    norm1_stats(0)
                if j == 1:
                    norm1_apply(0)
                    arrange_parameters()
            dve.sem_inc(scores_free, 3)
            dve.wait_ge(params_loaded, 16 * 15)
            for r in range(3):
                dve.wait_ge(stage_sent[r], 16 * len(range(r, OCTETS, 3)))
            batch(0, False, True)
            with dve.Fori(1, B - 1) as b:
                batch(b, True, True)
            batch(B - 1, True, False)
            dve.wait_ge(shared_T, 1)
            V.tensor_copy(w_up_all[:, E, :], score_bank[2][:, :])
            V.tensor_copy(w_dn_all[:, E, :], score_bank[1][:, 0:2 * P])
            make_silu_col(B - 1)
            e0 = EPILOGUE
            dve.wait_ge(misc_ready, e0 + 1)
            dve.wait_ge(y_divided, 2 * B)
            V.reciprocal(den[:, :], misc[:, :]).then_inc(misc_used, 1)
            dve.wait_ge(misc_used, e0 + 1)
            V.tensor_tensor(yT[:, 1, :], yT[:, 1, :], den[:, :], ALU.mult).then_inc(y_divided, 1)
            gates(B - 1, e0 + 1)
            finish_gates(B - 1)
            residual(B - 1, e0 + 2)
            norm2_stats(B - 1)
            norm2(B - 1)
            modulate2(B - 1)

            dve.wait_ge(misc_used, e0 + 5)
            te = [P, TOK, E]

            def e_bc(ap):
                return ap.unsqueeze(1).to_broadcast(te)

            def t_bc(ap):
                return ap.unsqueeze(2).to_broadcast(te)

            V.tensor_scalar(iota_e1[:, :], iota_e[:, :], -float(E), None, ALU.add)
            V.tensor_reduce(top, logits[:, :, :], AX.X, ALU.max).then_inc(top_ready, 1)
            dve.wait_ge(top_ready, 1)
            chain(V.tensor_tensor(wide, logits[:, :, :], t_bc(top), ALU.is_equal))
            chain(V.tensor_tensor(wide2, wide, e_bc(iota_e1[:, :]), ALU.mult))
            chain(V.tensor_reduce(top_e, wide2, AX.X, ALU.min))
            V.tensor_tensor(one_hot[:, :, :], e_bc(iota_e1[:, :]), t_bc(top_e), ALU.is_equal)\
             .then_inc(one_hot_made, 1)
            dve.wait_ge(score_exp, 1)
            chain(V.tensor_scalar(score, score, 1.0, None, ALU.add))
            chain(V.reciprocal(score, score))

            def mask_rows(n):
                r = slice(n * NQ, n * NQ + NQ)
                if n == 0:
                    dve.wait_ge(rows_loaded, 32)
                V.tensor_tensor(rows_all[:, r, 0:C], rows_all[:, r, 0:C],
                                score[:, r].unsqueeze(2).to_broadcast([P, NQ, C]), ALU.mult).then_inc(masked_ready, 1)

            def count_tiles():
                dve.wait_ge(ranks_ready, 1)
                tot = tiles_of[:, :]
                chain(V.tensor_reduce(tot, turned_bank[2][:, :].rearrange("p (t e) -> p e t", e=E), AX.X, ALU.add))
                chain(V.tensor_tensor(wide3, iota_k[:, :].unsqueeze(1).to_broadcast([P, E, TOK]),
                                      tot.unsqueeze(2).to_broadcast([P, E, TOK]), ALU.is_lt))
                chain(V.tensor_reduce(tiles_of[:, :], wide3, AX.X, ALU.add))

            def place_experts():
                chain(V.tensor_tensor(sq, lower[:, :, :], tiles_of[:, :].unsqueeze(1).to_broadcast([P, E, E]),
                                      ALU.mult))
                chain(V.tensor_reduce(first_tile[:, :], sq, AX.X, ALU.add))
                chain(V.tensor_tensor(end_tile[:, :], first_tile[:, :], tiles_of[:, :], ALU.add))
                chain(V.tensor_scalar(base_row[:, :], first_tile[:, :], float(P), None, ALU.mult))

            def place_token():
                chain(V.tensor_tensor(wide, score_bank[1][:, :].rearrange("p (t e) -> p t e", e=E),
                                      e_bc(base_row[:, :]), ALU.add))
                chain(V.tensor_tensor(wide2, wide, one_hot[:, :, :], ALU.mult))

            def store_places():
                chain(V.tensor_reduce(dest_f[:, :], wide2, AX.X, ALU.add))
                V.tensor_copy(dest[:, :], dest_f[:, :]).then_inc(dest_ready, 1)

            half = SORTED // 2

            def name_experts(q):
                v = (cmp_t, cmp_t2)[q][:, 0:half * E].rearrange("p (t e) -> p t e", e=E)
                chain(V.tensor_tensor(v, end_tile[:, :].unsqueeze(1).to_broadcast([P, half, E]),
                                      iota_t[:, half * q:half * q + half].unsqueeze(2).to_broadcast([P, half, E]),
                                      ALU.is_le))
                chain(V.tensor_reduce(expert_f[:, TOK + half * q:TOK + half * q + half], v, AX.X, ALU.add))

            def store_experts():
                chain(V.tensor_scalar(expert_f[:, TOK:SLOTS], expert_f[:, TOK:SLOTS], float(E - 1), None, ALU.min))
                V.tensor_copy(expert[:, :], expert_f[:, :]).then_inc(expert_ready, 1)

            routing = [count_tiles, place_experts, place_token, store_places]
            routing += [lambda n=n: mask_rows(n) for n in range(TOK // NQ)]
            routing += [lambda: name_experts(0), lambda: name_experts(1), store_experts]

            def row_t(t, k):
                dve.wait_ge(rowT_ready, t + 1)
                V.tensor_copy(rowT[:, k % 2, :], score_bank[0][:, 0:P]).then_inc(rowT_copied, 1)

            def first_eight(m):
                return isinstance(m, int) and m == 0

            def row_t_sorted(t, k, m):
                dve.wait_ge(rowT_ready, t + 1)
                V.tensor_copy(rowT[:, k % 2, :], score_bank[0][:, 0:P])
                if not first_eight(m):
                    dve.wait_ge(row_sent[k], m * 16)
                V.tensor_copy(token[:, k:k + 1], row_in[:, k % DEEP, C:ROW].bitcast(i32)).then_inc(rowT_copied, 1)

            def gate_up(t, k):
                dve.wait_ge(gate_done, t + 1)
                V.tensor_tensor(act_h[:, k % 2, :], gated[:, k % 2, :], turned_bank[k % 2][:, F:2 * F], ALU.mult)\
                 .then_inc(act_ready, 1)

            def out_shared(t, k, b):
                dve.wait_ge(down_ready, t + 1)
                V.tensor_tensor(row_out[:, k % DEEP, :], [y_bank, misc][k % 2][:, 0:C],
                                gb_all[:, ds(b, 1), :].rearrange("p a c -> p (a c)"), ALU.mult)\
                 .then_inc(out_copied, 1)
                dve.wait_ge(out_copied, t + 1)
                here = x1_all[:, ds(t, 1), :].rearrange("p a c -> p (a c)")
                V.tensor_tensor(here, here, row_out[:, k % DEEP, :], ALU.add).then_inc(shared_added, 1)

            def out_sorted(t, k, m):
                dve.wait_ge(down_ready, t + 1)
                if k >= 4:
                    dve.wait_ge(row_sent[k - 4], m * 16 + 16)
                elif not first_eight(m):
                    dve.wait_ge(row_sent[k + 4], m * 16)
                V.tensor_copy(row_out[:, k % DEEP, :], [y_bank, misc][k % 2][:, 0:C]).then_inc(out_copied, 1)

            row_t(0, 0)
            row_t(1, 1)
            row_t(2, 2)
            gate_up(0, 0)
            gate_up(1, 1)
            dve.wait_ge(x1_loaded, 16)
            for t in range(TOK):
                k = t % 8
                if t < TOK - 3:
                    row_t(t + 3, (k + 3) % 8)
                else:
                    row_t_sorted(t + 3, (k + 3) % 8, 0)
                gate_up(t + 2, k + 2)
                if t == TOK - NQ:
                    dve.wait_ge(x1_loaded, 32)
                out_shared(t, k, t // NQ)
                if t < len(routing):
                    routing[t]()

            def eight_sorted(m, last=False):
                for k in range(8):
                    t = m * 8 + TOK + k
                    if not (last and k >= 5):
                        row_t_sorted(t + 3, (k + 3) % 8, m if k < 5 else m + 1)
                    if not (last and k >= 6):
                        gate_up(t + 2, k + 2)
                    out_sorted(t, k, m)

            eight_sorted(0)
            with dve.Fori(1, SORTED // 8 - 1) as m:
                eight_sorted(m)
            eight_sorted(SORTED // 8 - 1, last=True)
            finish(dve, V, [b for b in range(B) if b not in BY_POOL], final_by_dve)

        @block.tensor
        def _(pe):
            mm = nc.tensor.matmul
            pe.sem_inc(turned_ready, 6)
            pe.sem_inc(turned_free, 3)
            pe.sem_inc(av_done, 2)
            pe.sem_inc(y_copied, 1)

            def transpose4(src, job):
                for i in range(NQ):
                    last = mm(misc[:, i * P:i * P + P], src[:, i, :], ident[:, :], is_transpose=True,
                              start=True, stop=True)
                last.then_inc(misc_ready, 1)

            def xT(b, job):
                pe.wait_ge(xn_ready, b + 1)
                if not (isinstance(job, int) and job == 0):
                    pe.wait_ge(misc_used, job)
                transpose4(xt, job)

            def qk_of(mat, job):
                pe.wait_ge(misc_used, job)
                mm(misc[:, :], Wqk[:, mat, :], hT[:, :], start=True, stop=True).then_inc(misc_ready, 1)

            def v_of(b, job):
                pe.wait_ge(misc_used, job)
                for i in range(NQ):
                    last = mm(misc[:, i * C:i * C + C], hT[:, i * P:i * P + P], Wv[:, :],
                              start=True, stop=True)
                last.then_inc(misc_ready, 1)

            def scores(b, h):
                u, g = b * 16 + h, h // 4
                if h % 4 == 0:
                    for mat in range(2):
                        pe.wait_ge(feat_ready[g % 2][mat], b * 2 * FEAT + FEAT * (g // 2 + 1))
                for i in reversed(range(NQ)):
                    k, c0 = (0, i * P) if i < 2 else (i - 1, 0)
                    if i:
                        pe.wait_ge(scores_free, u * 3 + 3 - k)
                    n = P * (i + 1)
                    last = mm(score_bank[k][:, c0:c0 + n], qf[:, g % 2, h % 4, i * P:i * P + P],
                              kf[:, g % 2, h % 4, 0:n], start=True, stop=True)
                    if i != 1:
                        last.then_inc(scores_ready, 1)

            def turn(b, h):
                u, s = b * 16 + h, h % 2
                pe.wait_ge(scores_free, u * 3 + 6)
                for k, blocks in enumerate(BANKS):
                    pe.wait_ge(turned_free, u * 3 + k + 1)
                    for j, i0, c0 in blocks:
                        for i in range(i0, NQ):
                            dst = turned_bank[k][:, c0 + (i - i0) * P:c0 + (i - i0) * P + P]
                            if k == 0 and i == NQ - 1:
                                pe.wait_ge(shifted, u + 1)
                            last = mm(dst, biased[:, s, OFF[i] + j * P:OFF[i] + j * P + P], ident[:, :],
                                      is_transpose=True, start=True, stop=(i == NQ - 1))
                            if i < NQ - 1:
                                last = mm(dst, rowmax[:, s, i:i + 1].to_broadcast([P, P]), neg_ident[:, :],
                                          start=False, stop=True)
                    last.then_inc(turned_ready, 1)

            def values(b, g):
                pe.wait_ge(turned_free, b * 48 + 12 * g + 12 + 3)
                if g % 2 == 0:
                    pe.wait_ge(y_copied, b * 2 + g // 2 + 1)
                for j in range(NQ):
                    n = P * (NQ - j)
                    for hh in range(4):
                        h = 4 * g + hh
                        c0 = (h % 8) * CAUSAL + PCOL[j]
                        last = mm(y_bank[W * hh:W * hh + W, j * P:T], vaug[:, j, g % 2 * 8 + g // 2 * 4 + hh, :],
                                  probs[:, c0:c0 + n], start=(g % 2 == 0 and j == 0), stop=(g % 2 == 1 and j == NQ - 1))
                last.then_inc(av_done, 1)

            def denominators(b, pair, job):
                pe.wait_ge(y_copied, b * 2 + pair + 2)
                pe.wait_ge(misc_used, job)
                mm(misc[:, :], pick_den[:, :], yT[:, pair, :], start=True, stop=True).then_inc(misc_ready, 1)

            def modulation(b, job):
                pe.wait_ge(silu_col_made, b + 1)
                pe.wait_ge(misc_used, job)
                mm(misc[:, :], silu_col[:, :], wmod_bc[:, :], start=True, stop=True).then_inc(misc_ready, 1)

            def project(b, job):
                pe.wait_ge(y_divided, b * 2 + 3)
                pe.wait_ge(misc_used, job)
                for i in range(NQ):
                    for pair in range(2):
                        last = mm(misc[:, i * C:i * C + C], yT[:, pair, i * P:i * P + P], Wproj[:, pair, :],
                                  start=(pair == 0), stop=(pair == 1))
                last.then_inc(misc_ready, 1)

            def turn_h2(b, job):
                pe.wait_ge(h2_ready, b + 1)
                pe.wait_ge(misc_used, job)
                transpose4(xr, job)

            def router(b, job):
                pe.wait_ge(misc_used, job)
                for i in range(NQ):
                    last = mm(misc[:, i * E:i * E + E], h2T[:, i * P:i * P + P], routerT[:, :], start=True, stop=True)
                last.then_inc(misc_ready, 1)

            def batch(b, post, prep):
                job = {j: first_job(b) + n for n, j in enumerate(jobs(post, prep))}
                for h in range(H):
                    if h < H - 1:
                        scores(b, h + 1)
                    elif prep:
                        scores(b + 1, 0)
                    turn(b, h)
                    if h == 0:
                        if post:
                            values(b - 1, 3)
                        v_of(b, job["V"])
                    if h == 1 and post:
                        denominators(b - 1, 1, job["den1"])
                    if h == 3 and post:
                        modulation(b - 1, job["mod"])
                    if h == 6 and post:
                        project(b - 1, job["proj"])
                    if h == 4:
                        pe.wait_ge(misc_used, job["V"] + 1)
                        values(b, 0)
                    if h == 5 and prep:
                        xT(b + 1, job["xT"])
                    if h == 7 and prep:
                        qk_of(0, job["q"])
                    if h == 9 and prep:
                        qk_of(1, job["k"])
                    if h == 8:
                        values(b, 1)
                    if h == 10:
                        denominators(b, 0, job["den0"])
                    if h == 12:
                        values(b, 2)
                    if h == 13 and post:
                        turn_h2(b - 1, job["h2T"])
                    if h == 14 and post:
                        router(b - 1, job["logits"])

            pe.wait_ge(w2_made, 1)
            for a in range(2):
                last = mm(y_bank[64 * a:64 * a + 64, 0:1], w2_bd, b1_col, start=True, stop=True)
            last.then_inc(b1_products, 1)
            for j in range(OCTETS):
                if j >= 2:
                    pe.wait_ge(stage_by_dve, j - 1)
                    if j % 2:
                        pe.wait_ge(stage_by_act, j // 2)
                for i in range(NQ):
                    if i < 2:
                        pe.wait_ge(hidden_by_dve, 2 * j + i + 1)
                    else:
                        pe.wait_ge(hidden_by_act, 2 * j + i - 1)
                    k, c0 = bias_bank(i)
                    for a in range(2):
                        last = mm(fire_banks[j % 2][k][64 * a:64 * a + 64, c0:c0 + P * (i + 1)], w2_bd,
                                  hidden_of(j, i, a), start=True, stop=True)
                    last.then_inc(hidden_used, 1)
                if j == 1:
                    pe.wait_ge(silu_made, 1)
                    pe.wait_ge(first_params_loaded, 16 * 10)
                    for m in range(2):
                        last = mm(misc[:, m * B:m * B + B], wmod_cols[:, m * C:m * C + C], siluT[:, :],
                                  start=True, stop=True)
                    last.then_inc(modT_ready, 1)
                if j == 2:
                    pe.wait_ge(consts_made, 3)
                    pe.wait_ge(modT_copied, 1)
                    xT(0, 0)
                if j in (3, 4):
                    qk_of(j - 3, j - 2)
            pe.wait_ge(stage_by_dve, OCTETS)
            pe.wait_ge(stage_by_act, OCTETS // 2)
            pe.wait_ge(params_loaded, 16 * 15)
            scores(0, 0)
            batch(0, False, True)
            with pe.Fori(1, B - 1) as b:
                batch(b, True, True)
            batch(B - 1, True, False)
            values(B - 1, 3)
            pe.wait_ge(shared_loaded, 16 * 5)
            pe.wait_ge(scores_free, 3 + 3 * 16 * B)
            for k in range(4):
                mm(score_bank[2][:, k * P:k * P + P], raw_up[:, k, :], ident[:, :], is_transpose=True,
                   start=True, stop=True)
            for k in range(2):
                last = mm(score_bank[1][:, k * P:k * P + P], raw_down[:, k, :], ident[:, :], is_transpose=True,
                          start=True, stop=True)
            last.then_inc(shared_T, 1)
            e0 = EPILOGUE
            denominators(B - 1, 1, e0)
            modulation(B - 1, e0 + 1)
            project(B - 1, e0 + 2)
            turn_h2(B - 1, e0 + 3)
            router(B - 1, e0 + 4)
            pe.wait_ge(one_hot_made, 1)
            hot = one_hot[:, :, :].rearrange("p t e -> p (t e)")
            rank = score_bank[1][:, :]
            mm(rank, before[:, :], hot, start=True, stop=False)
            for t in range(TOK - 1):
                left = TOK - 1 - t
                mm(rank[:, (t + 1) * E:TOK * E].rearrange("p (t e) -> p t e", e=E), ones_bf[:, :],
                   one_hot[:, t:t + 1, :].to_broadcast([P, left, E]), start=False, stop=(t == TOK - 2))
            mm(turned_bank[2][:, :], ones_bf[:, :], hot, start=True, stop=True).then_inc(ranks_ready, 1)
            def turn_row(t, k, n):
                pe.wait_ge(row_loaded[k], n * 16 + 16)
                mm(score_bank[0][:, 0:P], row_in[:, k, 0:C], ident[:, :], is_transpose=True, start=True, stop=True)\
                    .then_inc(rowT_ready, 1)

            def weights_of(t, count):
                return nc.values_load_multi_w_load_instructions(
                    expert[0:1, ds(t, count)], engines=[mybir.EngineType.PE], min_val=0, max_val=E,
                    skip_runtime_bounds_check_because="a count of experts, cut to E - 1, or the constant E")[1]

            def up(t, k, e):
                pe.wait_ge(rowT_copied, t + 1)
                mm(turned_bank[k % 2][:, :], rowT[:, k % 2, :],
                   w_up_all[:, ds(e, 1), :].rearrange("p a n -> p (a n)"), start=True, stop=True).then_inc(up_ready, 1)

            def turn_act(t, k):
                pe.wait_ge(act_ready, t + 1)
                for a in range(2):
                    last = mm(score_bank[2][:, a * P:a * P + P], act_h[:, k % 2, a * P:a * P + P], ident[:, :],
                              is_transpose=True, start=True, stop=True)
                last.then_inc(actT_ready, 1)

            def down(t, k, e):
                pe.wait_ge(actT_copied, t + 1)
                for a in range(2):
                    last = mm([y_bank, misc][k % 2][:, 0:C], act_hT[:, k % 2, a * P:a * P + P],
                              w_dn_all[:, ds(e, 1), a * C:a * C + C].rearrange("p a n -> p (a n)"),
                              start=(a == 0), stop=(a == 1))
                last.then_inc(down_ready, 1)

            def four_tiles(n, e, ups=DEEP, turns=DEEP, drain=False):
                for k in range(DEEP):
                    t = n * DEEP + k
                    if k < ups:
                        up(t + 2, k + 2, e[k + 2])
                    if k < turns:
                        turn_row(t + 3, (k + 3) % DEEP, n if k < 1 else n + 1)
                    if drain and k >= 2:
                        pe.wait_ge(out_copied, t - 1)
                    down(t, k, e[k])
                    if not (drain and k == 3):
                        turn_act(t + 1, k + 1)

            turn_row(0, 0, 0)
            up(0, 0, E)
            turn_row(1, 1, 0)
            up(1, 1, E)
            turn_row(2, 2, 0)
            turn_act(0, 0)
            with pe.Fori(0, TOK // DEEP - 1) as n:
                four_tiles(n, [E] * (DEEP + 2))
            pe.wait_ge(expert_ready, 1)
            pe.wait_ge(w_loaded, 16 * 2 * E)
            four_tiles(TOK // DEEP - 1, weights_of(TOK - DEEP, DEEP + 2))
            with pe.Fori(TOK // DEEP, SLOTS // DEEP - 1) as n:
                four_tiles(n, weights_of(n * DEEP, DEEP + 2))
            four_tiles(SLOTS // DEEP - 1, weights_of(SLOTS - DEEP, DEEP), ups=2, turns=1, drain=True)


_INS = ['L0_attn_x', 'L0_attn_Wqkv', 'L0_attn_bqkv', 'L0_attn_Wproj', 'L0_attn_bproj', 'L0_attn_w1', 'L0_attn_b1',
        'L0_attn_w2', 'L0_attn_b2', 'L0_attn_c_param', 'L0_attn_L_multiplier', 'L0_ffn_w_router',
        'L0_ffn_gate_up_proj', 'L0_ffn_down_proj', 'L0_ffn_w_gate', 'L0_ffn_w_up', 'L0_ffn_w_down', 'L0_c', 'L0_wmod']


def kernel(**inputs):
    import numpy as _np
    import concourse.bacc as _bacc
    from concourse import mybir as _mybir
    from concourse.bass_utils import run_bass_kernel_spmd as _run

    nc = _bacc.Bacc("TRN2", target_bir_lowering=False, num_devices=1)
    arrays, args = {}, []
    for name in _INS:
        a = _np.ascontiguousarray(inputs[name])
        if a.ndim == 0:
            a = a.reshape(1)
        arrays[f"in_{name}_dram"] = a
        args.append(nc.dram_tensor(f"in_{name}_dram", a.shape, _mybir.dt.from_np(a.dtype), kind="ExternalInput").ap())
    args.append(nc.dram_tensor("out_0_dram", (B, T, C), _mybir.dt.float32, kind="ExternalOutput").ap())
    bass_adaln_block(nc, *args)
    r = _run(nc, [arrays], core_ids=[0])
    return r.results[0]["out_0_dram"]
```
